# Optimizing a Trainium2 kernel written in Bass

```python
import numpy as np
import jax
import jax.numpy as jnp

def _softmax(x, axis=-1):
    return jax.nn.softmax(x, axis=axis)

def _gelu(x):
    return jax.nn.gelu(x, approximate=True)

def _silu(x):
    return jax.nn.silu(x)

def _sigmoid(x):
    return jax.nn.sigmoid(x)

def _layernorm(x, axis=-1, eps=1e-05):
    m = jnp.mean(x, axis=axis, keepdims=True)
    v = jnp.var(x, axis=axis, keepdims=True)
    return (x - m) / jnp.sqrt(v + eps)

def _scatter_add(tgt, idx, src, axis=0):
    return tgt.at[idx].add(src)

def _segment_sum(src, seg, n):
    return jax.ops.segment_sum(src, seg, n)
kernel_name = 'mk_gnn_resnorm_d2_gnn_r8_e07649'

def setup_inputs(seed: int=0):
    np.random.seed(seed)
    _w = jnp.asarray

    def _rec_inputs():
        import jax
        import jax.numpy as jnp
        _gk = jax.random.key(seed)
        x = -0.0001126 + 1 * jax.random.normal(jax.random.fold_in(_gk, 1), (1250, 768), jnp.float32)
        _s = jax.random.randint(jax.random.fold_in(_gk, 2), (20000,), 0, 1250, jnp.int32)
        _d = jax.random.randint(jax.random.fold_in(_gk, 3), (20000,), 0, 1250, jnp.int32)
        _loop = jnp.arange(1250, dtype=jnp.int32)
        src = jnp.concatenate([_s, _d, _loop])
        dst = jnp.concatenate([_d, _s, _loop])
        _o = jnp.argsort(dst, stable=True)
        src = src[_o]
        dst = dst[_o]
        return (x, src, dst)
    x, src, dst = _rec_inputs()

    def _L0_gnn_setup():
        import jax, jax.numpy as jnp
        import numpy as np
        N_NODES = 1250
        N_EDGES = 12500
        DIM = 768
        key = jax.random.key(seed)
        k1, k2, k3, k4 = jax.random.split(key, 4)
        x = jax.random.normal(k1, (N_NODES, DIM), dtype=jnp.float32)
        edge_index = jax.random.randint(k2, (2, N_EDGES), 0, N_NODES, dtype=jnp.int32)
        W = jax.random.normal(k3, (DIM, DIM), dtype=jnp.float32) / np.sqrt(DIM)
        b = jnp.zeros((DIM,), dtype=jnp.float32)
        return {'x': x, 'edge_index': edge_index, 'W': W, 'b': b}
    _L0_gnn_all = _L0_gnn_setup()
    _L0_gnn_in = {k: v for k, v in _L0_gnn_all.items() if k in ('W', 'b')}
    del _L0_gnn_all

    def _L1_gnn_setup():
        import jax, jax.numpy as jnp
        import numpy as np
        N_NODES = 2500
        N_EDGES = 20000
        IN_DIM = 768
        HID = 256
        HEADS = 4
        OUT_DIM = 768
        LN_EPS = 1e-05

        def _add_self_loops(edge_index, n):
            loop = jnp.arange(n, dtype=edge_index.dtype)
            return jnp.concatenate([edge_index, jnp.stack([loop, loop])], axis=1)

        def gat_conv(x, edge_index, W, a_src, a_dst, bias, heads, out_ch, concat):
            n = x.shape[0]
            ei = _add_self_loops(edge_index, n)
            src, dst = (ei[0], ei[1])
            xl = (x @ W).reshape(n, heads, out_ch)
            alpha_src = jnp.einsum('nhc,hc->nh', xl, a_src)
            alpha_dst = jnp.einsum('nhc,hc->nh', xl, a_dst)
            e = jax.nn.leaky_relu(alpha_src[src] + alpha_dst[dst], 0.2)
            m = jax.ops.segment_max(e, dst, num_segments=n)
            e = jnp.exp(e - m[dst])
            s = jax.ops.segment_sum(e, dst, num_segments=n)
            alpha = e / (s[dst] + 1e-16)
            msg = xl[src] * alpha[:, :, None]
            out = jax.ops.segment_sum(msg, dst, num_segments=n)
            out = out.reshape(n, heads * out_ch) if concat else out.mean(axis=1)
            return out + bias

        def layer_norm(x, g, b):
            mu = jnp.mean(x, axis=-1, keepdims=True)
            var = jnp.var(x, axis=-1, keepdims=True)
            return (x - mu) * jax.lax.rsqrt(var + LN_EPS) * g + b
        key = jax.random.key(seed)
        ks = jax.random.split(key, 16)
        s = 0.02
        HC = HID * HEADS
        return {'x': jax.random.normal(ks[0], (N_NODES, IN_DIM), jnp.float32), 'edge_index': jax.random.randint(ks[1], (2, N_EDGES), 0, N_NODES, jnp.int64 if jax.config.jax_enable_x64 else jnp.int32), 'W1': jax.random.normal(ks[2], (IN_DIM, HC), jnp.float32) * s, 'a_src1': jax.random.normal(ks[3], (HEADS, HID), jnp.float32) * s, 'a_dst1': jax.random.normal(ks[4], (HEADS, HID), jnp.float32) * s, 'b1': jnp.zeros((HC,), jnp.float32), 'g1': jnp.ones((HC,), jnp.float32), 'be1': jnp.zeros((HC,), jnp.float32), 'Wr1': jax.random.normal(ks[5], (IN_DIM, HC), jnp.float32) * s, 'br1': jnp.zeros((HC,), jnp.float32), 'W2': jax.random.normal(ks[6], (HC, OUT_DIM), jnp.float32) * s, 'a_src2': jax.random.normal(ks[7], (1, OUT_DIM), jnp.float32) * s, 'a_dst2': jax.random.normal(ks[8], (1, OUT_DIM), jnp.float32) * s, 'b2': jnp.zeros((OUT_DIM,), jnp.float32), 'g2': jnp.ones((OUT_DIM,), jnp.float32), 'be2': jnp.zeros((OUT_DIM,), jnp.float32), 'Wr2': jax.random.normal(ks[9], (HC, OUT_DIM), jnp.float32) * s, 'br2': jnp.zeros((OUT_DIM,), jnp.float32)}
    _L1_gnn_all = _L1_gnn_setup()
    _L1_gnn_in = {k: v for k, v in _L1_gnn_all.items() if k in ('W1', 'a_src1', 'a_dst1', 'b1', 'g1', 'be1', 'Wr1', 'br1', 'W2', 'a_src2', 'a_dst2', 'b2', 'g2', 'be2', 'Wr2', 'br2')}
    del _L1_gnn_all
    return {'x': x, 'src': src, 'dst': dst, 'L0_gnn_W': _L0_gnn_in['W'], 'L0_gnn_b': _L0_gnn_in['b'], 'L1_gnn_W1': _L1_gnn_in['W1'], 'L1_gnn_a_src1': _L1_gnn_in['a_src1'], 'L1_gnn_a_dst1': _L1_gnn_in['a_dst1'], 'L1_gnn_b1': _L1_gnn_in['b1'], 'L1_gnn_g1': _L1_gnn_in['g1'], 'L1_gnn_be1': _L1_gnn_in['be1'], 'L1_gnn_Wr1': _L1_gnn_in['Wr1'], 'L1_gnn_br1': _L1_gnn_in['br1'], 'L1_gnn_W2': _L1_gnn_in['W2'], 'L1_gnn_a_src2': _L1_gnn_in['a_src2'], 'L1_gnn_a_dst2': _L1_gnn_in['a_dst2'], 'L1_gnn_b2': _L1_gnn_in['b2'], 'L1_gnn_g2': _L1_gnn_in['g2'], 'L1_gnn_be2': _L1_gnn_in['be2'], 'L1_gnn_Wr2': _L1_gnn_in['Wr2'], 'L1_gnn_br2': _L1_gnn_in['br2']}

def reference(x, src, dst, L0_gnn_W, L0_gnn_b, L1_gnn_W1, L1_gnn_a_src1, L1_gnn_a_dst1, L1_gnn_b1, L1_gnn_g1, L1_gnn_be1, L1_gnn_Wr1, L1_gnn_br1, L1_gnn_W2, L1_gnn_a_src2, L1_gnn_a_dst2, L1_gnn_b2, L1_gnn_g2, L1_gnn_be2, L1_gnn_Wr2, L1_gnn_br2):
    import jax
    import jax.numpy as jnp

    def _L0_gnn_ref(x, edge_index, W, b):
        import jax, jax.numpy as jnp
        import numpy as np
        N_NODES = 1250
        N_EDGES = 12500
        DIM = 768
        n = x.shape[0]
        loop = jnp.arange(n, dtype=edge_index.dtype)
        src = jnp.concatenate([edge_index[0], loop])
        dst = jnp.concatenate([edge_index[1], loop])
        deg = jax.ops.segment_sum(jnp.ones_like(dst, dtype=x.dtype), dst, num_segments=n)
        deg_inv_sqrt = jnp.where(deg > 0, jax.lax.rsqrt(deg), 0.0)
        norm = deg_inv_sqrt[src] * deg_inv_sqrt[dst]
        h = x @ W
        msg = h[src] * norm[:, None]
        out = jax.ops.segment_sum(msg, dst, num_segments=n)
        return out + b

    def _L1_gnn_ref(x, edge_index, W1, a_src1, a_dst1, b1, g1, be1, Wr1, br1, W2, a_src2, a_dst2, b2, g2, be2, Wr2, br2):
        import jax, jax.numpy as jnp
        import numpy as np
        N_NODES = 2500
        N_EDGES = 20000
        IN_DIM = 768
        HID = 256
        HEADS = 4
        OUT_DIM = 768
        LN_EPS = 1e-05

        def _add_self_loops(edge_index, n):
            loop = jnp.arange(n, dtype=edge_index.dtype)
            return jnp.concatenate([edge_index, jnp.stack([loop, loop])], axis=1)

        def gat_conv(x, edge_index, W, a_src, a_dst, bias, heads, out_ch, concat):
            n = x.shape[0]
            ei = _add_self_loops(edge_index, n)
            src, dst = (ei[0], ei[1])
            xl = (x @ W).reshape(n, heads, out_ch)
            alpha_src = jnp.einsum('nhc,hc->nh', xl, a_src)
            alpha_dst = jnp.einsum('nhc,hc->nh', xl, a_dst)
            e = jax.nn.leaky_relu(alpha_src[src] + alpha_dst[dst], 0.2)
            m = jax.ops.segment_max(e, dst, num_segments=n)
            e = jnp.exp(e - m[dst])
            s = jax.ops.segment_sum(e, dst, num_segments=n)
            alpha = e / (s[dst] + 1e-16)
            msg = xl[src] * alpha[:, :, None]
            out = jax.ops.segment_sum(msg, dst, num_segments=n)
            out = out.reshape(n, heads * out_ch) if concat else out.mean(axis=1)
            return out + bias

        def layer_norm(x, g, b):
            mu = jnp.mean(x, axis=-1, keepdims=True)
            var = jnp.var(x, axis=-1, keepdims=True)
            return (x - mu) * jax.lax.rsqrt(var + LN_EPS) * g + b
        h0 = x
        h = gat_conv(x, edge_index, W1, a_src1, a_dst1, b1, HEADS, HID, True)
        h = layer_norm(h, g1, be1)
        h = jax.nn.relu(h)
        h = h + (h0 @ Wr1 + br1)
        h1 = h
        h = gat_conv(h, edge_index, W2, a_src2, a_dst2, b2, 1, OUT_DIM, False)
        h = layer_norm(h, g2, be2)
        h = h + (h1 @ Wr2 + br2)
        return h
    edge_index = jnp.stack([src, dst])
    x = _layernorm(x + _L0_gnn_ref(x, edge_index, L0_gnn_W, L0_gnn_b), axis=-1)
    x = _layernorm(x + _L1_gnn_ref(x, edge_index, L1_gnn_W1, L1_gnn_a_src1, L1_gnn_a_dst1, L1_gnn_b1, L1_gnn_g1, L1_gnn_be1, L1_gnn_Wr1, L1_gnn_br1, L1_gnn_W2, L1_gnn_a_src2, L1_gnn_a_dst2, L1_gnn_b2, L1_gnn_g2, L1_gnn_be2, L1_gnn_Wr2, L1_gnn_br2), axis=-1)
    return x

_drawn_inputs = setup_inputs


def setup_inputs(seed=0):
    import zlib

    import numpy as np

    out = dict(_drawn_inputs(seed))
    spreads = {'L0_gnn_b': (0.0, 0.1),
     'L1_gnn_b1': (0.0, 0.1),
     'L1_gnn_g1': (1.0, 0.2),
     'L1_gnn_be1': (0.0, 0.1),
     'L1_gnn_br1': (0.0, 0.1),
     'L1_gnn_b2': (0.0, 0.1),
     'L1_gnn_g2': (1.0, 0.2),
     'L1_gnn_be2': (0.0, 0.1),
     'L1_gnn_br2': (0.0, 0.1)}
    factors = {'L1_gnn_a_dst1': 6.031, 'L1_gnn_a_src2': 3.175, 'L1_gnn_a_dst2': 6.371}
    for name, (base, spread) in spreads.items():
        noise = np.random.default_rng([zlib.crc32(name.encode()), seed]).standard_normal(out[name].shape)
        drawn = base * np.exp(spread * noise) if base else spread * noise
        out[name] = jnp.asarray(drawn.astype(out[name].dtype))
    for name, factor in factors.items():
        out[name] = (out[name] * factor).astype(out[name].dtype)
    return out
```

```python
from contextlib import ExitStack

import concourse.bass as bass
from concourse import mybir

P = 128
N = 1250
T = -(-N // P)
NP = T * P
LAST = N - (T - 1) * P
E = 41250
ET = -(-E // P)
D = 768
KD = D // P
H, HID = 4, 256
HC = H * HID
KH = HC // P
HS = HID + 2
XS = D + 2
WSCALE = 64.0
LN_EPS = 1e-5
SOFTMAX_EPS = 1e-16
SLOPE = 0.2
NEG_BIG = -3e38

WD = 32
NB = NP // WD
G = 4
NG = -(-ET // G)
EG = -(-ET // P)
KS = 2 * NP
PAD_DST = 2000
KRING = 4
LO_STEP = 16
RANGE_BIG = 1024.0
F16_EXACT = 2048

C1 = 5
W1C = C1 * P
PSLOTS = 5
C2 = 2
W2C = C2 * P

KB = 1024


def gnn_program(nc, x, src, dst, W0, b0, W1, a_src1, a_dst1, b1, g1, be1, Wr1, br1,
                W2, a_src2, a_dst2, b2, g2, be2, Wr2, br2, out):
    dt = mybir.dt
    f32, f16, bf16, i32, i16, u16 = dt.float32, dt.float16, dt.bfloat16, dt.int32, dt.int16, dt.uint16
    ALU, AX, ACT = mybir.AluOpType, mybir.AxisListType, mybir.ActivationFunctionType
    ds = bass.ds
    bytes_of = {f32: 4, i32: 4, f16: 2, bf16: 2, i16: 2, u16: 2}

    with ExitStack() as ctx:
        def sem(name):
            return ctx.enter_context(nc.semaphore(name))

        ARENA = 207 * KB
        arena = ctx.enter_context(nc.sbuf_tensor("arena", [P, ARENA // 4], f32))
        psum = ctx.enter_context(nc.psum_tensor("psum", [P, 8 * 512], f32))

        def at(byte, shape, dtype, parts=P):
            n = 1
            for s in shape:
                n *= s
            size = n * bytes_of[dtype]
            assert byte % 4 == 0 and byte + size <= ARENA, (byte, shape)
            v = arena[0:parts, byte // 4:byte // 4 + -(-size // 4)]
            if dtype != f32:
                v = v.bitcast(dtype)
            v = v[:, 0:n]
            if len(shape) == 2:
                v = v.rearrange("p (a b) -> p a b", a=shape[0])
            elif len(shape) == 3:
                v = v.rearrange("p (a b c) -> p a b c", a=shape[0], b=shape[1])
            return v

        pos = 0

        def small(shape, dtype, parts=P):
            nonlocal pos
            v = at(pos, shape, dtype, parts)
            n = 1
            for s in shape:
                n *= s
            pos += -(-n * bytes_of[dtype] // 4) * 4
            return v

        ident = small([P], f32)
        ident_h = small([P], f16)
        ones_h = small([2], f16)
        half = small([T], f32)
        flag_i = small([1], i32)
        over = small([1], f32)
        ones_f = small([1], f32)
        deg = small([T], f32)
        dinv = small([T], f32)
        dinv_s = small([T], f32)
        stats = small([2, 6], f32)
        mv = small([2], f32)
        veps = small([1], f32)
        rstd = small([1], f32)
        wt = small([KH, 8], f32)
        wt_hi = small([KH, 8], f16)
        wt_lo = small([KH, 8], f16)
        asd = small([8, T], f32)
        as_s = small([4, T], f32)
        mx = small([4, T], f32)
        zz = small([4, T], f32)
        mm = small([4, T], f32)
        uv = small([8, T], f32)
        ssum = small([C1], f32)
        rsum = small([C1], f32)
        range_i = small([2 * NB], i32, 1)
        range_t = small([2 * NB], i32, 1)
        thr = small([2], f32, NB)
        span = small([2], f32, NB)
        endm1 = small([1], f32, NB)
        tmm = small([2, EG], f32)
        rows_sb = small([P], f32, 80)
        assert pos <= 4 * KB, pos
        par_rows = at(4 * KB, [4, HC], f32)
        CT = at(20 * KB, [T, NP], u16)
        assert T * NP * 2 == 25 * KB

        lo_oh = at(45 * KB, [P, NG * G], f16)
        x_sb = at(126 * KB, [T, D], f32)
        w0_hi = at(156 * KB, [KD, D], f16)
        w0_lo = at(165 * KB, [KD, D], f16)
        src_i = at(174 * KB, [EG, P], i32)
        dst_i = at(174 * KB + 1536, [EG, P], i32)
        hi_i = at(177 * KB, [EG, P], i32)
        lo_i = at(177 * KB + 1536, [EG, P], i32)
        dst_f = at(180 * KB, [EG, P], f32)
        key_f = at(180 * KB + 1536, [EG, P], f32)
        lo_f = at(183 * KB, [EG, P], f32)
        key_b = at(185 * KB, [2, NG * G], i16)
        lo_t = at(187 * KB, [NG * G], f16)
        jt = at(188 * KB, [P, LO_STEP], f16)
        key_io = at(192 * KB, [T * WD, G], i16)
        ring = at(195 * KB, [KRING, T * WD, G], f16)
        zero_h = at(205 * KB, [T * WD], f16)
        t_io = at(20 * KB, [EG * P], f32, NB)
        r_a = at(22 * KB, [EG * P], f32, NB)
        r_b = at(24 * KB, [EG * P], f32, NB)
        r_c = at(26 * KB, [EG * P], f32, NB)
        r_d = at(28 * KB, [EG * P], f32, NB)
        wst0 = [at(32 * KB, [D], f32), at(36 * KB, [D], f32)]

        c_hi = at(45 * KB, [T, NP], f16)
        c_lo = at(70 * KB, [T, NP], f16)
        xs_hi = at(95 * KB, [T, D], f16)
        xs_lo = at(110 * KB, [T, D], f16)
        ag_hi = at(174 * KB, [KD, NP], f16)
        ag_lo = at(189 * KB, [KD, NP], f16)
        y0 = at(95 * KB, [2, D], f32)
        x1_sb = x_sb

        neg = at(70 * KB, [T, NP], bf16)
        x1t_hi = at(101 * KB, [KD, NP], f16)
        x1t_lo = at(189 * KB, [KD, NP], f16)
        w1_hi = at(45 * KB, [KD, HC], f16)
        w1_lo = at(57 * KB, [KD, HC], f16)
        xl_hi = at(126 * KB, [T, H, HS], f16)
        xl_lo = at(147 * KB, [T, H, HS], f16)
        wr1_hi = w1_hi
        wr1_lo = w1_lo
        wst = [at(174 * KB, [HC], f32), at(178 * KB, [HC], f32)]
        as_row = [at(168 * KB, [NP], f32), at(182 * KB, [NP], f32)]
        junk = [at(116 * KB + 2560 * i, [NP], bf16) for i in range(2)]
        r_st = [at(121 * KB, [HC], f32), at(95 * KB, [HC], f32)]
        e1 = [at(45 * KB + 2560 * i, [W1C], f32) for i in range(2)]
        e2 = [at(50 * KB + 2560 * i, [W1C], f32) for i in range(2)]
        pf = [at(55 * KB + 2560 * i, [W1C], f32) for i in range(2)]
        h1t_hi = at(60 * KB + 256, [KH, NP], f16)
        p_hi = [at(80 * KB + 512 + 2560 * i, [W1C], f16) for i in range(PSLOTS)]
        p_lo = [at(80 * KB + 512 + 2560 * i + 1280, [W1C], f16) for i in range(PSLOTS)]
        att = at(94 * KB, [C1, HC], f32)
        r_ld = [at(114 * KB, [HC], f32), at(118 * KB, [HC], f32)]
        uv_row = [[at(168 * KB, [W1C], f32), at(168 * KB + 2560, [W1C], f32)],
                  [at(173 * KB, [W1C], f32), at(173 * KB + 2560, [W1C], f32)]]
        h1t_lo = at(186 * KB, [KH, NP], f16)

        w2_hi = at(126 * KB, [KH, D], f16)
        w2_lo = at(138 * KB, [KH, D], f16)
        wst2 = [at(150 * KB, [D], f32), at(153 * KB, [D], f32)]
        neg2 = at(94 * KB, [T, NP], bf16)
        xl2_hi = at(45 * KB, [T, XS], f16)
        xl2_lo = at(156 * KB, [T, XS], f16)
        as2_row = at(172 * KB, [NP], f32)
        junk2 = [at(177 * KB + 2560 * i, [NP], bf16) for i in range(2)]
        r2_st = [at(182 * KB + 512, [D], f32), at(119 * KB, [D], f32)]
        xb_ld = [at(81 * KB, [D], f32), at(85 * KB, [D], f32)]
        u2_row = at(126 * KB, [NP], f32)
        v2_row = at(131 * KB, [NP], f32)
        ee1 = [at(136 * KB + KB * i, [W2C], f32) for i in range(2)]
        ee2 = [at(138 * KB + KB * i, [W2C], f32) for i in range(2)]
        ppf = [at(140 * KB + KB * i, [W2C], f32) for i in range(2)]
        pp_hi = [at(142 * KB + KB * i, [W2C], f16) for i in range(PSLOTS)]
        pp_lo = [at(142 * KB + KB * i + 512, [W2C], f16) for i in range(PSLOTS)]
        y2 = [at(94 * KB + 3 * KB * i, [D], f32) for i in range(2)]
        y3 = [at(101 * KB + 3 * KB * i, [D], f32) for i in range(2)]
        r2_ld = [at(108 * KB, [D], f32), at(112 * KB, [D], f32)]

        fold_junk = at(95 * KB, [2, HC], bf16)
        asd2 = asd[:, 0:2, :].rearrange("p a t -> p (a t)")
        uv2 = uv[:, 0:2, :].rearrange("p a t -> p (a t)")

        def bank(i, n=512, parts=P):
            return psum[0:parts, 512 * i:512 * i + n]

        p_key, p_lo3, p_min, p_max, p_rng = bank(0, EG * P), bank(1, EG * P), bank(2, EG * P, NB), bank(3, EG * P, NB), bank(4, 2 * NB, 1)
        p_c = [bank(5, T * WD), bank(6, T * WD)]
        p_deg, p_flag = bank(7, T), psum[0:1, 512 * 7 + 16:512 * 7 + 17]
        p_ag = [psum[:, 1536 * i:1536 * i + NP] for i in range(2)]
        p_neg = psum[:, 512 * 6:512 * 6 + NP // 2].bitcast(f16)
        p_out = [psum[:, 1024 * i:1024 * i + D] for i in range(2)]
        p_tr = [psum[:, 2048 + 1024 * i:2048 + 1024 * i + D] for i in range(2)]
        p_as, p_rows = bank(0, 8 * T), bank(1, P, 80)
        p_x = [psum[:, 1024 + 1024 * i:2048 + 1024 * i] for i in range(2)]
        p_att = psum[:, 0:512 * C1].rearrange("p (j n) -> p j n", j=C1)
        p_h = psum[:, 512 * 6:512 * 8]
        p_att2 = [psum[:, 2048 * i:2048 * i + 2048].rearrange("p (j n) -> p j n", j=C2) for i in range(2)]

        x1_d = nc.dram_tensor("x1_scratch", [T, P, D], f32).ap()
        r1_d = nc.dram_tensor("r1_scratch", [T, P, HC], f32).ap()
        r2_d = nc.dram_tensor("r2_scratch", [T, P, D], f32).ap()
        neg_d = nc.dram_tensor("neg_scratch", [P, T * NP], bf16).ap()
        as_d = nc.dram_tensor("as_scratch", [8 * NP], f32).ap()
        uv_d = nc.dram_tensor("uv_scratch", [8 * NP], f32).ap()
        as2_d = nc.dram_tensor("as2_scratch", [2 * NP], f32).ap()
        uv2_d = nc.dram_tensor("uv2_scratch", [2 * NP], f32).ap()

        def everywhere(row):
            return row.rearrange("(a n) -> a n", a=1).to_broadcast([P, row.shape[0]])

        S = {n: sem(n) for n in """
            pads edges iotas ident_ok x_in keys_prep keys_tr tile_rows ranges_f ranges_t ranges_i lo_oh_ok key_shift
            keys_ready keys_free blk_done blk_free w_in0 w_in1 w_hi w_lo
            diag_ok chi_ok clo_ok deg_done dinv_ok flag_done flag_ok xs_hi_ok xs_lo_ok
            ag_done ag_hi_ok ag_lo_ok neg_tr neg_ok gcn_done gcn_read gcn_var gcn_rstd x1_ok x1_out
            x1_tr x1t_hi_ok x1t_lo_ok wt_ok as_done as_ok as_tr as_rows as_dram asr0 asr1 max_ok
            xl_done xl_hi_ok xl_lo_ok xl_ones r1_done r1_sb r1_out0 r1_out1 neg_out
            uv_free uv_ok uv_tr uv_rows uv_dram uvr0 uvr1 ex_ok g_ok pf_ok ph_ok pl_ok p_free att_read 
            ln_var ln_rstd h1_ok h1_tr h1t_hi_ok h1t_lo_ok r_in0 r_in1 
            wt2_ok as2_done as2_ok as2_tr as2_rows as2_dram asr2 neg_in 
            xl2_done xl2_hi_ok xl2_lo_ok xl2_ones r2_done r2_sb r2_out0 r2_out1 xb_in0 xb_in1
            uv2_ok uv2_tr uv2_rows uv2_dram uvr2 ex2_ok g2_ok pf2_ok ph2_ok pl2_ok p2_free att2_read
            ln2_var ln2_rstd r2_in0 r2_in1 r2_used out_ok out_dma
            par_b0 par_a1s par_a1d par_br1 par_b1 par_g1 par_be1 par_a2s par_a2d par_br2 par_b2 par_g2 par_be2
            half_ok dve
            """.split()}
        block = ctx.enter_context(nc.Block())


        def step_count():
            here, before = 0, 0

            def steps_done(new=0):
                nonlocal here
                here += new
                return here + before

            def enter_loop(i, steps):
                nonlocal before
                outside = (here, before)
                before = before + i * steps
                return outside

            def leave_loop(outside, rounds, steps):
                nonlocal here, before
                assert here - outside[0] == steps, (here - outside[0], steps)
                here, before = outside[0] + rounds * steps, outside[1]

            return steps_done, enter_loop, leave_loop

        W_ROWS = [(W0, KD), (W1, KD), (Wr1, KD), (W2, KH), (Wr2, KH)]
        W_FIRST = [sum(k for _, k in W_ROWS[:i]) for i in range(5)]
        W_STAGE = [wst0, wst, wst, wst2, wst2]
        W_PARTS = [(w0_hi, w0_lo), (w1_hi, w1_lo), (wr1_hi, wr1_lo), (w2_hi, w2_lo), (w2_hi, w2_lo)]

        @block.sync
        def _(sp):
            full = ET - 1
            sp.wait_ge(S["pads"], 2)
            for a, b in ((src, src_i), (dst, dst_i)):
                sp.dma_start(b[:, 0:2, :], a[0:2 * P * P].rearrange("(g p e) -> p g e", g=2, p=P)).then_inc(S["edges"], 16)
                sp.dma_start(b[0:full - 2 * P, 2, :], a[2 * P * P:full * P].rearrange("(p e) -> p e", e=P)).then_inc(S["edges"], 16)
                sp.dma_start(b[full - 2 * P:full - 2 * P + 1, 2, 0:E - full * P],
                             a[full * P:E].rearrange("(p e) -> p e", p=1)).then_inc(S["edges"], 16)

            def weights(i):
                for k in range(W_ROWS[i][1]):
                    q = W_FIRST[i] + k
                    if q >= 2:
                        sp.wait_ge(S["w_hi"], q - 1)
                        sp.wait_ge(S["w_lo"], q - 1)
                    sp.dma_start(W_STAGE[i][q % 2], W_ROWS[i][0][k * P:(k + 1) * P, :]).then_inc(S[f"w_in{q % 2}"], 16)

            weights(0)
            sp.wait_ge(S["pads"], 3)
            sp.dma_start(x_sb[:, 0:T - 1, :], x[0:(T - 1) * P, :].rearrange("(t p) d -> p t d", p=P)).then_inc(S["x_in"], 16)
            sp.dma_start(x_sb[0:LAST, T - 1, :], x[(T - 1) * P:N, :]).then_inc(S["x_in"], 16)
            sp.wait_ge(S["neg_ok"], T)
            sp.dma_start(neg_d, neg.rearrange("p t n -> p (t n)")).then_inc(S["neg_out"], 16)
            for t in range(T):
                sp.wait_ge(S["x1_ok"], t + 1)
                sp.dma_start(x1_d[t], x1_sb[:, t, :]).then_inc(S["x1_out"], 16)
            sp.wait_ge(S["gcn_done"], T)
            weights(1)
            sp.wait_ge(S["xl_done"], T)
            weights(2)
            for t in range(T):
                sp.wait_ge(S["r1_sb"], t + 3)
                sp.dma_start(r1_d[t], r_st[t % 2]).then_inc(S[f"r1_out{t % 2}"], 16)
            sp.wait_ge(S["r1_out0"], 16 * (T // 2))
            sp.wait_ge(S["r1_out1"], 16 * (T // 2))
            sp.wait_ge(S["uv_ok"], 1)
            for t in range(T):
                slot, before = t % C1 % 2, [u for u in range(t) if u % C1 % 2 == t % C1 % 2]
                if before:
                    sp.wait_ge(S["h1_ok"], before[-1] + 1)
                sp.dma_start(r_ld[slot], r1_d[t]).then_inc(S[f"r_in{slot}"], 16)
            sp.wait_ge(S["p_free"], 2 * H * T + PSLOTS)
            weights(3)
            sp.wait_ge(S["neg_out"], 16)
            sp.wait_ge(S["h1_tr"], T)
            sp.wait_ge(S["wt2_ok"], 1)
            sp.dma_start(neg2.rearrange("p t n -> p (t n)"), neg_d).then_inc(S["neg_in"], 16)
            sp.wait_ge(S["xl2_done"], T)
            weights(4)
            sp.wait_ge(S["x1_out"], 16 * T)
            for t in range(T):
                if t >= 2:
                    sp.wait_ge(S["r2_sb"], t + 1)
                sp.dma_start(xb_ld[t % 2], x1_d[t]).then_inc(S[f"xb_in{t % 2}"], 16)
                if t >= 1:
                    sp.wait_ge(S["r2_sb"], t + 2)
                    sp.dma_start(r2_d[t - 1], r2_st[(t - 1) % 2]).then_inc(S[f"r2_out{(t - 1) % 2}"], 16)
            sp.wait_ge(S["r2_sb"], T + 2)
            sp.dma_start(r2_d[T - 1], r2_st[(T - 1) % 2]).then_inc(S[f"r2_out{(T - 1) % 2}"], 16)
            sp.wait_ge(S["r2_out0"], 16 * (T // 2))
            sp.wait_ge(S["r2_out1"], 16 * (T // 2))
            sp.sem_inc(S["out_dma"], 16)
            sp.wait_ge(S["uv2_ok"], 1)
            for t in range(T):
                if t >= 2:
                    sp.wait_ge(S["r2_used"], t - 1)
                sp.dma_start(r2_ld[t % 2], r2_d[t]).then_inc(S[f"r2_in{t % 2}"], 16)
                if t >= 1:
                    sp.wait_ge(S["out_ok"], t)
                    sp.dma_start(out[(t - 1) * P:t * P, :], y3[(t - 1) % 2]).then_inc(S["out_dma"], 16)
            sp.wait_ge(S["out_ok"], T)
            sp.dma_start(out[(T - 1) * P:N, :], y3[(T - 1) % 2][0:LAST]).then_inc(S["out_dma"], 16)
            sp.wait_ge(S["out_dma"], 16 * (T + 1))

        @block.gpsimd
        def _(pool):
            pool.memset(src_i[:, 2, :], 0).then_inc(S["pads"], 1)
            pool.memset(dst_i[:, 2, :], PAD_DST).then_inc(S["pads"], 1)
            pool.memset(x_sb[:, T - 1, :], 0.0).then_inc(S["pads"], 1)
            pool.memset(ident, 0.0).then_inc(S["ident_ok"], 1)
            pool.memset(ident_h, 0.0).then_inc(S["ident_ok"], 1)
            pool.wait_ge(S["ident_ok"], 2)
            for m in (ident, ident_h):
                pool.affine_select(out=m, in_=m, compare_op=ALU.not_equal, fill=1.0, base=0,
                                   pattern=[[-1, P]], channel_multiplier=1).then_inc(S["ident_ok"], 1)
            loose = dict(channel_multiplier=0, allow_small_or_imprecise_dtypes=True)
            pool.iota(jt, [[1, P], [0, LO_STEP]], base=0, **loose).then_inc(S["iotas"], 1)
            pool.iota(key_io.rearrange("p (k j) g -> p k j g", k=T), [[KS, T], [1, WD], [0, G]], base=0,
                      channel_multiplier=0).then_inc(S["iotas"], 1)
            pool.iota(t_io, [[1, EG * P]], base=0, **loose).then_inc(S["iotas"], 1)
            for c in range(2):
                pool.iota(thr[:, c:c + 1], [[0, 1]], base=c * WD, channel_multiplier=WD,
                          allow_small_or_imprecise_dtypes=True).then_inc(S["iotas"], 1)
            pool.memset(zero_h, 0.0).then_inc(S["iotas"], 1)
            pool.memset(ones_h, 1.0).then_inc(S["iotas"], 1)
            pool.memset(ones_f, 1.0).then_inc(S["iotas"], 1)
            pool.memset(half, -0.5).then_inc(S["half_ok"], 1)

            def param(name, row, slot, n=HC):
                pool.dma_start(par_rows[:, slot, 0:n], everywhere(row)).then_inc(S[name], 16)

            flat = "h c -> (h c)"
            param("par_b0", b0, 2, D)
            param("par_br1", br1, 3)
            param("par_a1s", a_src1.rearrange(flat), 0)
            param("par_a1d", a_dst1.rearrange(flat), 1)

            pool.wait_ge(S["half_ok"], 1)
            pool.wait_ge(S["dinv_ok"], 1)
            pool.tensor_tensor(dinv, deg, half, ALU.pow).then_inc(S["dinv_ok"], 1)
            pool.sem_inc(S["gcn_rstd"], 1)
            with pool.Fori(0, T) as t:
                pool.wait_ge(S["gcn_var"], t + 1)
                pool.wait_ge(S["gcn_rstd"], t + 1)
                pool.tensor_tensor(rstd, veps, half[:, 0:1], ALU.pow).then_inc(S["gcn_rstd"], 1)
            pool.wait_ge(S["x1_ok"], T)
            pool.wait_ge(S["x1_tr"], T)
            pool.wait_ge(S["x1_out"], 16 * T)
            ones_col = xl_hi.rearrange("p t h n -> p (t h) n")
            pool.memset(ones_col[:, :, HID:HID + 2], 1.0).then_inc(S["xl_ones"], 1)

            pool.wait_ge(S["as_rows"], 1)
            pool.dma_start(as_d.rearrange("(r p) -> r p", p=P), rows_sb).then_inc(S["as_dram"], 16)
            pool.wait_ge(S["as_dram"], 16)
            pool.wait_ge(S["w_lo"], W_FIRST[2])
            for h in range(H):
                if h >= 2:
                    pool.wait_ge(S["max_ok"], h // 2)
                pool.dma_start(as_row[h % 2], everywhere(as_d[h * NP:(h + 1) * NP])).then_inc(S[f"asr{h % 2}"], 16)
            pool.wait_ge(S["wt_ok"], 1)
            pool.wait_ge(S["x1_ok"], T)
            param("par_b1", b1, 0)
            param("par_g1", g1, 1)
            param("par_be1", be1, 2)

            pool.wait_ge(S["uv_rows"], 1)
            pool.dma_start(uv_d.rearrange("(r p) -> r p", p=P), rows_sb).then_inc(S["uv_dram"], 16)
            pool.wait_ge(S["uv_dram"], 16)
            pool.wait_ge(S["r1_sb"], T + 2)
            pool.sem_inc(S["ln_rstd"], 1)
            with pool.Fori(0, 2) as c:
                for h in range(H):
                    pool.wait_ge(S["uv_free"], c * H + h + 1)
                    for part in range(2):
                        pool.dma_start(uv_row[h % 2][part],
                                       everywhere(uv_d[ds((part * H + h) * NP + c * W1C, W1C)])).then_inc(S[f"uvr{h % 2}"], 16)
                with pool.Fori(0, C1) as j:
                    pool.wait_ge(S["ln_var"], c * C1 + j + 1)
                    pool.wait_ge(S["ln_rstd"], c * C1 + j + 1)
                    pool.tensor_tensor(rstd, veps, half[:, 0:1], ALU.pow).then_inc(S["ln_rstd"], 1)

            pool.wait_ge(S["h1_ok"], T)
            param("par_a2s", a_src2.rearrange(flat), 0, D)
            param("par_a2d", a_dst2.rearrange(flat), 1, D)
            pool.dma_start(par_rows[:, 3, 0:D], everywhere(br2)).then_inc(S["par_br2"], 16)
            pool.dma_start(par_rows[:, 2, 0:D], everywhere(be2)).then_inc(S["par_be2"], 16)
            pool.wait_ge(S["h1t_hi_ok"], T)
            pool.memset(xl2_hi[:, :, D:D + 2], 1.0).then_inc(S["xl2_ones"], 1)
            pool.wait_ge(S["as2_rows"], 1)
            pool.dma_start(as2_d.rearrange("(r p) -> r p", p=P), rows_sb[0:2 * T]).then_inc(S["as2_dram"], 16)
            pool.wait_ge(S["as2_dram"], 16)
            pool.dma_start(as2_row, everywhere(as2_d[0:NP])).then_inc(S["asr2"], 16)
            pool.wait_ge(S["wt2_ok"], 1)
            pool.dma_start(par_rows[:, 0, 0:D], everywhere(b2)).then_inc(S["par_b2"], 16)
            pool.dma_start(par_rows[:, 1, 0:D], everywhere(g2)).then_inc(S["par_g2"], 16)
            pool.wait_ge(S["uv2_rows"], 1)
            pool.dma_start(uv2_d.rearrange("(r p) -> r p", p=P), rows_sb[0:2 * T]).then_inc(S["uv2_dram"], 16)
            pool.wait_ge(S["uv2_dram"], 16)
            pool.wait_ge(S["r2_done"], T)
            for part, row in enumerate((u2_row, v2_row)):
                pool.dma_start(row, everywhere(uv2_d[part * NP:(part + 1) * NP])).then_inc(S["uvr2"], 16)
            pool.sem_inc(S["ln2_rstd"], 1)
            with pool.Fori(0, 2 * T) as n:
                pool.wait_ge(S["ln2_var"], n + 1)
                pool.wait_ge(S["ln2_rstd"], n + 1)
                pool.tensor_tensor(rstd, veps, half[:, 0:1], ALU.pow).then_inc(S["ln2_rstd"], 1)

        @block.tensor
        def _(pe):
            pe.wait_ge(S["ident_ok"], 4)
            pe.wait_ge(S["keys_prep"], 4)
            for g in range(EG):
                pe.transpose(p_key[:, g * P:(g + 1) * P], key_f[:, g, :], ident)
                last = pe.transpose(p_lo3[:, g * P:(g + 1) * P], lo_f[:, g, :], ident)
            last.then_inc(S["keys_tr"], 1)
            for g in range(EG):
                for m, o in enumerate((p_min, p_max)):
                    last = pe.matmul(o[:, g * P:(g + 1) * P], tmm[:, m, g:g + 1].to_broadcast([P, NB]), ident,
                                     start=True, stop=True)
            last.then_inc(S["tile_rows"], 1)
            pe.wait_ge(S["ranges_f"], 1)
            for c in range(2):
                last = pe.matmul(p_rng[:, c * NB:(c + 1) * NB], span[:, c:c + 1], ident[0:NB, 0:NB], start=True, stop=True)
            last.then_inc(S["ranges_t"], 1)

            pe.wait_ge(S["ranges_i"], 1)
            pe.wait_ge(S["iotas"], 8)
            pe.wait_ge(S["lo_oh_ok"], -(-NG * G // LO_STEP))
            pe.sem_inc(S["keys_free"], KRING)
            count = pe.alloc_register("pe_groups")
            pe.reg_mov(count, 0)
            r0, r1 = pe.alloc_register("pe_first"), pe.alloc_register("pe_end")

            def count_block(b, par):
                pe.reg_load(r0, range_i[0:1, ds(b, 1)])
                pe.reg_load(r1, range_i[0:1, ds(b + NB, 1)])
                first, end = pe.snap(r0, min_val=0, max_val=NG - 1), pe.snap(r1, min_val=1, max_val=NG)
                pe.wait_ge(S["blk_free"], b + 1)
                pe.matmul(p_c[par], zero_h[:, 0:P], zero_h, start=True, stop=False)
                with pe.Fori(first, end) as g:
                    n = pe.snap(count)
                    pe.wait_ge(S["keys_ready"], n + 2)
                    for i in range(G):
                        last = pe.matmul(p_c[par], lo_oh[:, :, ds(g * G + i, 1)].rearrange("p a c -> p (a c)"),
                                         ring[:, ds(n % KRING, 1), :, i].rearrange("p a c -> p (a c)"),
                                         start=False, stop=False)
                    last.then_inc(S["keys_free"], 1)
                    pe.reg_add(count, count, 1)
                pe.matmul(p_c[par], zero_h[:, 0:P], zero_h, start=False, stop=True).then_inc(S["blk_done"], 1)

            with pe.Fori(0, NB // 2) as i:
                count_block(i * 2, 0)
                count_block(i * 2 + 1, 1)

            pe.wait_ge(S["chi_ok"], 1)
            pe.wait_ge(S["clo_ok"], 1)
            for t in range(T):
                for n, c in enumerate((c_hi, c_lo)):
                    for k in range(T):
                        last = pe.matmul(p_deg[:, t:t + 1], c[:, k, t * P:(t + 1) * P], ones_h[:, 0:1],
                                         start=(n == 0 and k == 0), stop=(n == 1 and k == T - 1))
            last.then_inc(S["deg_done"], 1)
            pe.wait_ge(S["dinv_ok"], 3)
            pe.matmul(p_flag, over, ones_f, start=True, stop=True).then_inc(S["flag_done"], 1)
            pe.wait_ge(S["flag_ok"], 1)
            big = pe.alloc_register("big_counts")
            pe.reg_load(big, flag_i[0:1, 0:1])

            pe.wait_ge(S["xs_hi_ok"], T)
            pe.wait_ge(S["xs_lo_ok"], T)
            pe.sem_inc(S["ag_hi_ok"], 2)
            pe.sem_inc(S["ag_lo_ok"], 2)
            with pe.Fori(0, KD // 2) as i:
                for par in range(2):
                    c = i * 2 + par
                    pe.wait_ge(S["ag_hi_ok"], c + 1)
                    pe.wait_ge(S["ag_lo_ok"], c + 1)

                    def aggregate(counts, k):
                        for n, part in enumerate((xs_hi, xs_lo)):
                            for a, w in ((0, 512), (512, 512), (1024, NP - 1024)):
                                ins = pe.matmul(p_ag[par][:, a:a + w], part[:, k, ds(c * P, P)], counts[:, k, a:a + w],
                                                start=(counts is c_hi and k == 0 and n == 0),
                                                stop=(counts is c_hi and k == T - 1 and n == 1))
                        return ins

                    for k in range(T - 1):
                        aggregate(c_hi, k)
                    with pe.If_ne(big, 0):
                        for k in range(T):
                            aggregate(c_lo, k)
                    aggregate(c_hi, T - 1).then_inc(S["ag_done"], 1)

            pe.wait_ge(S["ag_hi_ok"], KD + 2)
            for t in range(T):
                if t >= 1:
                    pe.wait_ge(S["neg_ok"], t)
                for k in range(T):
                    last = pe.transpose(p_neg[:, k * P:(k + 1) * P], c_hi[:, k, t * P:(t + 1) * P], ident_h)
                last.then_inc(S["neg_tr"], 1)

            def product(o, lhs, rhs, t, kn, width):
                for k in range(kn):
                    for n, part in enumerate(lhs):
                        for m, w in enumerate(rhs[:2 - n]):
                            for a in range(0, width, 512):
                                b = min(a + 512, width)
                                ins = pe.matmul(o[:, a:b], part[:, k, ds(t * P, P)], w[:, k, a:b],
                                                start=(k == 0 and n == 0 and m == 0), stop=(k == kn - 1 and n == 1))
                return ins

            pe.wait_ge(S["w_hi"], W_FIRST[1])
            pe.wait_ge(S["w_lo"], W_FIRST[1])
            pe.wait_ge(S["ag_lo_ok"], KD + 2)
            pe.sem_inc(S["gcn_read"], 2)
            with pe.Fori(0, T // 2) as i:
                for par in range(2):
                    t = i * 2 + par
                    pe.wait_ge(S["gcn_read"], t + 1)
                    product(p_out[par], (ag_hi, ag_lo), (w0_hi, w0_lo), t, KD, D).then_inc(S["gcn_done"], 1)

            pe.wait_ge(S["neg_ok"], T)
            pe.sem_inc(S["x1t_lo_ok"], 2)
            for t in range(T):
                pe.wait_ge(S["x1_ok"], t + 1)
                pe.wait_ge(S["x1t_lo_ok"], t + 1)
                for k in range(KD):
                    last = pe.transpose(p_tr[t % 2][:, k * P:(k + 1) * P], x1_sb[:, t, k * P:(k + 1) * P], ident)
                last.then_inc(S["x1_tr"], 1)

            pe.wait_ge(S["wt_ok"], 1)
            pe.wait_ge(S["x1t_lo_ok"], T + 2)
            for t in range(T):
                last = product(p_as[:, 8 * t:8 * t + 8], (x1t_hi, x1t_lo), (wt_hi, wt_lo), t, KD, 8)
            last.then_inc(S["as_done"], 1)
            pe.wait_ge(S["as_ok"], 1)
            pe.transpose(p_rows, asd.rearrange("p a t -> p (a t)"), ident).then_inc(S["as_tr"], 1)

            pe.wait_ge(S["w_lo"], W_FIRST[2])
            pe.sem_inc(S["xl_lo_ok"], 2)
            with pe.Fori(0, T // 2) as i:
                for par in range(2):
                    t = i * 2 + par
                    pe.wait_ge(S["xl_lo_ok"], t + 1)
                    product(p_x[par], (x1t_hi, x1t_lo), (w1_hi, w1_lo), t, KD, HC).then_inc(S["xl_done"], 1)
            pe.wait_ge(S["w_lo"], W_FIRST[3])
            pe.wait_ge(S["xl_lo_ok"], T + 2)
            pe.sem_inc(S["r1_sb"], 2)
            with pe.Fori(0, T // 2) as i:
                for par in range(2):
                    t = i * 2 + par
                    pe.wait_ge(S["r1_sb"], t + 1)
                    product(p_x[par], (x1t_hi, x1t_lo), (wr1_hi, wr1_lo), t, KD, HC).then_inc(S["r1_done"], 1)

            pe.wait_ge(S["uv_ok"], 1)
            pe.transpose(p_rows, uv.rearrange("p a t -> p (a t)"), ident).then_inc(S["uv_tr"], 1)
            pe.wait_ge(S["uv_rows"], 1)
            pe.wait_ge(S["r1_sb"], T + 2)

            pe.wait_ge(S["xl_ones"], 1)
            pe.sem_inc(S["att_read"], 1)
            with pe.Fori(0, 2) as c:
                with pe.Fori(0, H // 2) as hp:
                    for hpar in range(2):
                        h = hp * 2 + hpar
                        ch = c * H + h
                        pe.wait_ge(S["att_read"], ch + 1)
                        for k in range(T):
                            pe.wait_ge(S["pl_ok"], ch * T + k + 1)
                            for j in range(C1):
                                for m, (p, xl, w) in enumerate(((p_hi, xl_hi, HID + 1), (p_hi, xl_lo, HID), (p_lo, xl_hi, HID + 1))):
                                    last = pe.matmul(p_att[:, j, 0:w], p[k % PSLOTS][:, j * P:(j + 1) * P],
                                                     xl[:, k, ds(h, 1), 0:w].rearrange("p a n -> p (a n)"),
                                                     start=(k == 0 and m == 0), stop=(k == T - 1 and m == 2))
                            last.then_inc(S["p_free"], 1)
                for j in range(C1):
                    t = c * C1 + j
                    pe.wait_ge(S["h1_ok"], t + 1)
                    pe.wait_ge(S["h1t_lo_ok"], t + 1)
                    for k in range(KH):
                        last = pe.transpose(p_h[:, k * P:(k + 1) * P], att[:, j, k * P:(k + 1) * P], ident)
                    last.then_inc(S["h1_tr"], 1)

            pe.wait_ge(S["wt2_ok"], 1)
            pe.wait_ge(S["h1t_lo_ok"], T + 1)
            pe.wait_ge(S["att_read"], 2 * H + 1)
            for t in range(T):
                last = product(p_as[:, 2 * t:2 * t + 2], (h1t_hi, h1t_lo), (wt_hi[:, :, 0:2], wt_lo[:, :, 0:2]), t, KH, 2)
            last.then_inc(S["as2_done"], 1)
            pe.wait_ge(S["as2_ok"], 1)
            pe.transpose(p_rows[0:2 * T], asd2, ident).then_inc(S["as2_tr"], 1)

            pe.wait_ge(S["w_lo"], W_FIRST[4])
            pe.sem_inc(S["xl2_lo_ok"], 2)
            with pe.Fori(0, T // 2) as i:
                for par in range(2):
                    t = i * 2 + par
                    pe.wait_ge(S["xl2_lo_ok"], t + 1)
                    product(p_x[par], (h1t_hi, h1t_lo), (w2_hi, w2_lo), t, KH, D).then_inc(S["xl2_done"], 1)
            pe.wait_ge(S["w_lo"], W_FIRST[4] + KH)
            pe.wait_ge(S["xl2_lo_ok"], T + 2)
            pe.sem_inc(S["r2_sb"], 2)
            with pe.Fori(0, T // 2) as i:
                for par in range(2):
                    t = i * 2 + par
                    pe.wait_ge(S["r2_sb"], t + 1)
                    product(p_x[par], (h1t_hi, h1t_lo), (w2_hi, w2_lo), t, KH, D).then_inc(S["r2_done"], 1)
            pe.wait_ge(S["uv2_ok"], 1)
            pe.transpose(p_rows[0:2 * T], uv2, ident).then_inc(S["uv2_tr"], 1)
            pe.wait_ge(S["uv2_rows"], 1)
            pe.wait_ge(S["r2_sb"], T + 2)

            pe.wait_ge(S["xl2_ones"], 1)
            pe.sem_inc(S["att2_read"], 2)
            with pe.Fori(0, T // C2) as c:
                pe.wait_ge(S["att2_read"], c + 1)
                for k in range(T):
                    pe.wait_ge(S["pl2_ok"], c * T + k + 1)
                    for j in range(C2):
                        for m, (p, xl, w) in enumerate(((pp_hi, xl2_hi, D + 1), (pp_hi, xl2_lo, D), (pp_lo, xl2_hi, D + 1))):
                            for a, b in ((0, 512), (512, w)):
                                last = pe.matmul(psum[:, ds((c % 2) * 2048 + j * 1024 + a, b - a)],
                                                 p[k % PSLOTS][:, j * P:(j + 1) * P], xl[:, k, a:b],
                                                 start=(k == 0 and m == 0), stop=(k == T - 1 and m == 2))
                    last.then_inc(S["p2_free"], 1)

        @block.scalar
        def _(act):
            awaited = act.alloc_register("awaited")

            def cast(out_, in_, signal, scale=1.0):
                act.activation(out_, in_, ACT.Copy, scale=scale).then_inc(signal, 1)

            def weights(i):
                for k in range(W_ROWS[i][1]):
                    q = W_FIRST[i] + k
                    act.wait_ge(S[f"w_in{q % 2}"], 16 * (q // 2 + 1))
                    cast(W_PARTS[i][0][:, k, :], W_STAGE[i][q % 2], S["w_hi"], WSCALE)

            weights(0)
            act.wait_ge(S["w_lo"], KD)
            act.wait_ge(S["w_hi"], KD)
            act.wait_ge(S["ranges_i"], 1)
            act.sem_inc(S["blk_free"], 2)
            with act.Fori(0, NB // 2) as i:
                for par in range(2):
                    b = i * 2 + par
                    act.reg_mov(awaited, b + 1)
                    act.wait_ge(S["iotas"], 8)
                    act.wait_ge(S["blk_done"], awaited)
                    cast(CT[:, :, ds(b * WD, WD)], p_c[par].rearrange("p (k j) -> p k j", k=T), S["blk_free"])
            act.wait_ge(S["x_in"], 32)
            act.wait_ge(S["dinv_ok"], 2)
            for t in range(T):
                act.activation(xs_hi[:, t, :], x_sb[:, t, :], ACT.Copy, scale=dinv[:, t:t + 1]).then_inc(S["xs_hi_ok"], 1)
            with act.Fori(0, KD // 2) as i:
                for par in range(2):
                    c = i * 2 + par
                    act.reg_mov(awaited, c + 1)
                    act.wait_ge(S["iotas"], 8)
                    act.wait_ge(S["ag_done"], awaited)
                    cast(ag_hi[:, ds(c, 1), :].rearrange("p a n -> p (a n)"), p_ag[par], S["ag_hi_ok"])
            act.wait_ge(S["gcn_done"], T)
            for t in range(T):
                act.wait_ge(S["x1_tr"], t + 1)
                cast(x1t_hi[:, :, t * P:(t + 1) * P], p_tr[t % 2].rearrange("p (k n) -> p k n", k=KD), S["x1t_hi_ok"])
            act.wait_ge(S["neg_tr"], T)
            weights(1)
            for t in range(T):
                act.wait_ge(S["xl_done"], t + 1)
                if t == 0:
                    act.wait_ge(S["x1_out"], 16 * T)
                cast(xl_hi[:, t, :, 0:HID], p_x[t % 2].rearrange("p (h n) -> p h n", h=H), S["xl_hi_ok"], 1 / WSCALE)
            weights(2)

            act.wait_ge(S["r1_done"], T)
            act.wait_ge(S["uv_ok"], 1)
            act.wait_ge(S["neg_out"], 16)
            act.sem_inc(S["uv_free"], 2)
            act.sem_inc(S["pf_ok"], 2)
            act.sem_inc(S["p_free"], PSLOTS)
            with act.Fori(0, 2) as c:
                with act.Fori(0, H // 2) as hp:
                    for hpar in range(2):
                        h = hp * 2 + hpar
                        ch = c * H + h

                        def high(k):
                            act.wait_ge(S["pf_ok"], ch * T + k + 3)
                            act.wait_ge(S["p_free"], ch * T + k + 1)
                            cast(p_hi[k % PSLOTS], pf[k % 2], S["ph_ok"])

                        act.wait_ge(S[f"uvr{hpar}"], (c * 2 + hp + 1) * 32)
                        for k in range(T):
                            act.reg_mov(awaited, ch * T + k + 1)
                            act.wait_ge(S["iotas"], 8)
                            act.wait_ge(S["pf_ok"], awaited)
                            act.activation(e1[k % 2], uv_row[hpar][0], ACT.Exp,
                                           bias=asd[:, ds(h, 1), k:k + 1].rearrange("p a b -> p (a b)")).then_inc(S["ex_ok"], 1)
                            act.activation(e2[k % 2], uv_row[hpar][1], ACT.Exp,
                                           bias=as_s[:, ds(h, 1), k:k + 1].rearrange("p a b -> p (a b)")).then_inc(S["ex_ok"], 1)
                            if k >= 1:
                                high(k - 1)
                        high(T - 1)
                        act.sem_inc(S["uv_free"], 1)
                for j in range(C1):
                    t = c * C1 + j
                    act.reg_mov(awaited, t + 1)
                    act.wait_ge(S["iotas"], 8)
                    act.wait_ge(S["h1_tr"], awaited)
                    cast(h1t_hi[:, :, ds(t * P, P)], p_h.rearrange("p (k n) -> p k n", k=KH), S["h1t_hi_ok"])

            weights(3)
            for t in range(T):
                act.wait_ge(S["xl2_done"], t + 1)
                cast(xl2_hi[:, t, 0:D], p_x[t % 2][:, 0:D], S["xl2_hi_ok"], 1 / WSCALE)
            weights(4)

            act.wait_ge(S["r2_done"], T)
            act.wait_ge(S["uvr2"], 32)
            act.sem_inc(S["pf2_ok"], 2)
            act.sem_inc(S["p2_free"], PSLOTS)
            with act.Fori(0, T // C2) as c:
                def high2(k):
                    act.wait_ge(S["pf2_ok"], c * T + k + 3)
                    act.wait_ge(S["p2_free"], c * T + k + 1)
                    cast(pp_hi[k % PSLOTS], ppf[k % 2], S["ph2_ok"])

                for k in range(T):
                    act.reg_mov(awaited, c * T + k + 1)
                    act.wait_ge(S["iotas"], 8)
                    act.wait_ge(S["pf2_ok"], awaited)
                    act.activation(ee1[k % 2], u2_row[:, ds(c * W2C, W2C)], ACT.Exp, bias=asd[:, 0, k:k + 1]).then_inc(S["ex2_ok"], 1)
                    act.activation(ee2[k % 2], v2_row[:, ds(c * W2C, W2C)], ACT.Exp, bias=as_s[:, 0, k:k + 1]).then_inc(S["ex2_ok"], 1)
                    if k >= 1:
                        high2(k - 1)
                high2(T - 1)

        @block.vector
        def _(dve):
            steps_done, enter_loop, leave_loop = step_count()
            awaited = dve.alloc_register("awaited")

            def weights(i, fold=None):
                for k in range(W_ROWS[i][1]):
                    q = W_FIRST[i] + k
                    dve.wait_ge(S[f"w_in{q % 2}"], 16 * (q // 2 + 1))
                    if fold:
                        fold(k, W_STAGE[i][q % 2])
                    dve.wait_ge(S["w_hi"], q + 1)
                    dve.scalar_tensor_tensor(W_PARTS[i][1][:, k, :], W_STAGE[i][q % 2], WSCALE, W_PARTS[i][0][:, k, :],
                                             ALU.mult, ALU.subtract).then_inc(S["w_lo"], 1)

            dve.wait_ge(S["edges"], 96)
            dve.tensor_copy(dst_f, dst_i).then_inc(S["dve"], 1)
            dve.wait_ge(S["dve"], steps_done(1))
            dve.tensor_scalar(hi_i, src_i, 7, None, ALU.arith_shift_right).then_inc(S["dve"], 1)
            dve.wait_ge(S["dve"], steps_done(1))
            dve.tensor_scalar(lo_i, src_i, P - 1, None, ALU.bitwise_and).then_inc(S["dve"], 1)
            dve.wait_ge(S["dve"], steps_done(1))
            dve.scalar_tensor_tensor(key_f, hi_i, float(KS), dst_f, ALU.mult, ALU.add).then_inc(S["keys_prep"], 1)
            dve.tensor_copy(lo_f, lo_i).then_inc(S["keys_prep"], 1)
            dve.tensor_reduce(tmm[:, 0, :], dst_f, axis=AX.X, op=ALU.min).then_inc(S["keys_prep"], 1)
            dve.tensor_reduce(tmm[:, 1, :], dst_f, axis=AX.X, op=ALU.max).then_inc(S["keys_prep"], 1)
            dve.wait_ge(S["keys_tr"], 1)
            dve.tensor_copy(key_b[:, 0, :], p_key[:, 0:NG * G]).then_inc(S["dve"], 1)
            dve.wait_ge(S["dve"], steps_done(1))
            dve.tensor_copy(lo_t, p_lo3[:, 0:NG * G]).then_inc(S["dve"], 1)
            dve.wait_ge(S["dve"], steps_done(1))
            dve.wait_ge(S["tile_rows"], 1)
            dve.wait_ge(S["iotas"], 8)
            dve.tensor_scalar(r_a, p_max, thr[:, 0:1], None, ALU.is_ge).then_inc(S["dve"], 1)
            dve.wait_ge(S["dve"], steps_done(1))
            dve.scalar_tensor_tensor(r_b, p_min, thr[:, 1:2], r_a, ALU.is_lt, ALU.mult).then_inc(S["dve"], 1)
            dve.wait_ge(S["dve"], steps_done(1))
            dve.scalar_tensor_tensor(r_c, r_b, -RANGE_BIG, t_io, ALU.mult, ALU.add).then_inc(S["dve"], 1)
            dve.wait_ge(S["dve"], steps_done(1))
            dve.scalar_tensor_tensor(r_d, t_io, 1.0, r_b, ALU.add, ALU.mult).then_inc(S["dve"], 1)
            dve.wait_ge(S["dve"], steps_done(1))
            dve.tensor_reduce(span[:, 0:1], r_c, axis=AX.X, op=ALU.min).then_inc(S["dve"], 1)
            dve.wait_ge(S["dve"], steps_done(1))
            dve.tensor_reduce(span[:, 1:2], r_d, axis=AX.X, op=ALU.max).then_inc(S["dve"], 1)
            dve.wait_ge(S["dve"], steps_done(1))
            dve.tensor_scalar(span[:, 0:1], span[:, 0:1], RANGE_BIG, None, ALU.add).then_inc(S["dve"], 1)
            dve.wait_ge(S["dve"], steps_done(1))
            dve.tensor_scalar(span[:, 1:2], span[:, 1:2], 1.0, None, ALU.max).then_inc(S["dve"], 1)
            dve.wait_ge(S["dve"], steps_done(1))
            dve.tensor_scalar(endm1, span[:, 1:2], -1.0, None, ALU.add).then_inc(S["dve"], 1)
            dve.wait_ge(S["dve"], steps_done(1))
            dve.tensor_tensor(span[:, 0:1], span[:, 0:1], endm1, ALU.min).then_inc(S["ranges_f"], 1)
            dve.wait_ge(S["ranges_t"], 1)
            dve.tensor_copy(range_t, p_rng).then_inc(S["dve"], 1)
            dve.wait_ge(S["dve"], steps_done(1))
            dve.tensor_scalar(range_t[:, NB:2 * NB], range_t[:, NB:2 * NB], float(G - 1), None, ALU.add).then_inc(S["dve"], 1)
            dve.wait_ge(S["dve"], steps_done(1))
            dve.tensor_scalar(range_i, range_t, G.bit_length() - 1, None, ALU.arith_shift_right).then_inc(S["ranges_i"], 1)

            for a in range(0, NG * G, LO_STEP):
                w = min(LO_STEP, NG * G - a)
                dve.tensor_tensor(lo_oh[:, :, a:a + w], lo_t[:, a:a + w].unsqueeze(1).to_broadcast([P, P, w]),
                                  jt[:, :, 0:w], ALU.is_equal).then_inc(S["lo_oh_ok"], 1)
            weights(0)

            dve.wait_ge(S["ranges_i"], 1)
            count = dve.alloc_register("dve_groups")
            dve.reg_mov(count, 0)
            dve.sem_inc(S["keys_ready"], 1)
            r0, r1 = dve.alloc_register("dve_first"), dve.alloc_register("dve_end")

            def key_block(b, par):
                dve.reg_load(r0, range_i[0:1, ds(b, 1)])
                dve.reg_load(r1, range_i[0:1, ds(b + NB, 1)])
                first, end = dve.snap(r0, min_val=0, max_val=NG - 1), dve.snap(r1, min_val=1, max_val=NG)
                dve.wait_ge(S["keys_ready"], dve.snap(count) + 1)
                dve.tensor_scalar(key_b[:, 1 - par, :], key_b[:, par, :], float(-WD), None, ALU.add).then_inc(S["key_shift"], 1)
                with dve.Fori(first, end) as g:
                    n = dve.snap(count)
                    dve.wait_ge(S["keys_free"], n + 1)
                    dve.tensor_tensor(ring[:, ds(n % KRING, 1), :, :].rearrange("p a c g -> p (a c) g"), key_io,
                                      key_b[:, par, ds(g * G, G)].unsqueeze(1).to_broadcast([P, T * WD, G]),
                                      ALU.is_equal).then_inc(S["keys_ready"], 1)
                    dve.reg_add(count, count, 1)
                dve.wait_ge(S["key_shift"], b + 1)

            with dve.Fori(0, NB // 2) as i:
                key_block(i * 2, 0)
                key_block(i * 2 + 1, 1)

            dve.wait_ge(S["blk_free"], NB + 2)
            for k in range(T):
                dg = CT[:, k, k * P:(k + 1) * P]
                dve.tensor_tensor(dg, dg, ident, ALU.add).then_inc(S["diag_ok"], 1)
            dve.wait_ge(S["diag_ok"], T)
            dve.wait_ge(S["blk_done"], NB)
            dve.tensor_copy(c_hi, CT).then_inc(S["chi_ok"], 1)
            dve.wait_ge(S["chi_ok"], 1)
            dve.tensor_tensor(c_lo, CT, c_hi, ALU.subtract).then_inc(S["clo_ok"], 1)
            dve.wait_ge(S["deg_done"], 1)
            dve.tensor_copy(deg, p_deg).then_inc(S["dinv_ok"], 1)
            dve.tensor_scalar(zz[:, 0, :], p_deg, float(F16_EXACT), None, ALU.is_gt).then_inc(S["dve"], 1)
            dve.wait_ge(S["dve"], steps_done(1))
            dve.tensor_reduce(over, zz[:, 0, :], axis=AX.X, op=ALU.max).then_inc(S["dve"], 1)
            dve.wait_ge(S["dve"], steps_done(1))
            dve.wait_ge(S["dinv_ok"], 2)
            dve.tensor_scalar(dinv_s, dinv, 1 / WSCALE, None, ALU.mult).then_inc(S["dinv_ok"], 1)
            dve.wait_ge(S["flag_done"], 1)
            dve.tensor_copy(flag_i[0:1], p_flag).then_inc(S["flag_ok"], 1)
            for t in range(T):
                dve.wait_ge(S["xs_hi_ok"], t + 1)
                dve.scalar_tensor_tensor(xs_lo[:, t, :], x_sb[:, t, :], dinv[:, t:t + 1], xs_hi[:, t, :],
                                         ALU.mult, ALU.subtract).then_inc(S["xs_lo_ok"], 1)
            with dve.Fori(0, KD // 2) as i:
                for par in range(2):
                    c = i * 2 + par
                    dve.wait_ge(S["ag_hi_ok"], c + 3)
                    hi = ag_hi[:, ds(c, 1), :].rearrange("p a n -> p (a n)")
                    lo = ag_lo[:, ds(c, 1), :].rearrange("p a n -> p (a n)")
                    dve.tensor_tensor(lo, p_ag[par], hi, ALU.subtract).then_inc(S["ag_lo_ok"], 1)
            dve.wait_ge(S["ag_done"], KD)
            for t in range(T):
                dve.wait_ge(S["neg_tr"], t + 1)
                dve.tensor_scalar(neg[:, t, :], p_neg, 0.0, NEG_BIG, ALU.is_equal, ALU.mult).then_inc(S["neg_ok"], 1)

            def moments(y, width, signal):
                for m in range(2):
                    ins = dve.bn_stats(stats[:, m, :], y[:, m * width // 2:(m + 1) * width // 2])
                ins.then_inc(S["dve"], 1)
                dve.reg_mov(awaited, steps_done(1))
                dve.wait_ge(S["iotas"], 8)
                dve.wait_ge(S["dve"], awaited)
                dve.bn_aggr(mv, stats.rearrange("p a b -> p (a b)")).then_inc(S["dve"], 1)
                dve.wait_ge(S["dve"], steps_done(1))
                dve.tensor_scalar(veps, mv[:, 1:2], LN_EPS, None, ALU.add).then_inc(signal, 1)

            dve.wait_ge(S["ag_lo_ok"], KD + 2)
            dve.wait_ge(S["par_b0"], 16)
            with dve.Fori(0, T // 2) as i:
                kept = enter_loop(i, 2 * 3)
                for par in range(2):
                    t = i * 2 + par
                    xt = x_sb[:, ds(t, 1), :].rearrange("p a n -> p (a n)")
                    y = y0[:, par, :]
                    dve.wait_ge(S["gcn_done"], t + 1)
                    dve.scalar_tensor_tensor(y, p_out[par], dinv_s[:, ds(t, 1)], xt, ALU.mult, ALU.add).then_inc(S["gcn_read"], 1)
                    dve.wait_ge(S["gcn_read"], t + 3)
                    dve.tensor_tensor(y, y, par_rows[:, 2, 0:D], ALU.add).then_inc(S["dve"], 1)
                    dve.wait_ge(S["dve"], steps_done(1))
                    moments(y, D, S["gcn_var"])
                    dve.wait_ge(S["gcn_rstd"], t + 2)
                    dve.tensor_scalar(xt, y, mv[:, 0:1], rstd, ALU.subtract, ALU.mult).then_inc(S["x1_ok"], 1)
                    dve.wait_ge(S["x1_ok"], t + 1)
                leave_loop(kept, T // 2, 2 * 3)
            for t in range(T):
                dve.wait_ge(S["x1t_hi_ok"], t + 1)
                dve.tensor_tensor(x1t_lo[:, :, t * P:(t + 1) * P], p_tr[t % 2].rearrange("p (k n) -> p k n", k=KD),
                                  x1t_hi[:, :, t * P:(t + 1) * P], ALU.subtract).then_inc(S["x1t_lo_ok"], 1)

            def folded(width, heads):
                def fold(k, stage):
                    for j in range(2 * heads):
                        a = slice(j % heads * width, (j % heads + 1) * width)
                        ins = dve.tensor_tensor_reduce(out=fold_junk[:, j // heads, a], in0=stage[:, a],
                                                       in1=par_rows[:, j // heads, a], scale=1.0, scalar=0.0,
                                                       op0=ALU.mult, op1=ALU.add, accum_out=wt[:, k, j:j + 1])
                    ins.then_inc(S["dve"], 1)
                    dve.wait_ge(S["dve"], steps_done(1))
                return fold

            dve.wait_ge(S["par_a1s"], 16)
            dve.wait_ge(S["par_a1d"], 16)
            weights(1, folded(HID, H))
            dve.tensor_scalar(wt_hi[:, 0:KD, :], wt[:, 0:KD, :], WSCALE, None, ALU.mult).then_inc(S["dve"], 1)
            dve.wait_ge(S["dve"], steps_done(1))
            dve.scalar_tensor_tensor(wt_lo[:, 0:KD, :], wt[:, 0:KD, :], WSCALE, wt_hi[:, 0:KD, :],
                                     ALU.mult, ALU.subtract).then_inc(S["wt_ok"], 1)
            dve.wait_ge(S["as_done"], 1)
            dve.tensor_scalar(asd, p_as.rearrange("p (t a) -> p a t", a=8), 1 / WSCALE, None, ALU.mult).then_inc(S["as_ok"], 1)
            dve.wait_ge(S["as_tr"], 1)
            dve.tensor_copy(rows_sb, p_rows).then_inc(S["as_rows"], 1)
            dve.tensor_scalar(as_s, asd[:, 0:H, :], SLOPE, None, ALU.mult).then_inc(S["dve"], 1)
            dve.wait_ge(S["dve"], steps_done(1))

            def max_as(row, col, t, out_, mask):
                dve.wait_ge(S["dve"], steps_done() - 1)
                dve.tensor_tensor_reduce(out=out_, in0=mask[:, t, :], in1=row, scale=1.0, scalar=NEG_BIG,
                                         op0=ALU.add, op1=ALU.max, accum_out=mx[:, col, t:t + 1]).then_inc(S["dve"], 1)
                steps_done(1)

            for t in range(T):
                dve.wait_ge(S["xl_hi_ok"], t + 1)
                dve.scalar_tensor_tensor(xl_lo[:, t, :, 0:HID], p_x[t % 2].rearrange("p (h n) -> p h n", h=H), 1 / WSCALE,
                                         xl_hi[:, t, :, 0:HID], ALU.mult, ALU.subtract).then_inc(S["xl_lo_ok"], 1)
                for h in range(2):
                    if t == 0:
                        dve.wait_ge(S[f"asr{h}"], 16)
                    max_as(as_row[h], h, t, junk[h], neg)
            dve.wait_ge(S["dve"], steps_done())
            dve.drain().then_inc(S["max_ok"], 1)
            weights(2)
            dve.wait_ge(S["par_br1"], 16)
            for t in range(T):
                dve.wait_ge(S["r1_done"], t + 1)
                if t >= 2:
                    dve.wait_ge(S[f"r1_out{t % 2}"], 16 * (t // 2))
                dve.scalar_tensor_tensor(r_st[t % 2], p_x[t % 2], 1 / WSCALE, par_rows[:, 3, :], ALU.mult, ALU.add).then_inc(S["r1_sb"], 1)
                for h in range(2):
                    if t == 0:
                        dve.wait_ge(S[f"asr{h}"], 32)
                    max_as(as_row[h], 2 + h, t, junk[h], neg)
            dve.wait_ge(S["dve"], steps_done())

            def shifts(heads, signal):
                ad, z, m = asd[:, heads:2 * heads, :], zz[:, 0:heads, :], mm[:, 0:heads, :]
                dve.tensor_tensor(z, mx[:, 0:heads, :], ad, ALU.add).then_inc(S["dve"], 1)
                dve.wait_ge(S["dve"], steps_done(1))
                dve.scalar_tensor_tensor(m, z, SLOPE, z, ALU.mult, ALU.max).then_inc(S["dve"], 1)
                dve.wait_ge(S["dve"], steps_done(1))
                dve.tensor_tensor(uv[:, 0:heads, :], ad, m, ALU.subtract).then_inc(S["dve"], 1)
                dve.wait_ge(S["dve"], steps_done(1))
                dve.scalar_tensor_tensor(uv[:, heads:2 * heads, :], ad, SLOPE, m, ALU.mult, ALU.subtract).then_inc(signal, 1)

            shifts(H, S["uv_ok"])
            dve.wait_ge(S["uv_tr"], 1)
            dve.wait_ge(S["as_dram"], 16)
            dve.tensor_copy(rows_sb, p_rows).then_inc(S["uv_rows"], 1)

            dve.wait_ge(S["r1_out0"], 16 * (T // 2))
            dve.wait_ge(S["r1_out1"], 16 * (T // 2))
            for p in ("par_b1", "par_g1", "par_be1"):
                dve.wait_ge(S[p], 16)
            dve.sem_inc(S["h1t_lo_ok"], 1)
            with dve.Fori(0, 2) as c:
                outer = enter_loop(c, (H // 2) * 2 * 2 + C1 * 5)
                with dve.Fori(0, H // 2) as hp:
                    inner = enter_loop(hp, 2 * 2)
                    for hpar in range(2):
                        h = hp * 2 + hpar
                        ch = c * H + h

                        def low(k):
                            dve.wait_ge(S["ph_ok"], ch * T + k + 1)
                            dve.tensor_tensor(p_lo[k % PSLOTS], pf[k % 2], p_hi[k % PSLOTS], ALU.subtract).then_inc(S["pl_ok"], 1)

                        for k in range(T):
                            n = ch * T + k
                            dve.wait_ge(S["ex_ok"], n * 2 + 2)
                            dve.tensor_tensor(e1[k % 2], e1[k % 2], e2[k % 2], ALU.max).then_inc(S["g_ok"], 1)
                            if k >= 1:
                                low(k - 1)
                            dve.wait_ge(S["g_ok"], n + 1)
                            if k >= 2:
                                dve.wait_ge(S["pl_ok"], n - 1)
                            dve.scalar_tensor_tensor(pf[k % 2], e1[k % 2], 1.0, CT[:, k, ds(c * W1C, W1C)],
                                                     ALU.min, ALU.mult).then_inc(S["pf_ok"], 1)
                        low(T - 1)
                        dve.wait_ge(S["pl_ok"], ch * T + T)
                        dve.wait_ge(S["p_free"], ch * T + T + PSLOTS)
                        dve.tensor_scalar(ssum, p_att[:, :, HID:HID + 1].rearrange("p j n -> p (j n)"), SOFTMAX_EPS, None, ALU.add).then_inc(S["dve"], 1)
                        dve.wait_ge(S["dve"], steps_done(1))
                        dve.reciprocal(rsum, ssum).then_inc(S["dve"], 1)
                        dve.wait_ge(S["dve"], steps_done(1))
                        for j in range(C1):
                            ins = dve.scalar_tensor_tensor(att[:, j, ds(h * HID, HID)], p_att[:, j, 0:HID], rsum[:, j:j + 1],
                                                           par_rows[:, 0, ds(h * HID, HID)], ALU.mult, ALU.add)
                        ins.then_inc(S["att_read"], 1)
                        dve.wait_ge(S["att_read"], ch + 2)
                    leave_loop(inner, H // 2, 2 * 2)

                def h1_low(j):
                    t = c * C1 + j
                    dve.wait_ge(S["h1t_hi_ok"], t + 1)
                    dve.tensor_tensor(h1t_lo[:, :, ds(t * P, P)], p_h.rearrange("p (k n) -> p k n", k=KH),
                                      h1t_hi[:, :, ds(t * P, P)], ALU.subtract).then_inc(S["h1t_lo_ok"], 1)

                for j in range(C1):
                    t = c * C1 + j
                    y = att[:, j, :]
                    moments(y, HC, S["ln_var"])
                    dve.wait_ge(S["ln_rstd"], t + 2)
                    dve.tensor_scalar(y, y, mv[:, 0:1], rstd, ALU.subtract, ALU.mult).then_inc(S["dve"], 1)
                    dve.wait_ge(S["dve"], steps_done(1))
                    dve.tensor_tensor(y, y, par_rows[:, 1, :], ALU.mult).then_inc(S["dve"], 1)
                    dve.wait_ge(S["dve"], steps_done(1))
                    dve.tensor_tensor(y, y, par_rows[:, 2, :], ALU.add).then_inc(S["dve"], 1)
                    dve.wait_ge(S["dve"], steps_done(1))
                    if j >= 1:
                        h1_low(j - 1)
                    slots = (C1 + 1) // 2 if j % 2 == 0 else C1 // 2
                    dve.wait_ge(S[f"r_in{j % 2}"], (c * slots + j // 2 + 1) * 16)
                    dve.scalar_tensor_tensor(y, y, 0.0, r_ld[j % 2], ALU.max, ALU.add).then_inc(S["h1_ok"], 1)
                h1_low(C1 - 1)
                leave_loop(outer, 2, (H // 2) * 2 * 2 + C1 * 5)

            dve.wait_ge(S["h1_tr"], T)
            dve.wait_ge(S["par_a2s"], 16)
            dve.wait_ge(S["par_a2d"], 16)
            weights(3, folded(D, 1))
            dve.tensor_scalar(wt_hi[:, :, 0:2], wt[:, :, 0:2], WSCALE, None, ALU.mult).then_inc(S["dve"], 1)
            dve.wait_ge(S["dve"], steps_done(1))
            dve.scalar_tensor_tensor(wt_lo[:, :, 0:2], wt[:, :, 0:2], WSCALE, wt_hi[:, :, 0:2],
                                     ALU.mult, ALU.subtract).then_inc(S["wt2_ok"], 1)
            dve.wait_ge(S["as2_done"], 1)
            dve.tensor_scalar(asd[:, 0:2, :], p_as[:, 0:2 * T].rearrange("p (t a) -> p a t", a=2), 1 / WSCALE, None,
                              ALU.mult).then_inc(S["as2_ok"], 1)
            dve.wait_ge(S["as2_tr"], 1)
            dve.tensor_copy(rows_sb[0:2 * T], p_rows[0:2 * T]).then_inc(S["as2_rows"], 1)
            dve.tensor_scalar(as_s[:, 0, :], asd[:, 0, :], SLOPE, None, ALU.mult).then_inc(S["dve"], 1)
            dve.wait_ge(S["dve"], steps_done(1))
            for t in range(T):
                dve.wait_ge(S["xl2_hi_ok"], t + 1)
                dve.scalar_tensor_tensor(xl2_lo[:, t, 0:D], p_x[t % 2][:, 0:D], 1 / WSCALE, xl2_hi[:, t, 0:D],
                                         ALU.mult, ALU.subtract).then_inc(S["xl2_lo_ok"], 1)
                if t == 0:
                    dve.wait_ge(S["asr2"], 16)
                    dve.wait_ge(S["neg_in"], 16)
                max_as(as2_row, 0, t, junk2[t % 2], neg2)
            dve.wait_ge(S["dve"], steps_done())
            shifts(1, S["uv2_ok"])
            weights(4)
            dve.wait_ge(S["par_br2"], 16)
            dve.wait_ge(S["par_be2"], 16)
            dve.tensor_tensor(par_rows[:, 3, 0:D], par_rows[:, 3, 0:D], par_rows[:, 2, 0:D], ALU.add).then_inc(S["dve"], 1)
            dve.wait_ge(S["dve"], steps_done(1))
            for t in range(T):
                dve.wait_ge(S[f"xb_in{t % 2}"], 16 * (t // 2 + 1))
                dve.tensor_tensor(xb_ld[t % 2], xb_ld[t % 2], par_rows[:, 3, 0:D], ALU.add).then_inc(S["dve"], 1)
                dve.wait_ge(S["dve"], steps_done(1))
                dve.wait_ge(S["r2_done"], t + 1)
                if t >= 2:
                    dve.wait_ge(S[f"r2_out{t % 2}"], 16 * (t // 2))
                dve.scalar_tensor_tensor(r2_st[t % 2], p_x[t % 2][:, 0:D], 1 / WSCALE, xb_ld[t % 2],
                                         ALU.mult, ALU.add).then_inc(S["r2_sb"], 1)
            dve.wait_ge(S["uv2_tr"], 1)
            dve.wait_ge(S["as2_dram"], 16)
            dve.tensor_copy(rows_sb[0:2 * T], p_rows[0:2 * T]).then_inc(S["uv2_rows"], 1)

            dve.wait_ge(S["par_b2"], 16)
            dve.wait_ge(S["par_g2"], 16)
            with dve.Fori(0, T // C2) as c:
                kept = enter_loop(c, 2 + C2 * 6)

                def low2(k):
                    dve.wait_ge(S["ph2_ok"], c * T + k + 1)
                    dve.tensor_tensor(pp_lo[k % PSLOTS], ppf[k % 2], pp_hi[k % PSLOTS], ALU.subtract).then_inc(S["pl2_ok"], 1)

                for k in range(T):
                    n = c * T + k
                    dve.wait_ge(S["ex2_ok"], n * 2 + 2)
                    dve.tensor_tensor(ee1[k % 2], ee1[k % 2], ee2[k % 2], ALU.max).then_inc(S["g2_ok"], 1)
                    if k >= 1:
                        low2(k - 1)
                    dve.wait_ge(S["g2_ok"], n + 1)
                    if k >= 2:
                        dve.wait_ge(S["pl2_ok"], n - 1)
                    dve.scalar_tensor_tensor(ppf[k % 2], ee1[k % 2], 1.0, CT[:, k, ds(c * W2C, W2C)],
                                             ALU.min, ALU.mult).then_inc(S["pf2_ok"], 1)
                low2(T - 1)
                dve.wait_ge(S["pl2_ok"], c * T + T)
                dve.wait_ge(S["p2_free"], c * T + T + PSLOTS)
                acc = psum[:, ds((c % 2) * 2048, 2048)].rearrange("p (j n) -> p j n", j=C2)
                dve.tensor_scalar(ssum[:, 0:C2], acc[:, :, D:D + 1].rearrange("p j n -> p (j n)"), SOFTMAX_EPS, None, ALU.add).then_inc(S["dve"], 1)
                dve.wait_ge(S["dve"], steps_done(1))
                dve.reciprocal(rsum[:, 0:C2], ssum[:, 0:C2]).then_inc(S["dve"], 1)
                dve.wait_ge(S["dve"], steps_done(1))
                for j in range(C2):
                    y, z = y2[j], y3[j]
                    ins = dve.scalar_tensor_tensor(y, acc[:, j, 0:D], rsum[:, j:j + 1], par_rows[:, 0, 0:D], ALU.mult, ALU.add)
                ins.then_inc(S["att2_read"], 1)
                dve.wait_ge(S["att2_read"], c + 3)
                for j in range(C2):
                    t = c * C2 + j
                    y, z = y2[j], y3[j]
                    moments(y, D, S["ln2_var"])
                    dve.wait_ge(S["ln2_rstd"], t * 2 + 2)
                    dve.tensor_scalar(y, y, mv[:, 0:1], rstd, ALU.subtract, ALU.mult).then_inc(S["dve"], 1)
                    dve.wait_ge(S["dve"], steps_done(1))
                    dve.tensor_tensor(y, y, par_rows[:, 1, 0:D], ALU.mult).then_inc(S["dve"], 1)
                    dve.wait_ge(S["dve"], steps_done(1))
                    dve.wait_ge(S[f"r2_in{j}"], (c + 1) * 16)
                    dve.tensor_tensor(y, y, r2_ld[j], ALU.add).then_inc(S["r2_used"], 1)
                    dve.wait_ge(S["r2_used"], t + 1)
                    moments(y, D, S["ln2_var"])
                    dve.wait_ge(S["ln2_rstd"], t * 2 + 3)
                    dve.wait_ge(S["out_dma"], (t + 1) * 16)
                    dve.tensor_scalar(z, y, mv[:, 0:1], rstd, ALU.subtract, ALU.mult).then_inc(S["out_ok"], 1)
                leave_loop(kept, T // C2, 2 + C2 * 6)


_INS = ["x", "src", "dst", "L0_gnn_W", "L0_gnn_b", "L1_gnn_W1", "L1_gnn_a_src1", "L1_gnn_a_dst1", "L1_gnn_b1",
        "L1_gnn_g1", "L1_gnn_be1", "L1_gnn_Wr1", "L1_gnn_br1", "L1_gnn_W2", "L1_gnn_a_src2", "L1_gnn_a_dst2",
        "L1_gnn_b2", "L1_gnn_g2", "L1_gnn_be2", "L1_gnn_Wr2", "L1_gnn_br2"]


def kernel(**inputs):
    import numpy as _np
    import concourse.bacc as _bacc
    from concourse import mybir as _mybir
    from concourse.bass_utils import run_bass_kernel_spmd as _run

    nc = _bacc.Bacc("TRN2", target_bir_lowering=False, num_devices=1)
    arrays, args = {}, []
    for name in _INS:
        a = _np.ascontiguousarray(inputs[name])
        arrays[f"in_{name}_dram"] = a
        args.append(nc.dram_tensor(f"in_{name}_dram", a.shape, _mybir.dt.from_np(a.dtype), kind="ExternalInput").ap())
    out = nc.dram_tensor("out_dram", (N, D), _mybir.dt.float32, kind="ExternalOutput").ap()
    gnn_program(nc, *args, out)
    r = _run(nc, [arrays], core_ids=[0])
    return r.results[0]["out_dram"]
```

```python
from contextlib import ExitStack

import concourse.bass as bass
from concourse import mybir

P = 128
N = 1250
T = -(-N // P)
NP = T * P
LAST = N - (T - 1) * P
E = 41250
ET = -(-E // P)
D = 768
KD = D // P
H, HID = 4, 256
HC = H * HID
KH = HC // P
HS = HID + 2
XS = D + 2
WSCALE = 64.0
LN_EPS = 1e-5
SOFTMAX_EPS = 1e-16
SLOPE = 0.2
NEG_BIG = -3e38

WD = 32
NB = NP // WD
G = 4
NG = -(-ET // G)
EG = -(-ET // P)
KS = 2 * NP
PAD_DST = 2000
KRING = 4
LO_STEP = 16
RANGE_BIG = 1024.0
F16_EXACT = 2048

C1 = 5
W1C = C1 * P
PSLOTS = 5
ESLOTS = 3
E_BACK = [ESLOTS if k >= ESLOTS else T - max(j for j in range(T) if j % ESLOTS == k) + k for k in range(T)]
E_CREDIT = max(E_BACK)
EVICT_AT = 3
SHIFT_AT = 4
P2SLOTS = 10
C2 = 2
W2C = C2 * P

KB = 1024


def gnn_program(nc, x, src, dst, W0, b0, W1, a_src1, a_dst1, b1, g1, be1, Wr1, br1,
                W2, a_src2, a_dst2, b2, g2, be2, Wr2, br2, out):
    dt = mybir.dt
    f32, f16, bf16, i32, i16, u16 = dt.float32, dt.float16, dt.bfloat16, dt.int32, dt.int16, dt.uint16
    ALU, AX, ACT = mybir.AluOpType, mybir.AxisListType, mybir.ActivationFunctionType
    ds = bass.ds
    bytes_of = {f32: 4, i32: 4, f16: 2, bf16: 2, i16: 2, u16: 2}

    with ExitStack() as ctx:
        def sem(name):
            return ctx.enter_context(nc.semaphore(name))

        ARENA = 207 * KB
        arena = ctx.enter_context(nc.sbuf_tensor("arena", [P, ARENA // 4], f32))
        psum = ctx.enter_context(nc.psum_tensor("psum", [P, 8 * 512], f32))

        def at(byte, shape, dtype, parts=P):
            n = 1
            for s in shape:
                n *= s
            size = n * bytes_of[dtype]
            assert byte % 4 == 0 and byte + size <= ARENA, (byte, shape)
            v = arena[0:parts, byte // 4:byte // 4 + -(-size // 4)]
            if dtype != f32:
                v = v.bitcast(dtype)
            v = v[:, 0:n]
            if len(shape) == 2:
                v = v.rearrange("p (a b) -> p a b", a=shape[0])
            elif len(shape) == 3:
                v = v.rearrange("p (a b c) -> p a b c", a=shape[0], b=shape[1])
            return v

        pos = 0

        def small(shape, dtype, parts=P):
            nonlocal pos
            v = at(pos, shape, dtype, parts)
            n = 1
            for s in shape:
                n *= s
            pos += -(-n * bytes_of[dtype] // 4) * 4
            return v

        ident = small([P], f32)
        ident_h = small([P], f16)
        ones_h = small([2], f16)
        half = small([T], f32)
        flag_i = small([1], i32)
        over = small([1], f32)
        ones_f = small([1], f32)
        deg = small([T], f32)
        dinv = small([T], f32)
        dinv_s = small([T], f32)
        stats = small([2, 6], f32)
        mv = small([2], f32)
        veps = small([1], f32)
        rstd = small([1], f32)
        asd_w = small([8, T], f32)
        asd = small([8, T], f32)
        as_s = small([4, T], f32)
        mx = small([4, T], f32)
        zz = small([4, T], f32)
        mm = small([4, T], f32)
        uv = small([8, T], f32)
        ssum = small([C1], f32)
        rsum = small([C1], f32)
        range_i = small([2 * NB], i32, 1)
        thr = small([2], f32, NB)
        span = small([2], f32, NB)
        endm1 = small([1], f32, NB)
        tmm = small([2, EG], f32)
        rows_sb = small([P], f32, 80)
        assert pos <= 4 * KB, pos
        par_rows = at(4 * KB, [4, HC], f32)
        CT = at(20 * KB, [T, NP], u16)
        assert T * NP * 2 == 25 * KB

        lo_oh = at(45 * KB, [P, NG * G], f16)
        x_sb = at(126 * KB, [T, D], f32)
        w0_hi = at(156 * KB, [KD, D], f16)
        w0_lo = at(165 * KB, [KD, D], f16)
        src_i = at(174 * KB, [EG, P], i32)
        dst_i = at(174 * KB + 1536, [EG, P], i32)
        hi_i = at(177 * KB, [EG, P], i32)
        lo_i = at(177 * KB + 1536, [EG, P], i32)
        dst_f = at(180 * KB, [EG, P], f32)
        key_f = at(180 * KB + 1536, [EG, P], f32)
        lo_f = at(183 * KB, [EG, P], f32)
        key_b = at(185 * KB, [2, NG * G], i16)
        lo_t = at(187 * KB, [NG * G], f16)
        jt = at(188 * KB, [P, LO_STEP], f16)
        key_io = at(192 * KB, [T * WD, G], i16)
        ring = at(195 * KB, [KRING, T * WD, G], f16)
        zero_h = at(205 * KB, [T * WD], f16)
        t_io = at(20 * KB, [EG * P], f32, NB)
        r_a = at(22 * KB, [EG * P], f32, NB)
        r_b = at(24 * KB, [EG * P], f32, NB)
        r_c = at(26 * KB, [EG * P], f32, NB)
        r_d = at(28 * KB, [EG * P], f32, NB)
        range_t = at(30 * KB, [2 * NB], i32, 1)
        wst0 = [at(32 * KB, [D], f32), at(36 * KB, [D], f32)]

        c_hi = at(45 * KB, [T, NP], f16)
        c_lo = at(70 * KB, [T, NP], f16)
        xs_hi = at(95 * KB, [T, D], f16)
        xs_lo = at(110 * KB, [T, D], f16)
        ag_hi = at(174 * KB, [KD, NP], f16)
        ag_lo = at(189 * KB, [KD, NP], f16)
        y0 = at(95 * KB, [2, D], f32)
        x1_sb = x_sb

        neg = at(70 * KB, [T, NP], bf16)
        x1t_hi = at(111 * KB, [KD, NP], f16)
        x1t_lo = at(189 * KB, [KD, NP], f16)
        w1_hi = at(45 * KB, [KD, HC], f16)
        w1_lo = at(57 * KB, [KD, HC], f16)
        xl = at(126 * KB, [T, 2, H * HS], f16)
        xl_hi = xl[:, :, 0, :].rearrange("p t (h n) -> p t h n", h=H)
        xl_lo = xl[:, :, 1, :].rearrange("p t (h n) -> p t h n", h=H)
        wst1 = [at(103 * KB, [HC], f32), at(107 * KB, [HC], f32)]
        wr1_hi = at(176 * KB, [KD, HC], f16)
        wr1_lo = at(95 * KB, [KD, HC], f16)
        wstr1 = [at(168 * KB, [HC], f32), at(172 * KB, [HC], f32)]
        as_row = [at(45 * KB, [NP], f32), at(50 * KB, [NP], f32)]
        junk = [at(55 * KB + 2560 * i, [NP], bf16) for i in range(2)]
        r_st = [at(60 * KB, [HC], f32), at(64 * KB, [HC], f32)]
        e1 = [at(b, [W1C], f32) for b in (45 * KB, 47 * KB + 512, 178 * KB)]
        e2 = [at(b, [W1C], f32) for b in (50 * KB, 52 * KB + 512, 180 * KB + 512)]
        pf = [at(b, [W1C], f32) for b in (55 * KB, 57 * KB + 512, 183 * KB)]
        h1t_hi = at(60 * KB + 256, [KH, NP], f16)
        p_hi = [at(80 * KB + 512 + 2560 * i, [W1C], f16) for i in range(PSLOTS)]
        p_lo = [at(80 * KB + 512 + 2560 * i + 1280, [W1C], f16) for i in range(PSLOTS)]
        att = at(94 * KB, [C1, HC], f32)
        r_ld = [at(114 * KB, [HC], f32), at(118 * KB, [HC], f32)]
        uv_row = [[at(168 * KB, [W1C], f32), at(168 * KB + 2560, [W1C], f32)],
                  [at(173 * KB, [W1C], f32), at(173 * KB + 2560, [W1C], f32)]]
        h1t_lo = at(186 * KB, [KH, NP], f16)

        w2_hi = at(126 * KB, [KH, D], f16)
        w2_lo = at(138 * KB, [KH, D], f16)
        wst2 = [at(b * KB, [D], f32) for b in (150, 153, 172, 175)]
        wr2_hi = at(81 * KB, [KH, D], f16)
        wr2_lo = at(94 * KB, [KH, D], f16)
        wstr2 = [at(112 * KB, [D], f32), at(115 * KB, [D], f32)]
        neg2 = at(126 * KB, [T, NP], bf16)
        xl2_hi = at(45 * KB, [T, XS], f16)
        xl2_lo = at(156 * KB, [T, XS], f16)
        as2_row = at(172 * KB, [NP], f32)
        a_junk = at(107 * KB, [8, HID], bf16)
        a2_junk = at(178 * KB, [2, D], bf16)
        junk2 = [at(177 * KB + 2560 * i, [NP], bf16) for i in range(2)]
        r2_st = [at(182 * KB + 512, [D], f32), at(119 * KB, [D], f32)]
        xb_ld = [at(106 * KB, [D], f32), at(109 * KB, [D], f32)]
        u2_row = at(126 * KB, [NP], f32)
        v2_row = at(131 * KB, [NP], f32)
        ee1 = [at(136 * KB + KB * i, [W2C], f32) for i in range(2)]
        ee2 = [at(138 * KB + KB * i, [W2C], f32) for i in range(2)]
        ppf = [at(140 * KB + KB * i, [W2C], f32) for i in range(2)]
        pp_hi = [at(142 * KB + KB * i, [W2C], f16) for i in range(P2SLOTS)]
        pp_lo = [at(142 * KB + KB * i + 512, [W2C], f16) for i in range(P2SLOTS)]
        y2 = [at(94 * KB + 3 * KB * i, [D], f32) for i in range(2)]
        y3 = [at(101 * KB + 3 * KB * i, [D], f32) for i in range(2)]
        r2_ld = [at(108 * KB, [D], f32), at(112 * KB, [D], f32)]

        asd2 = asd[:, 0:2, :].rearrange("p a t -> p (a t)")
        uv2 = uv[:, 0:2, :].rearrange("p a t -> p (a t)")

        def bank(i, n=512, parts=P):
            return psum[0:parts, 512 * i:512 * i + n]

        p_key, p_lo3, p_min, p_max, p_rng = bank(0, EG * P), bank(1, EG * P), bank(2, EG * P, NB), bank(3, EG * P, NB), bank(4, 2 * NB, 1)
        p_c = [bank(5, T * WD), bank(6, T * WD)]
        p_deg, p_flag = bank(7, T), psum[0:1, 512 * 7 + 16:512 * 7 + 17]
        p_ag = [psum[:, 1536 * i:1536 * i + NP] for i in range(2)]
        p_neg = psum[:, 512 * 6:512 * 6 + NP // 2].bitcast(f16)
        p_out = [psum[:, 1024 * i:1024 * i + D] for i in range(2)]
        p_tr = [psum[:, 3072:3072 + D], psum[:, 0:D]]
        p_rows = bank(1, P, 80)
        p_x = [psum[:, 1024 + 1024 * i:2048 + 1024 * i] for i in range(2)]
        p_att = psum[:, 0:512 * C1].rearrange("p (j n) -> p j n", j=C1)
        p_h = psum[:, 512 * 6:512 * 8]
        p_att2 = [psum[:, 2048 * i:2048 * i + 2048].rearrange("p (j n) -> p j n", j=C2) for i in range(2)]

        x1_d = nc.dram_tensor("x1_scratch", [T, P, D], f32).ap()
        r1_d = nc.dram_tensor("r1_scratch", [T, P, HC], f32).ap()
        r2_d = nc.dram_tensor("r2_scratch", [T, P, D], f32).ap()
        neg_d = nc.dram_tensor("neg_scratch", [P, T * NP], bf16).ap()
        as_d = nc.dram_tensor("as_scratch", [8 * NP], f32).ap()
        uv_d = nc.dram_tensor("uv_scratch", [8 * NP], f32).ap()
        as2_d = nc.dram_tensor("as2_scratch", [2 * NP], f32).ap()
        uv2_d = nc.dram_tensor("uv2_scratch", [2 * NP], f32).ap()

        def everywhere(row):
            return row.rearrange("(a n) -> a n", a=1).to_broadcast([P, row.shape[0]])

        S = {n: sem(n) for n in """
            pads edges iotas ident_ok x_in keys_prep keys_tr tile_rows ranges_f ranges_t ranges_i lo_oh_ok key_shift
            keys_ready keys_free blk_done blk_free w_in0 w_in1 w_in2 w_in3 w_hi w_lo
            diag_ok chi_ok clo_ok deg_done dinv_ok flag_done flag_ok xs_hi_ok xs_lo_ok
            ag_done ag_hi_ok ag_lo_ok neg_tr neg_ok gcn_done gcn_read gcn_var gcn_rstd x1_ok x1_out
            x1_tr x1t_hi_ok x1t_lo_ok as_ok as_tr as_rows as_dram asr0 asr1 max_ok
            xl_done xl_hi_ok xl_lo_ok xl_ones r1_done r1_read r1_sb r1_out0 r1_out1 neg_out
            uv_free uv_ok uv_tr uv_rows uv_dram uvr0 uvr1 ex_ok g_ok pf_ok ph_even ph_odd pl_ok p_free att_read 
            ln_var ln_rstd h1_ok h1_tr h1t_hi_ok h1t_lo_ok r_in0 r_in1 
            as2_ok as2_tr as2_rows as2_dram asr2 neg_in 
            xl2_done xl2_hi_ok xl2_lo_ok xl2_ones r2_done r2_sb r2_out0 r2_out1 xb_in0 xb_in1
            uv2_ok uv2_tr uv2_rows uv2_dram uvr2 ex2_ok g2_ok pf2_ok ph2_ok pl2_ok p2_free att2_read
            ln2_var ln2_rstd r2_in0 r2_in1 r2_used out_ok out_dma
            par_b0 par_a1s par_a1d par_br1 par_b1 par_g1 par_be1 par_a2s par_a2d par_br2 par_b2 par_g2 par_be2
            half_ok dve
            """.split()}
        block = ctx.enter_context(nc.Block())


        def step_count():
            here, before = 0, 0

            def steps_done(new=0):
                nonlocal here
                here += new
                return here + before

            def enter_loop(i, steps):
                nonlocal before
                outside = (here, before)
                before = before + i * steps
                return outside

            def leave_loop(outside, rounds, steps):
                nonlocal here, before
                assert here - outside[0] == steps, (here - outside[0], steps)
                here, before = outside[0] + rounds * steps, outside[1]

            return steps_done, enter_loop, leave_loop

        X1_ORDER = [s for i in range(T) for s in [("tr", t) for t in (2 * i, 2 * i + 1) if t < T] + [("xl", i)]]

        W_ROWS = [(W0, KD), (W1, KD), (Wr1, KD), (W2, KH), (Wr2, KH)]
        W_FIRST = [sum(k for _, k in W_ROWS[:i]) for i in range(5)]
        W_STAGE = [wst0, wst1, wstr1, wst2, wstr2]
        W_PARTS = [(w0_hi, w0_lo), (w1_hi, w1_lo), (wr1_hi, wr1_lo), (w2_hi, w2_lo), (wr2_hi, wr2_lo)]

        @block.sync
        def _(sp):
            full = ET - 1
            sp.wait_ge(S["pads"], 2)
            for a, b in ((src, src_i), (dst, dst_i)):
                sp.dma_start(b[:, 0:2, :], a[0:2 * P * P].rearrange("(g p e) -> p g e", g=2, p=P)).then_inc(S["edges"], 16)
                sp.dma_start(b[0:full - 2 * P, 2, :], a[2 * P * P:full * P].rearrange("(p e) -> p e", e=P)).then_inc(S["edges"], 16)
                sp.dma_start(b[full - 2 * P:full - 2 * P + 1, 2, 0:E - full * P],
                             a[full * P:E].rearrange("(p e) -> p e", p=1)).then_inc(S["edges"], 16)

            def weights(i):
                for k in range(W_ROWS[i][1]):
                    q = W_FIRST[i] + k
                    slots = len(W_STAGE[i])
                    if k >= slots:
                        sp.wait_ge(S["w_hi"], q - slots + 1)
                        sp.wait_ge(S["w_lo"], q - slots + 1)
                    sp.dma_start(W_STAGE[i][k % slots], W_ROWS[i][0][k * P:(k + 1) * P, :]).then_inc(S[f"w_in{q % 4}"], 16)

            weights(0)
            sp.wait_ge(S["pads"], 3)
            sp.dma_start(x_sb[:, 0:T - 1, :], x[0:(T - 1) * P, :].rearrange("(t p) d -> p t d", p=P)).then_inc(S["x_in"], 16)
            sp.dma_start(x_sb[0:LAST, T - 1, :], x[(T - 1) * P:N, :]).then_inc(S["x_in"], 16)
            sp.wait_ge(S["neg_tr"], T)
            sp.wait_ge(S["ag_done"], KD)
            weights(1)
            sp.wait_ge(S["neg_ok"], T)
            sp.dma_start(neg_d, neg.rearrange("p t n -> p (t n)")).then_inc(S["neg_out"], 16)
            for t in range(T):
                sp.wait_ge(S["x1_ok"], t + 1)
                sp.dma_start(x1_d[t], x1_sb[:, t, :]).then_inc(S["x1_out"], 16)
            sp.wait_ge(S["gcn_done"], T)
            weights(2)
            for t in range(T):
                sp.wait_ge(S["r1_sb"], t + 1)
                sp.dma_start(r1_d[t], r_st[t % 2]).then_inc(S[f"r1_out{t % 2}"], 16)
            sp.wait_ge(S["r1_out0"], 16 * (T // 2))
            sp.wait_ge(S["r1_out1"], 16 * (T // 2))
            sp.wait_ge(S["uv_ok"], 1)

            def rows(c, h):
                sp.wait_ge(S["uv_free"], c * H + h + 1)
                for part in range(2):
                    sp.dma_start(uv_row[h % 2][part],
                                 everywhere(uv_d[(part * H + h) * NP + c * W1C:(part * H + h) * NP + (c + 1) * W1C])).then_inc(S[f"uvr{h % 2}"], 16)

            def residual(t):
                slot, before = t % C1 % 2, [u for u in range(t) if u % C1 % 2 == t % C1 % 2]
                if before:
                    sp.wait_ge(S["h1_ok"], before[-1] + 1)
                sp.dma_start(r_ld[slot], r1_d[t]).then_inc(S[f"r_in{slot}"], 16)

            sp.wait_ge(S["uv_dram"], 16)
            sp.wait_ge(S["r1_sb"], T)
            for h in range(H):
                rows(0, h)
            rows(1, 0)
            rows(1, 1)
            for t in range(C1):
                residual(t)
            rows(1, 2)
            rows(1, 3)
            residual(C1)
            residual(C1 + 1)
            sp.wait_ge(S["p_free"], 2 * H * T + PSLOTS)
            weights(3)
            for t in range(C1 + 2, T):
                residual(t)
            sp.wait_ge(S["h1_tr"], T)
            weights(4)
            sp.wait_ge(S["neg_out"], 16)
            sp.wait_ge(S["xl2_done"], T)
            sp.dma_start(neg2.rearrange("p t n -> p (t n)"), neg_d).then_inc(S["neg_in"], 16)
            sp.wait_ge(S["x1_out"], 16 * T)
            for t in range(T):
                if t >= 2:
                    sp.wait_ge(S["r2_sb"], t + 1)
                sp.dma_start(xb_ld[t % 2], x1_d[t]).then_inc(S[f"xb_in{t % 2}"], 16)
                if t >= 1:
                    sp.wait_ge(S["r2_sb"], t + 2)
                    sp.dma_start(r2_d[t - 1], r2_st[(t - 1) % 2]).then_inc(S[f"r2_out{(t - 1) % 2}"], 16)
            sp.wait_ge(S["r2_sb"], T + 2)
            sp.dma_start(r2_d[T - 1], r2_st[(T - 1) % 2]).then_inc(S[f"r2_out{(T - 1) % 2}"], 16)
            sp.wait_ge(S["r2_out0"], 16 * (T // 2))
            sp.wait_ge(S["r2_out1"], 16 * (T // 2))
            sp.sem_inc(S["out_dma"], 16)
            sp.wait_ge(S["uv2_ok"], 1)
            for t in range(T):
                if t >= 2:
                    sp.wait_ge(S["r2_used"], t - 1)
                sp.dma_start(r2_ld[t % 2], r2_d[t]).then_inc(S[f"r2_in{t % 2}"], 16)
                if t >= 1:
                    sp.wait_ge(S["out_ok"], t)
                    sp.dma_start(out[(t - 1) * P:t * P, :], y3[(t - 1) % 2]).then_inc(S["out_dma"], 16)
            sp.wait_ge(S["out_ok"], T)
            sp.dma_start(out[(T - 1) * P:N, :], y3[(T - 1) % 2][0:LAST]).then_inc(S["out_dma"], 16)
            sp.wait_ge(S["out_dma"], 16 * (T + 1))

        @block.gpsimd
        def _(pool):
            pool.memset(src_i[:, 2, :], 0).then_inc(S["pads"], 1)
            pool.memset(dst_i[:, 2, :], PAD_DST).then_inc(S["pads"], 1)
            pool.memset(x_sb[:, T - 1, :], 0.0).then_inc(S["pads"], 1)
            pool.memset(ident, 0.0).then_inc(S["ident_ok"], 1)
            pool.memset(ident_h, 0.0).then_inc(S["ident_ok"], 1)
            pool.wait_ge(S["ident_ok"], 2)
            for m in (ident, ident_h):
                pool.affine_select(out=m, in_=m, compare_op=ALU.not_equal, fill=1.0, base=0,
                                   pattern=[[-1, P]], channel_multiplier=1).then_inc(S["ident_ok"], 1)
            loose = dict(channel_multiplier=0, allow_small_or_imprecise_dtypes=True)
            pool.iota(jt, [[1, P], [0, LO_STEP]], base=0, **loose).then_inc(S["iotas"], 1)
            pool.iota(key_io.rearrange("p (k j) g -> p k j g", k=T), [[KS, T], [1, WD], [0, G]], base=0,
                      channel_multiplier=0).then_inc(S["iotas"], 1)
            pool.iota(t_io, [[1, EG * P]], base=0, **loose).then_inc(S["iotas"], 1)
            for c in range(2):
                pool.iota(thr[:, c:c + 1], [[0, 1]], base=c * WD, channel_multiplier=WD,
                          allow_small_or_imprecise_dtypes=True).then_inc(S["iotas"], 1)
            pool.memset(zero_h, 0.0).then_inc(S["iotas"], 1)
            pool.memset(ones_h, 1.0).then_inc(S["iotas"], 1)
            pool.memset(ones_f, 1.0).then_inc(S["iotas"], 1)
            pool.memset(half, -0.5).then_inc(S["half_ok"], 1)

            def param(name, row, slot, n=HC):
                pool.dma_start(par_rows[:, slot, 0:n], everywhere(row)).then_inc(S[name], 16)

            flat = "h c -> (h c)"
            param("par_b0", b0, 2, D)
            param("par_br1", br1, 3)
            param("par_a1s", a_src1.rearrange(flat), 0)
            param("par_a1d", a_dst1.rearrange(flat), 1)

            pool.wait_ge(S["half_ok"], 1)
            pool.wait_ge(S["dinv_ok"], 1)
            pool.tensor_tensor(dinv, deg, half, ALU.pow).then_inc(S["dinv_ok"], 1)
            pool.sem_inc(S["gcn_rstd"], 1)
            with pool.Fori(0, T) as t:
                pool.wait_ge(S["gcn_var"], t + 1)
                pool.wait_ge(S["gcn_rstd"], t + 1)
                pool.tensor_tensor(rstd, veps, half[:, 0:1], ALU.pow).then_inc(S["gcn_rstd"], 1)
            pool.wait_ge(S["x1_tr"], T)
            pool.wait_ge(S["x1_out"], 16 * T)
            pool.memset(xl_hi[:, :, :, HID:HID + 2], 1.0).then_inc(S["xl_ones"], 1)

            pool.wait_ge(S["as_rows"], 1)
            pool.dma_start(as_d.rearrange("(r p) -> r p", p=P), rows_sb).then_inc(S["as_dram"], 16)
            pool.wait_ge(S["as_dram"], 16)
            for h in range(2):
                pool.dma_start(as_row[h % 2], everywhere(as_d[h * NP:(h + 1) * NP])).then_inc(S[f"asr{h % 2}"], 16)
            pool.wait_ge(S["par_br1"], 16)
            for t in range(T):
                pool.wait_ge(S["r1_read"], t + 3)
                pool.tensor_tensor(r_st[t % 2], r_st[t % 2], par_rows[:, 3, :], ALU.add).then_inc(S["r1_sb"], 1)
                if t == 3:
                    for h in (2, 3):
                        pool.wait_ge(S["max_ok"], 1)
                        pool.dma_start(as_row[h % 2], everywhere(as_d[h * NP:(h + 1) * NP])).then_inc(S[f"asr{h % 2}"], 16)
            param("par_b1", b1, 0)
            param("par_g1", g1, 1)
            param("par_be1", be1, 2)

            pool.wait_ge(S["uv_rows"], 1)
            pool.dma_start(uv_d.rearrange("(r p) -> r p", p=P), rows_sb).then_inc(S["uv_dram"], 16)
            pool.sem_inc(S["ln_rstd"], 1)
            pool.sem_inc(S["pl_ok"], E_CREDIT)
            for c in range(2):
                with pool.Fori(0, H) as h:
                    for k in range(T):
                        pool.wait_ge(S["ph_odd" if k % 2 else "ph_even"], (c * H + h) * (T // 2) + k // 2 + 1)
                        pool.tensor_tensor(p_lo[k % PSLOTS], pf[k % ESLOTS], p_hi[k % PSLOTS], ALU.subtract).then_inc(S["pl_ok"], 1)
                if c == 1:
                    pool.wait_ge(S["p_free"], 2 * H * T + PSLOTS)
                    pool.memset(xl2_hi[:, :, D:D + 2], 1.0).then_inc(S["xl2_ones"], 1)
                    pool.wait_ge(S["att_read"], (2 * H + 1) * C1)
                    param("par_a2s", a_src2.rearrange(flat), 3, D)
                    param("par_a2d", a_dst2.rearrange(flat), 0, D)
                with pool.Fori(0, C1) as j:
                    pool.wait_ge(S["ln_var"], c * C1 + j + 1)
                    pool.wait_ge(S["ln_rstd"], c * C1 + j + 1)
                    pool.tensor_tensor(rstd, veps, half[:, 0:1], ALU.pow).then_inc(S["ln_rstd"], 1)

            pool.wait_ge(S["h1_ok"], T)
            param("par_g2", g2, 1, D)
            param("par_be2", be2, 2, D)
            pool.wait_ge(S["as2_ok"], 1)
            param("par_b2", b2, 0, D)
            param("par_br2", br2, 3, D)
            pool.wait_ge(S["as2_rows"], 1)
            pool.dma_start(as2_d.rearrange("(r p) -> r p", p=P), rows_sb[0:2 * T]).then_inc(S["as2_dram"], 16)
            pool.wait_ge(S["as2_dram"], 16)
            pool.dma_start(as2_row, everywhere(as2_d[0:NP])).then_inc(S["asr2"], 16)
            pool.wait_ge(S["uv2_rows"], 1)
            pool.dma_start(uv2_d.rearrange("(r p) -> r p", p=P), rows_sb[0:2 * T]).then_inc(S["uv2_dram"], 16)
            pool.wait_ge(S["uv2_dram"], 16)
            for part, row in enumerate((u2_row, v2_row)):
                pool.dma_start(row, everywhere(uv2_d[part * NP:(part + 1) * NP])).then_inc(S["uvr2"], 16)
            pool.sem_inc(S["ln2_rstd"], 1)
            pool.sem_inc(S["pl2_ok"], 2)

            def low_parts(c):
                for k in range(T):
                    pool.wait_ge(S["ph2_ok"], c * T + k + 1)
                    pool.tensor_tensor(pp_lo[k % P2SLOTS], ppf[k % 2], pp_hi[k % P2SLOTS], ALU.subtract).then_inc(S["pl2_ok"], 1)

            def roots(c):
                for i in range(2 * C2):
                    pool.wait_ge(S["ln2_var"], c * 2 * C2 + i + 1)
                    pool.wait_ge(S["ln2_rstd"], c * 2 * C2 + i + 1)
                    pool.tensor_tensor(rstd, veps, half[:, 0:1], ALU.pow).then_inc(S["ln2_rstd"], 1)

            low_parts(0)
            with pool.Fori(0, T // C2 - 1) as c:
                low_parts(c + 1)
                roots(c)
            roots(T // C2 - 1)

        @block.tensor
        def _(pe):
            pe.wait_ge(S["ident_ok"], 4)
            pe.wait_ge(S["keys_prep"], 4)
            for g in range(EG):
                pe.transpose(p_key[:, g * P:(g + 1) * P], key_f[:, g, :], ident)
                last = pe.transpose(p_lo3[:, g * P:(g + 1) * P], lo_f[:, g, :], ident)
            last.then_inc(S["keys_tr"], 1)
            for g in range(EG):
                for m, o in enumerate((p_min, p_max)):
                    last = pe.matmul(o[:, g * P:(g + 1) * P], tmm[:, m, g:g + 1].to_broadcast([P, NB]), ident,
                                     start=True, stop=True)
            last.then_inc(S["tile_rows"], 1)
            pe.wait_ge(S["ranges_f"], 1)
            for c in range(2):
                last = pe.matmul(p_rng[:, c * NB:(c + 1) * NB], span[:, c:c + 1], ident[0:NB, 0:NB], start=True, stop=True)
            last.then_inc(S["ranges_t"], 1)

            pe.wait_ge(S["ranges_i"], 1)
            pe.wait_ge(S["iotas"], 8)
            pe.wait_ge(S["lo_oh_ok"], -(-NG * G // LO_STEP))
            pe.sem_inc(S["keys_free"], KRING)
            count = pe.alloc_register("pe_groups")
            pe.reg_mov(count, 0)
            r0, r1 = pe.alloc_register("pe_first"), pe.alloc_register("pe_end")

            def count_block(b, par):
                pe.reg_load(r0, range_i[0:1, ds(b, 1)])
                pe.reg_load(r1, range_i[0:1, ds(b + NB, 1)])
                first, end = pe.snap(r0, min_val=0, max_val=NG - 1), pe.snap(r1, min_val=1, max_val=NG)
                pe.wait_ge(S["blk_free"], b + 1)
                pe.matmul(p_c[par], zero_h[:, 0:P], zero_h, start=True, stop=False)
                with pe.Fori(first, end) as g:
                    n = pe.snap(count)
                    pe.wait_ge(S["keys_ready"], n + 2)
                    for i in range(G):
                        last = pe.matmul(p_c[par], lo_oh[:, :, ds(g * G + i, 1)].rearrange("p a c -> p (a c)"),
                                         ring[:, ds(n % KRING, 1), :, i].rearrange("p a c -> p (a c)"),
                                         start=False, stop=False)
                    last.then_inc(S["keys_free"], 1)
                    pe.reg_add(count, count, 1)
                pe.matmul(p_c[par], zero_h[:, 0:P], zero_h, start=False, stop=True).then_inc(S["blk_done"], 1)

            with pe.Fori(0, NB // 2) as i:
                count_block(i * 2, 0)
                count_block(i * 2 + 1, 1)

            pe.wait_ge(S["chi_ok"], 1)
            pe.wait_ge(S["clo_ok"], 1)
            for t in range(T):
                for n, c in enumerate((c_hi, c_lo)):
                    for k in range(T):
                        last = pe.matmul(p_deg[:, t:t + 1], c[:, k, t * P:(t + 1) * P], ones_h[:, 0:1],
                                         start=(n == 0 and k == 0), stop=(n == 1 and k == T - 1))
            last.then_inc(S["deg_done"], 1)
            pe.wait_ge(S["dinv_ok"], 3)
            pe.matmul(p_flag, over, ones_f, start=True, stop=True).then_inc(S["flag_done"], 1)
            pe.wait_ge(S["flag_ok"], 1)
            big = pe.alloc_register("big_counts")
            pe.reg_load(big, flag_i[0:1, 0:1])

            pe.wait_ge(S["xs_hi_ok"], T)
            pe.wait_ge(S["xs_lo_ok"], T)
            pe.sem_inc(S["ag_hi_ok"], 2)
            pe.sem_inc(S["ag_lo_ok"], 2)
            with pe.Fori(0, KD // 2) as i:
                for par in range(2):
                    c = i * 2 + par
                    pe.wait_ge(S["ag_hi_ok"], c + 1)
                    pe.wait_ge(S["ag_lo_ok"], c + 1)

                    def aggregate(counts, k):
                        for n, part in enumerate((xs_hi, xs_lo)):
                            for a, w in ((0, 512), (512, 512), (1024, NP - 1024)):
                                ins = pe.matmul(p_ag[par][:, a:a + w], part[:, k, ds(c * P, P)], counts[:, k, a:a + w],
                                                start=(counts is c_hi and k == 0 and n == 0),
                                                stop=(counts is c_hi and k == T - 1 and n == 1))
                        return ins

                    for k in range(T - 1):
                        aggregate(c_hi, k)
                    with pe.If_ne(big, 0):
                        for k in range(T):
                            aggregate(c_lo, k)
                    aggregate(c_hi, T - 1).then_inc(S["ag_done"], 1)

            pe.wait_ge(S["ag_hi_ok"], KD + 2)
            for t in range(T):
                if t >= 1:
                    pe.wait_ge(S["neg_ok"], t)
                for k in range(T):
                    last = pe.transpose(p_neg[:, k * P:(k + 1) * P], c_hi[:, k, t * P:(t + 1) * P], ident_h)
                last.then_inc(S["neg_tr"], 1)

            def product(o, lhs, rhs, t, kn, width):
                for k in range(kn):
                    for n, part in enumerate(lhs):
                        for m, w in enumerate(rhs[:2 - n]):
                            for a in range(0, width, 512):
                                b = min(a + 512, width)
                                ins = pe.matmul(o[:, a:b], part[:, k, ds(t * P, P)], w[:, k, a:b],
                                                start=(k == 0 and n == 0 and m == 0), stop=(k == kn - 1 and n == 1))
                return ins

            pe.wait_ge(S["w_hi"], W_FIRST[1])
            pe.wait_ge(S["w_lo"], W_FIRST[1])
            pe.wait_ge(S["ag_lo_ok"], KD + 2)
            pe.sem_inc(S["gcn_read"], 2)
            with pe.Fori(0, T // 2) as i:
                for par in range(2):
                    t = i * 2 + par
                    pe.wait_ge(S["gcn_read"], t + 1)
                    product(p_out[par], (ag_hi, ag_lo), (w0_hi, w0_lo), t, KD, D).then_inc(S["gcn_done"], 1)

            pe.wait_ge(S["neg_ok"], T)
            pe.wait_ge(S["gcn_read"], T + 2)
            pe.wait_ge(S["w_lo"], W_FIRST[2])
            pe.sem_inc(S["x1t_lo_ok"], 2)
            pe.sem_inc(S["xl_lo_ok"], 2)
            for what, t in X1_ORDER:
                if what == "tr":
                    pe.wait_ge(S["x1_ok"], t + 1)
                    pe.wait_ge(S["x1t_lo_ok"], t + 1)
                    for k in range(KD):
                        last = pe.transpose(p_tr[t % 2][:, k * P:(k + 1) * P], x1_sb[:, t, k * P:(k + 1) * P], ident)
                    last.then_inc(S["x1_tr"], 1)
                else:
                    pe.wait_ge(S["x1t_lo_ok"], t + 3)
                    pe.wait_ge(S["xl_lo_ok"], t + 1)
                    product(p_x[t % 2], (x1t_hi, x1t_lo), (w1_hi, w1_lo), t, KD, HC).then_inc(S["xl_done"], 1)

            pe.wait_ge(S["w_lo"], W_FIRST[3])
            pe.wait_ge(S["xl_lo_ok"], T + 2)
            pe.wait_ge(S["as_ok"], 1)
            pe.transpose(p_rows, asd.rearrange("p a t -> p (a t)"), ident).then_inc(S["as_tr"], 1)
            pe.sem_inc(S["r1_read"], 2)
            with pe.Fori(0, T // 2) as i:
                for par in range(2):
                    t = i * 2 + par
                    pe.wait_ge(S["r1_read"], t + 1)
                    product(p_x[par], (x1t_hi, x1t_lo), (wr1_hi, wr1_lo), t, KD, HC).then_inc(S["r1_done"], 1)

            pe.wait_ge(S["uv_ok"], 1)
            pe.transpose(p_rows, uv.rearrange("p a t -> p (a t)"), ident).then_inc(S["uv_tr"], 1)
            pe.wait_ge(S["uv_rows"], 1)
            pe.wait_ge(S["r1_read"], T + 2)

            pe.wait_ge(S["xl_ones"], 1)
            pe.sem_inc(S["att_read"], C1)

            def xl2_tile(t):
                pe.wait_ge(S["h1t_lo_ok"], t + 2)
                pe.wait_ge(S["xl2_lo_ok"], t + 1)
                product(p_x[t % 2], (h1t_hi, h1t_lo), (w2_hi, w2_lo), t, KH, D).then_inc(S["xl2_done"], 1)

            for c in range(2):
                with pe.Fori(0, H // 2) as hp:
                    for hpar in range(2):
                        h = hp * 2 + hpar
                        ch = c * H + h
                        for k in range(T):
                            pe.wait_ge(S["pl_ok"], ch * T + k + 1 + E_CREDIT)
                            for j in range(C1):
                                if k == 0:
                                    pe.wait_ge(S["att_read"], ch * C1 + j + 1)
                                for m, (p, xl, w) in enumerate(((p_hi, xl_hi, HID + 1), (p_hi, xl_lo, HID), (p_lo, xl_hi, HID + 1))):
                                    last = pe.matmul(p_att[:, j, 0:w], p[k % PSLOTS][:, j * P:(j + 1) * P],
                                                     xl[:, k, ds(h, 1), 0:w].rearrange("p a n -> p (a n)"),
                                                     start=(k == 0 and m == 0), stop=(k == T - 1 and m == 2))
                            last.then_inc(S["p_free"], 1)
                if c == 1:
                    pe.wait_ge(S["att_read"], (2 * H + 1) * C1)
                    pe.sem_inc(S["xl2_lo_ok"], 2)
                for j in range(C1):
                    t = c * C1 + j
                    pe.wait_ge(S["h1_ok"], t + 1)
                    pe.wait_ge(S["h1t_lo_ok"], t + 1)
                    for k in range(KH):
                        last = pe.transpose(p_h[:, k * P:(k + 1) * P], att[:, j, k * P:(k + 1) * P], ident)
                    last.then_inc(S["h1_tr"], 1)
                    if c == 1:
                        pe.wait_ge(S["w_lo"], W_FIRST[4])
                        xl2_tile(j)
            for t in range(C1, T):
                xl2_tile(t)

            pe.wait_ge(S["w_lo"], W_FIRST[4] + KH)
            pe.wait_ge(S["xl2_lo_ok"], T + 2)
            pe.wait_ge(S["as2_ok"], 1)
            pe.transpose(p_rows[0:2 * T], asd2, ident).then_inc(S["as2_tr"], 1)
            pe.sem_inc(S["r2_sb"], 2)
            for first, end in ((0, SHIFT_AT), (SHIFT_AT, T)):
                if first:
                    pe.wait_ge(S["uv2_ok"], 1)
                    pe.transpose(p_rows[0:2 * T], uv2, ident).then_inc(S["uv2_tr"], 1)
                with pe.Fori(first // 2, end // 2) as i:
                    for par in range(2):
                        t = i * 2 + par
                        pe.wait_ge(S["r2_sb"], t + 1)
                        product(p_x[par], (h1t_hi, h1t_lo), (wr2_hi, wr2_lo), t, KH, D).then_inc(S["r2_done"], 1)
            pe.wait_ge(S["uv2_rows"], 1)
            pe.wait_ge(S["r2_sb"], T + 2)

            pe.wait_ge(S["xl2_ones"], 1)
            pe.sem_inc(S["att2_read"], 2)
            with pe.Fori(0, T // C2) as c:
                pe.wait_ge(S["att2_read"], c + 1)
                for k in range(T):
                    pe.wait_ge(S["pl2_ok"], c * T + k + 3)
                    for j in range(C2):
                        for m, (p, xl, w) in enumerate(((pp_hi, xl2_hi, D + 1), (pp_hi, xl2_lo, D), (pp_lo, xl2_hi, D + 1))):
                            for a, b in ((0, 512), (512, w)):
                                last = pe.matmul(psum[:, ds((c % 2) * 2048 + j * 1024 + a, b - a)],
                                                 p[k % P2SLOTS][:, j * P:(j + 1) * P], xl[:, k, a:b],
                                                 start=(k == 0 and m == 0), stop=(k == T - 1 and m == 2))
                    last.then_inc(S["p2_free"], 1)

        @block.scalar
        def _(act):
            awaited = act.alloc_register("awaited")

            def cast(out_, in_, signal, scale=1.0):
                act.activation(out_, in_, ACT.Copy, scale=scale).then_inc(signal, 1)

            def weights(i, ks=None):
                for k in ks if ks is not None else range(W_ROWS[i][1]):
                    q = W_FIRST[i] + k
                    act.wait_ge(S[f"w_in{q % 4}"], 16 * (q // 4 + 1))
                    cast(W_PARTS[i][0][:, k, :], W_STAGE[i][k % len(W_STAGE[i])], S["w_hi"], WSCALE)

            weights(0)
            act.wait_ge(S["w_lo"], KD)
            act.wait_ge(S["w_hi"], KD)
            act.wait_ge(S["ranges_i"], 1)
            act.sem_inc(S["blk_free"], 2)
            with act.Fori(0, NB // 2) as i:
                for par in range(2):
                    b = i * 2 + par
                    act.reg_mov(awaited, b + 1)
                    act.wait_ge(S["iotas"], 8)
                    act.wait_ge(S["blk_done"], awaited)
                    cast(CT[:, :, ds(b * WD, WD)], p_c[par].rearrange("p (k j) -> p k j", k=T), S["blk_free"])
            act.wait_ge(S["x_in"], 32)
            act.wait_ge(S["dinv_ok"], 2)
            for t in range(T):
                act.activation(xs_hi[:, t, :], x_sb[:, t, :], ACT.Copy, scale=dinv[:, t:t + 1]).then_inc(S["xs_hi_ok"], 1)
            with act.Fori(0, KD // 2) as i:
                for par in range(2):
                    c = i * 2 + par
                    act.reg_mov(awaited, c + 1)
                    act.wait_ge(S["iotas"], 8)
                    act.wait_ge(S["ag_done"], awaited)
                    cast(ag_hi[:, ds(c, 1), :].rearrange("p a n -> p (a n)"), p_ag[par], S["ag_hi_ok"])
            weights(1)
            act.wait_ge(S["gcn_done"], T)
            for what, t in X1_ORDER:
                if what == "tr":
                    act.wait_ge(S["x1_tr"], t + 1)
                    cast(x1t_hi[:, :, t * P:(t + 1) * P], p_tr[t % 2].rearrange("p (k n) -> p k n", k=KD), S["x1t_hi_ok"])
                else:
                    act.wait_ge(S["xl_done"], t + 1)
                    act.wait_ge(S["x1_tr"], min(2 * t + 2, T))
                    act.wait_ge(S["x1_out"], 16 * T)
                    cast(xl_hi[:, t, :, 0:HID], p_x[t % 2].rearrange("p (h n) -> p h n", h=H), S["xl_hi_ok"], 1 / WSCALE)
                    if 2 <= t < 2 + KD:
                        weights(2, [t - 2])

            for t in range(T):
                act.wait_ge(S["r1_done"], t + 1)
                act.wait_ge(S["xl_done"], T)
                if t >= 2:
                    act.wait_ge(S[f"r1_out{t % 2}"], 16 * (t // 2))
                cast(r_st[t % 2], p_x[t % 2], S["r1_read"], 1 / WSCALE)

            act.wait_ge(S["r1_done"], T)
            act.wait_ge(S["uv_ok"], 1)
            act.wait_ge(S["neg_out"], 16)
            act.sem_inc(S["uv_free"], 2)
            act.sem_inc(S["pf_ok"], E_CREDIT)
            act.sem_inc(S["p_free"], PSLOTS)

            def xl2_high(t):
                act.wait_ge(S["xl2_done"], t + 1)
                cast(xl2_hi[:, t, 0:D], p_x[t % 2][:, 0:D], S["xl2_hi_ok"], 1 / WSCALE)

            for c in range(2):
                with act.Fori(0, H // 2) as hp:
                    for hpar in range(2):
                        h = hp * 2 + hpar
                        ch = c * H + h

                        def high(k):
                            act.wait_ge(S["pf_ok"], ch * T + k + 1 + E_CREDIT)
                            act.wait_ge(S["p_free"], ch * T + k + 1)
                            cast(p_hi[k % PSLOTS], pf[k % ESLOTS], S["ph_even"])

                        act.wait_ge(S[f"uvr{hpar}"], (c * 2 + hp + 1) * 32)
                        for k in range(T):
                            act.reg_mov(awaited, ch * T + k + 1 + E_CREDIT - E_BACK[k])
                            act.wait_ge(S["iotas"], 8)
                            act.wait_ge(S["pf_ok"], awaited)
                            act.activation(e1[k % ESLOTS], uv_row[hpar][0], ACT.Exp,
                                           bias=asd[:, ds(h, 1), k:k + 1].rearrange("p a b -> p (a b)")).then_inc(S["ex_ok"], 1)
                            act.activation(e2[k % ESLOTS], uv_row[hpar][1], ACT.Exp,
                                           bias=as_s[:, ds(h, 1), k:k + 1].rearrange("p a b -> p (a b)")).then_inc(S["ex_ok"], 1)
                            if k >= 2 and k % 2 == 0:
                                high(k - 2)
                        high(T - 2)
                if c == 1:
                    weights(3)
                for j in range(C1):
                    t = c * C1 + j
                    act.wait_ge(S["h1_tr"], t + 1)
                    cast(h1t_hi[:, :, t * P:(t + 1) * P], p_h.rearrange("p (k n) -> p k n", k=KH), S["h1t_hi_ok"])
                    if c == 1:
                        xl2_high(j)
            for t in range(C1, T):
                xl2_high(t)
                for k in range(2 * (t - C1), min(2 * (t - C1) + 2, KH)):
                    weights(4, [k])

            act.wait_ge(S["uvr2"], 32)
            act.sem_inc(S["pf2_ok"], 2)
            act.sem_inc(S["p2_free"], P2SLOTS)
            with act.Fori(0, T // C2) as c:
                def high2(k):
                    act.wait_ge(S["pf2_ok"], c * T + k + 3)
                    act.wait_ge(S["p2_free"], c * T + k + 1)
                    cast(pp_hi[k % P2SLOTS], ppf[k % 2], S["ph2_ok"])

                for k in range(T):
                    act.reg_mov(awaited, c * T + k + 1)
                    act.wait_ge(S["iotas"], 8)
                    act.wait_ge(S["pf2_ok"], awaited)
                    act.activation(ee1[k % 2], u2_row[:, ds(c * W2C, W2C)], ACT.Exp, bias=asd[:, 0, k:k + 1]).then_inc(S["ex2_ok"], 1)
                    act.activation(ee2[k % 2], v2_row[:, ds(c * W2C, W2C)], ACT.Exp, bias=as_s[:, 0, k:k + 1]).then_inc(S["ex2_ok"], 1)
                    if k >= 1:
                        high2(k - 1)
                high2(T - 1)

        @block.vector
        def _(dve):
            steps_done, enter_loop, leave_loop = step_count()
            awaited = dve.alloc_register("awaited")

            def weights(i, ks=None):
                for k in ks if ks is not None else range(W_ROWS[i][1]):
                    q = W_FIRST[i] + k
                    dve.wait_ge(S[f"w_in{q % 4}"], 16 * (q // 4 + 1))
                    dve.wait_ge(S["w_hi"], q + 1)
                    dve.scalar_tensor_tensor(W_PARTS[i][1][:, k, :], W_STAGE[i][k % len(W_STAGE[i])], WSCALE, W_PARTS[i][0][:, k, :],
                                             ALU.mult, ALU.subtract).then_inc(S["w_lo"], 1)

            dve.wait_ge(S["edges"], 96)
            dve.tensor_copy(dst_f, dst_i).then_inc(S["dve"], 1)
            dve.wait_ge(S["dve"], steps_done(1))
            dve.tensor_scalar(hi_i, src_i, 7, None, ALU.arith_shift_right).then_inc(S["dve"], 1)
            dve.wait_ge(S["dve"], steps_done(1))
            dve.tensor_scalar(lo_i, src_i, P - 1, None, ALU.bitwise_and).then_inc(S["dve"], 1)
            dve.wait_ge(S["dve"], steps_done(1))
            dve.scalar_tensor_tensor(key_f, hi_i, float(KS), dst_f, ALU.mult, ALU.add).then_inc(S["keys_prep"], 1)
            dve.tensor_copy(lo_f, lo_i).then_inc(S["keys_prep"], 1)
            dve.tensor_reduce(tmm[:, 0, :], dst_f, axis=AX.X, op=ALU.min).then_inc(S["keys_prep"], 1)
            dve.tensor_reduce(tmm[:, 1, :], dst_f, axis=AX.X, op=ALU.max).then_inc(S["keys_prep"], 1)
            dve.wait_ge(S["keys_tr"], 1)
            dve.tensor_copy(key_b[:, 0, :], p_key[:, 0:NG * G]).then_inc(S["dve"], 1)
            dve.wait_ge(S["dve"], steps_done(1))
            dve.tensor_copy(lo_t, p_lo3[:, 0:NG * G]).then_inc(S["dve"], 1)
            dve.wait_ge(S["dve"], steps_done(1))
            dve.wait_ge(S["tile_rows"], 1)
            dve.wait_ge(S["iotas"], 8)
            dve.tensor_scalar(r_a, p_max, thr[:, 0:1], None, ALU.is_ge).then_inc(S["dve"], 1)
            dve.wait_ge(S["dve"], steps_done(1))
            dve.scalar_tensor_tensor(r_b, p_min, thr[:, 1:2], r_a, ALU.is_lt, ALU.mult).then_inc(S["dve"], 1)
            dve.wait_ge(S["dve"], steps_done(1))
            dve.scalar_tensor_tensor(r_c, r_b, -RANGE_BIG, t_io, ALU.mult, ALU.add).then_inc(S["dve"], 1)
            dve.wait_ge(S["dve"], steps_done(1))
            dve.scalar_tensor_tensor(r_d, t_io, 1.0, r_b, ALU.add, ALU.mult).then_inc(S["dve"], 1)
            dve.wait_ge(S["dve"], steps_done(1))
            dve.tensor_reduce(span[:, 0:1], r_c, axis=AX.X, op=ALU.min).then_inc(S["dve"], 1)
            dve.wait_ge(S["dve"], steps_done(1))
            dve.tensor_reduce(span[:, 1:2], r_d, axis=AX.X, op=ALU.max).then_inc(S["dve"], 1)
            dve.wait_ge(S["dve"], steps_done(1))
            dve.tensor_scalar(span[:, 0:1], span[:, 0:1], RANGE_BIG, None, ALU.add).then_inc(S["dve"], 1)
            dve.wait_ge(S["dve"], steps_done(1))
            dve.tensor_scalar(span[:, 1:2], span[:, 1:2], 1.0, None, ALU.max).then_inc(S["dve"], 1)
            dve.wait_ge(S["dve"], steps_done(1))
            dve.tensor_scalar(endm1, span[:, 1:2], -1.0, None, ALU.add).then_inc(S["dve"], 1)
            dve.wait_ge(S["dve"], steps_done(1))
            dve.tensor_tensor(span[:, 0:1], span[:, 0:1], endm1, ALU.min).then_inc(S["ranges_f"], 1)
            dve.wait_ge(S["ranges_t"], 1)
            dve.tensor_copy(range_t, p_rng).then_inc(S["dve"], 1)
            dve.wait_ge(S["dve"], steps_done(1))
            dve.tensor_scalar(range_t[:, NB:2 * NB], range_t[:, NB:2 * NB], float(G - 1), None, ALU.add).then_inc(S["dve"], 1)
            dve.wait_ge(S["dve"], steps_done(1))
            dve.tensor_scalar(range_i, range_t, G.bit_length() - 1, None, ALU.arith_shift_right).then_inc(S["ranges_i"], 1)

            for a in range(0, NG * G, LO_STEP):
                w = min(LO_STEP, NG * G - a)
                dve.tensor_tensor(lo_oh[:, :, a:a + w], lo_t[:, a:a + w].unsqueeze(1).to_broadcast([P, P, w]),
                                  jt[:, :, 0:w], ALU.is_equal).then_inc(S["lo_oh_ok"], 1)
            weights(0)

            dve.wait_ge(S["ranges_i"], 1)
            count = dve.alloc_register("dve_groups")
            dve.reg_mov(count, 0)
            dve.sem_inc(S["keys_ready"], 1)
            r0, r1 = dve.alloc_register("dve_first"), dve.alloc_register("dve_end")

            def key_block(b, par):
                dve.reg_load(r0, range_i[0:1, ds(b, 1)])
                dve.reg_load(r1, range_i[0:1, ds(b + NB, 1)])
                first, end = dve.snap(r0, min_val=0, max_val=NG - 1), dve.snap(r1, min_val=1, max_val=NG)
                dve.wait_ge(S["keys_ready"], dve.snap(count) + 1)
                dve.tensor_scalar(key_b[:, 1 - par, :], key_b[:, par, :], float(-WD), None, ALU.add).then_inc(S["key_shift"], 1)
                with dve.Fori(first, end) as g:
                    n = dve.snap(count)
                    dve.wait_ge(S["keys_free"], n + 1)
                    dve.tensor_tensor(ring[:, ds(n % KRING, 1), :, :].rearrange("p a c g -> p (a c) g"), key_io,
                                      key_b[:, par, ds(g * G, G)].unsqueeze(1).to_broadcast([P, T * WD, G]),
                                      ALU.is_equal).then_inc(S["keys_ready"], 1)
                    dve.reg_add(count, count, 1)
                dve.wait_ge(S["key_shift"], b + 1)

            with dve.Fori(0, NB // 2) as i:
                key_block(i * 2, 0)
                key_block(i * 2 + 1, 1)

            dve.wait_ge(S["blk_free"], NB + 2)
            for k in range(T):
                dg = CT[:, k, k * P:(k + 1) * P]
                dve.tensor_tensor(dg, dg, ident, ALU.add).then_inc(S["diag_ok"], 1)
            dve.wait_ge(S["diag_ok"], T)
            dve.wait_ge(S["blk_done"], NB)
            dve.tensor_copy(c_hi, CT).then_inc(S["chi_ok"], 1)
            dve.wait_ge(S["chi_ok"], 1)
            dve.tensor_tensor(c_lo, CT, c_hi, ALU.subtract).then_inc(S["clo_ok"], 1)
            dve.wait_ge(S["deg_done"], 1)
            dve.tensor_copy(deg, p_deg).then_inc(S["dinv_ok"], 1)
            dve.tensor_scalar(zz[:, 0, :], p_deg, float(F16_EXACT), None, ALU.is_gt).then_inc(S["dve"], 1)
            dve.wait_ge(S["dve"], steps_done(1))
            dve.tensor_reduce(over, zz[:, 0, :], axis=AX.X, op=ALU.max).then_inc(S["dve"], 1)
            dve.wait_ge(S["dve"], steps_done(1))
            dve.wait_ge(S["dinv_ok"], 2)
            dve.tensor_scalar(dinv_s, dinv, 1 / WSCALE, None, ALU.mult).then_inc(S["dinv_ok"], 1)
            dve.wait_ge(S["flag_done"], 1)
            dve.tensor_copy(flag_i[0:1], p_flag).then_inc(S["flag_ok"], 1)
            for t in range(T):
                dve.wait_ge(S["xs_hi_ok"], t + 1)
                dve.scalar_tensor_tensor(xs_lo[:, t, :], x_sb[:, t, :], dinv[:, t:t + 1], xs_hi[:, t, :],
                                         ALU.mult, ALU.subtract).then_inc(S["xs_lo_ok"], 1)
            with dve.Fori(0, KD // 2) as i:
                for par in range(2):
                    c = i * 2 + par
                    dve.wait_ge(S["ag_hi_ok"], c + 3)
                    hi = ag_hi[:, ds(c, 1), :].rearrange("p a n -> p (a n)")
                    lo = ag_lo[:, ds(c, 1), :].rearrange("p a n -> p (a n)")
                    dve.tensor_tensor(lo, p_ag[par], hi, ALU.subtract).then_inc(S["ag_lo_ok"], 1)
            dve.wait_ge(S["ag_done"], KD)
            for t in range(T):
                dve.wait_ge(S["neg_tr"], t + 1)
                dve.tensor_scalar(neg[:, t, :], p_neg, 0.0, NEG_BIG, ALU.is_equal, ALU.mult).then_inc(S["neg_ok"], 1)

            def moments(y, width, signal):
                for m in range(2):
                    ins = dve.bn_stats(stats[:, m, :], y[:, m * width // 2:(m + 1) * width // 2])
                ins.then_inc(S["dve"], 1)
                dve.reg_mov(awaited, steps_done(1))
                dve.wait_ge(S["iotas"], 8)
                dve.wait_ge(S["dve"], awaited)
                dve.bn_aggr(mv, stats.rearrange("p a b -> p (a b)")).then_inc(S["dve"], 1)
                dve.wait_ge(S["dve"], steps_done(1))
                dve.tensor_scalar(veps, mv[:, 1:2], LN_EPS, None, ALU.add).then_inc(signal, 1)

            weights(1)
            dve.wait_ge(S["ag_lo_ok"], KD + 2)
            dve.wait_ge(S["par_b0"], 16)
            with dve.Fori(0, T // 2) as i:
                kept = enter_loop(i, 2 * 3)
                for par in range(2):
                    t = i * 2 + par
                    xt = x_sb[:, ds(t, 1), :].rearrange("p a n -> p (a n)")
                    y = y0[:, par, :]
                    dve.wait_ge(S["gcn_done"], t + 1)
                    dve.scalar_tensor_tensor(y, p_out[par], dinv_s[:, ds(t, 1)], xt, ALU.mult, ALU.add).then_inc(S["gcn_read"], 1)
                    dve.wait_ge(S["gcn_read"], t + 3)
                    dve.tensor_tensor(y, y, par_rows[:, 2, 0:D], ALU.add).then_inc(S["dve"], 1)
                    dve.wait_ge(S["dve"], steps_done(1))
                    moments(y, D, S["gcn_var"])
                    dve.wait_ge(S["gcn_rstd"], t + 2)
                    dve.tensor_scalar(xt, y, mv[:, 0:1], rstd, ALU.subtract, ALU.mult).then_inc(S["x1_ok"], 1)
                    dve.wait_ge(S["x1_ok"], t + 1)
                leave_loop(kept, T // 2, 2 * 3)
            def max_as(row, col, t, out_, mask):
                dve.wait_ge(S["dve"], steps_done() - 1)
                dve.tensor_tensor_reduce(out=out_, in0=mask[:, t, :], in1=row, scale=1.0, scalar=NEG_BIG,
                                         op0=ALU.add, op1=ALU.max, accum_out=mx[:, col, t:t + 1]).then_inc(S["dve"], 1)
                steps_done(1)

            def project(t, heads, width, psum_, junk_, rows=(0, 1)):
                if t:
                    dve.wait_ge(S["dve"], steps_done())
                for j in range(2 * heads):
                    a = slice(j % heads * width, (j % heads + 1) * width)
                    ins = dve.tensor_tensor_reduce(out=junk_[:, j, :], in0=psum_[:, a], in1=par_rows[:, rows[j // heads], a], scale=1.0,
                                                   scalar=0.0, op0=ALU.mult, op1=ALU.add, accum_out=asd_w[:, j, t:t + 1])
                ins.then_inc(S["dve"], 1)
                steps_done(1)

            dve.wait_ge(S["par_a1s"], 16)
            dve.wait_ge(S["par_a1d"], 16)
            for what, t in X1_ORDER:
                if what == "tr":
                    dve.wait_ge(S["x1t_hi_ok"], t + 1)
                    dve.tensor_tensor(x1t_lo[:, :, t * P:(t + 1) * P], p_tr[t % 2].rearrange("p (k n) -> p k n", k=KD),
                                      x1t_hi[:, :, t * P:(t + 1) * P], ALU.subtract).then_inc(S["x1t_lo_ok"], 1)
                else:
                    dve.wait_ge(S["xl_hi_ok"], t + 1)
                    project(t, H, HID, p_x[t % 2], a_junk)
                    dve.scalar_tensor_tensor(xl_lo[:, t, :, 0:HID], p_x[t % 2].rearrange("p (h n) -> p h n", h=H), 1 / WSCALE,
                                             xl_hi[:, t, :, 0:HID], ALU.mult, ALU.subtract).then_inc(S["xl_lo_ok"], 1)
                    if 2 <= t < 2 + KD:
                        weights(2, [t - 2])
            dve.wait_ge(S["dve"], steps_done())
            dve.tensor_scalar(asd, asd_w, 1 / WSCALE, None, ALU.mult).then_inc(S["as_ok"], 1)
            dve.wait_ge(S["as_ok"], 1)
            dve.tensor_scalar(as_s, asd[:, 0:H, :], SLOPE, None, ALU.mult).then_inc(S["dve"], 1)
            dve.wait_ge(S["dve"], steps_done(1))
            dve.wait_ge(S["as_tr"], 1)
            dve.tensor_copy(rows_sb, p_rows).then_inc(S["as_rows"], 1)

            dve.wait_ge(S["xl_done"], T)
            for t in range(T):
                second = t // (T // 2)
                for h in range(2):
                    if t % (T // 2) == 0:
                        dve.wait_ge(S[f"asr{h}"], 16 * (1 + second))
                    for i in range(2):
                        max_as(as_row[h], 2 * second + h, t % (T // 2) * 2 + i, junk[i], neg)
                if t == T // 2 - 1:
                    dve.wait_ge(S["dve"], steps_done())
                    dve.sem_inc(S["max_ok"], 1)
            dve.wait_ge(S["dve"], steps_done())

            def shifts(heads, signal):
                ad, z, m = asd[:, heads:2 * heads, :], zz[:, 0:heads, :], mm[:, 0:heads, :]
                dve.tensor_tensor(z, mx[:, 0:heads, :], ad, ALU.add).then_inc(S["dve"], 1)
                dve.wait_ge(S["dve"], steps_done(1))
                dve.scalar_tensor_tensor(m, z, SLOPE, z, ALU.mult, ALU.max).then_inc(S["dve"], 1)
                dve.wait_ge(S["dve"], steps_done(1))
                dve.tensor_tensor(uv[:, 0:heads, :], ad, m, ALU.subtract).then_inc(S["dve"], 1)
                dve.wait_ge(S["dve"], steps_done(1))
                dve.scalar_tensor_tensor(uv[:, heads:2 * heads, :], ad, SLOPE, m, ALU.mult, ALU.subtract).then_inc(signal, 1)

            shifts(H, S["uv_ok"])
            dve.wait_ge(S["uv_tr"], 1)
            dve.wait_ge(S["as_dram"], 16)
            dve.tensor_copy(rows_sb, p_rows).then_inc(S["uv_rows"], 1)

            dve.wait_ge(S["r1_out0"], 16 * (T // 2))
            dve.wait_ge(S["r1_out1"], 16 * (T // 2))
            for p in ("par_b1", "par_g1", "par_be1"):
                dve.wait_ge(S[p], 16)
            dve.sem_inc(S["h1t_lo_ok"], 1)

            def xl2_low(t):
                dve.wait_ge(S["xl2_hi_ok"], t + 1)
                project(t, 1, D, p_x[t % 2], a2_junk, rows=(3, 0))
                dve.scalar_tensor_tensor(xl2_lo[:, t, 0:D], p_x[t % 2][:, 0:D], 1 / WSCALE, xl2_hi[:, t, 0:D],
                                         ALU.mult, ALU.subtract).then_inc(S["xl2_lo_ok"], 1)

            for c in range(2):
                def evict(h):
                    ch = c * H + h
                    dve.wait_ge(S["p_free"], ch * T + T + PSLOTS)
                    dve.tensor_scalar(ssum, p_att[:, :, HID:HID + 1].rearrange("p j n -> p (j n)"), SOFTMAX_EPS, None, ALU.add).then_inc(S["dve"], 1)
                    dve.wait_ge(S["dve"], steps_done(1))
                    dve.reciprocal(rsum, ssum).then_inc(S["dve"], 1)
                    dve.wait_ge(S["dve"], steps_done(1))
                    cols = slice(h * HID, (h + 1) * HID)
                    for j in range(C1):
                        dve.scalar_tensor_tensor(att[:, j, cols], p_att[:, j, 0:HID], rsum[:, j:j + 1],
                                                 par_rows[:, 0, cols], ALU.mult, ALU.add).then_inc(S["att_read"], 1)

                for h in range(H):
                    ch = c * H + h

                    def high(k):
                        dve.wait_ge(S["pf_ok"], ch * T + k + 1 + E_CREDIT)
                        dve.wait_ge(S["p_free"], ch * T + k + 1)
                        dve.tensor_copy(p_hi[k % PSLOTS], pf[k % ESLOTS]).then_inc(S["ph_odd"], 1)

                    for k in range(T):
                        n, s = ch * T + k, k % ESLOTS
                        if h and k == EVICT_AT:
                            evict(h - 1)
                        dve.wait_ge(S["ex_ok"], n * 2 + 2)
                        dve.tensor_tensor(e1[s], e1[s], e2[s], ALU.max).then_inc(S["g_ok"], 1)
                        if k >= 2 and k % 2 == 0:
                            high(k - 1)
                        dve.wait_ge(S["g_ok"], n + 1)
                        dve.wait_ge(S["pl_ok"], n + 1 + E_CREDIT - E_BACK[k])
                        dve.scalar_tensor_tensor(pf[s], e1[s], 1.0, CT[:, k, ds(c * W1C, W1C)],
                                                 ALU.min, ALU.mult).then_inc(S["pf_ok"], 1)
                    high(T - 1)
                    dve.sem_inc(S["uv_free"], 1)
                evict(H - 1)
                dve.wait_ge(S["att_read"], (c + 1) * H * C1 + C1)
                if c == 1:
                    weights(3)
                    dve.wait_ge(S["par_a2s"], 16)
                    dve.wait_ge(S["par_a2d"], 16)

                def h1_low(j):
                    t = c * C1 + j
                    dve.wait_ge(S["h1t_hi_ok"], t + 1)
                    dve.tensor_tensor(h1t_lo[:, :, ds(t * P, P)], p_h.rearrange("p (k n) -> p k n", k=KH),
                                      h1t_hi[:, :, ds(t * P, P)], ALU.subtract).then_inc(S["h1t_lo_ok"], 1)

                for j in range(C1):
                    t = c * C1 + j
                    y = att[:, j, :]
                    moments(y, HC, S["ln_var"])
                    dve.scalar_tensor_tensor(y, y, mv[:, 0:1], par_rows[:, 1, :], ALU.subtract, ALU.mult).then_inc(S["dve"], 1)
                    dve.wait_ge(S["ln_rstd"], t + 2)
                    dve.wait_ge(S["dve"], steps_done(1))
                    dve.scalar_tensor_tensor(y, y, rstd, par_rows[:, 2, :], ALU.mult, ALU.add).then_inc(S["dve"], 1)
                    dve.wait_ge(S["dve"], steps_done(1))
                    if j >= 1:
                        h1_low(j - 1)
                    slots = (C1 + 1) // 2 if j % 2 == 0 else C1 // 2
                    dve.wait_ge(S[f"r_in{j % 2}"], (c * slots + j // 2 + 1) * 16)
                    dve.scalar_tensor_tensor(y, y, 0.0, r_ld[j % 2], ALU.max, ALU.add).then_inc(S["h1_ok"], 1)
                    if c == 1 and j >= 1:
                        xl2_low(j - 1)
                h1_low(C1 - 1)

            xl2_low(C1 - 1)
            for t in range(C1, T):
                xl2_low(t)
                weights(4, range(2 * (t - C1), min(2 * (t - C1) + 2, KH)))
            dve.wait_ge(S["dve"], steps_done())
            dve.tensor_scalar(asd[:, 0:2, :], asd_w[:, 0:2, :], 1 / WSCALE, None, ALU.mult).then_inc(S["as2_ok"], 1)
            dve.wait_ge(S["as2_ok"], 1)
            dve.tensor_scalar(as_s[:, 0, :], asd[:, 0, :], SLOPE, None, ALU.mult).then_inc(S["dve"], 1)
            dve.wait_ge(S["dve"], steps_done(1))
            dve.wait_ge(S["as2_tr"], 1)
            dve.tensor_copy(rows_sb[0:2 * T], p_rows[0:2 * T]).then_inc(S["as2_rows"], 1)
            dve.wait_ge(S["par_br2"], 16)
            dve.wait_ge(S["par_be2"], 16)
            dve.tensor_tensor(par_rows[:, 3, 0:D], par_rows[:, 3, 0:D], par_rows[:, 2, 0:D], ALU.add).then_inc(S["dve"], 1)
            dve.wait_ge(S["dve"], steps_done(1))
            for t in range(T):
                dve.wait_ge(S[f"xb_in{t % 2}"], 16 * (t // 2 + 1))
                dve.tensor_tensor(xb_ld[t % 2], xb_ld[t % 2], par_rows[:, 3, 0:D], ALU.add).then_inc(S["dve"], 1)
                dve.wait_ge(S["dve"], steps_done(1))
                dve.wait_ge(S["r2_done"], t + 1)
                if t >= 2:
                    dve.wait_ge(S[f"r2_out{t % 2}"], 16 * (t // 2))
                dve.scalar_tensor_tensor(r2_st[t % 2], p_x[t % 2][:, 0:D], 1 / WSCALE, xb_ld[t % 2],
                                         ALU.mult, ALU.add).then_inc(S["r2_sb"], 1)
                if t == 0:
                    dve.wait_ge(S["asr2"], 16)
                    dve.wait_ge(S["neg_in"], 16)
                for i in range(3 * t, min(3 * t + 3, T)):
                    max_as(as2_row, 0, i, junk2[i % 2], neg2)
                if t == SHIFT_AT - 1:
                    dve.wait_ge(S["dve"], steps_done())
                    shifts(1, S["uv2_ok"])
                if t == SHIFT_AT:
                    dve.wait_ge(S["uv2_tr"], 1)
                    dve.wait_ge(S["as2_dram"], 16)
                    dve.tensor_copy(rows_sb[0:2 * T], p_rows[0:2 * T]).then_inc(S["uv2_rows"], 1)
            dve.wait_ge(S["par_b2"], 16)
            dve.wait_ge(S["par_g2"], 16)

            def make_p(c):
                for k in range(T):
                    n = c * T + k
                    dve.wait_ge(S["ex2_ok"], n * 2 + 2)
                    dve.tensor_tensor(ee1[k % 2], ee1[k % 2], ee2[k % 2], ALU.max).then_inc(S["g2_ok"], 1)
                    dve.wait_ge(S["g2_ok"], n + 1)
                    dve.wait_ge(S["pl2_ok"], n + 1)
                    dve.scalar_tensor_tensor(ppf[k % 2], ee1[k % 2], 1.0, CT[:, k, ds(c * W2C, W2C)],
                                             ALU.min, ALU.mult).then_inc(S["pf2_ok"], 1)

            def finish(c):
                dve.wait_ge(S["p2_free"], c * T + T + P2SLOTS)
                acc = psum[:, ds((c % 2) * 2048, 2048)].rearrange("p (j n) -> p j n", j=C2)
                dve.tensor_scalar(ssum[:, 0:C2], acc[:, :, D:D + 1].rearrange("p j n -> p (j n)"), SOFTMAX_EPS, None, ALU.add).then_inc(S["dve"], 1)
                dve.wait_ge(S["dve"], steps_done(1))
                dve.reciprocal(rsum[:, 0:C2], ssum[:, 0:C2]).then_inc(S["dve"], 1)
                dve.wait_ge(S["dve"], steps_done(1))
                for j in range(C2):
                    y, z = y2[j], y3[j]
                    ins = dve.scalar_tensor_tensor(y, acc[:, j, 0:D], rsum[:, j:j + 1], par_rows[:, 0, 0:D], ALU.mult, ALU.add)
                ins.then_inc(S["att2_read"], 1)
                dve.wait_ge(S["att2_read"], c + 3)
                for j in range(C2):
                    t = c * C2 + j
                    y, z = y2[j], y3[j]
                    moments(y, D, S["ln2_var"])
                    dve.scalar_tensor_tensor(y, y, mv[:, 0:1], par_rows[:, 1, 0:D], ALU.subtract, ALU.mult).then_inc(S["dve"], 1)
                    dve.wait_ge(S["ln2_rstd"], t * 2 + 2)
                    dve.wait_ge(S["dve"], steps_done(1))
                    dve.wait_ge(S[f"r2_in{j}"], (c + 1) * 16)
                    dve.scalar_tensor_tensor(y, y, rstd, r2_ld[j], ALU.mult, ALU.add).then_inc(S["r2_used"], 1)
                    dve.wait_ge(S["r2_used"], t + 1)
                    moments(y, D, S["ln2_var"])
                    dve.wait_ge(S["ln2_rstd"], t * 2 + 3)
                    dve.wait_ge(S["out_dma"], (t + 1) * 16)
                    dve.tensor_scalar(z, y, mv[:, 0:1], rstd, ALU.subtract, ALU.mult).then_inc(S["out_ok"], 1)

            make_p(0)
            with dve.Fori(0, T // C2 - 1) as c:
                kept = enter_loop(c, 2 + C2 * 5)
                make_p(c + 1)
                finish(c)
                leave_loop(kept, T // C2 - 1, 2 + C2 * 5)
            finish(T // C2 - 1)



_INS = ["x", "src", "dst", "L0_gnn_W", "L0_gnn_b", "L1_gnn_W1", "L1_gnn_a_src1", "L1_gnn_a_dst1", "L1_gnn_b1",
        "L1_gnn_g1", "L1_gnn_be1", "L1_gnn_Wr1", "L1_gnn_br1", "L1_gnn_W2", "L1_gnn_a_src2", "L1_gnn_a_dst2",
        "L1_gnn_b2", "L1_gnn_g2", "L1_gnn_be2", "L1_gnn_Wr2", "L1_gnn_br2"]


def kernel(**inputs):
    import numpy as _np
    import concourse.bacc as _bacc
    from concourse import mybir as _mybir
    from concourse.bass_utils import run_bass_kernel_spmd as _run

    nc = _bacc.Bacc("TRN2", target_bir_lowering=False, num_devices=1)
    arrays, args = {}, []
    for name in _INS:
        a = _np.ascontiguousarray(inputs[name])
        arrays[f"in_{name}_dram"] = a
        args.append(nc.dram_tensor(f"in_{name}_dram", a.shape, _mybir.dt.from_np(a.dtype), kind="ExternalInput").ap())
    out = nc.dram_tensor("out_dram", (N, D), _mybir.dt.float32, kind="ExternalOutput").ap()
    gnn_program(nc, *args, out)
    r = _run(nc, [arrays], core_ids=[0])
    return r.results[0]["out_dram"]
```

```python
from contextlib import ExitStack

import concourse.bass as bass
from concourse import mybir

P = 128
N = 1250
T = -(-N // P)
NP = T * P
LAST = N - (T - 1) * P
E = 41250
ET = -(-E // P)
D = 768
KD = D // P
H, HID = 4, 256
HC = H * HID
KH = HC // P
HS = HID + 2
XS = D + 2
WSCALE = 64.0
LN_EPS = 1e-5
SOFTMAX_EPS = 1e-16
SLOPE = 0.2
NEG_BIG = -3e38

WD = 32
NB = NP // WD
G = 12
ETP = -(-ET // G) * G
G_SHIFT = 18
G_INVERSE = -(-2 ** G_SHIFT // G)
EG = -(-ET // P)
KS = 2 * NP
PAD_DST = 2000
KRING = 2
KSLOTS = 4
LO_STEP = 16
RANGE_BIG = 1024.0
F16_EXACT = 2048

C1 = 5
W1C = C1 * P
PSLOTS = 5
ESLOTS = 3
E_BACK = [ESLOTS if k >= ESLOTS else T - max(j for j in range(T) if j % ESLOTS == k) + k for k in range(T)]
E_CREDIT = max(E_BACK)
EVICT_AT = 3
SHIFT_AT = 4
P2SLOTS = 10
C2 = 2
W2C = C2 * P

KB = 1024


def gnn_program(nc, x, src, dst, W0, b0, W1, a_src1, a_dst1, b1, g1, be1, Wr1, br1,
                W2, a_src2, a_dst2, b2, g2, be2, Wr2, br2, out):
    dt = mybir.dt
    f32, f16, bf16, i32, i16, u16 = dt.float32, dt.float16, dt.bfloat16, dt.int32, dt.int16, dt.uint16
    ALU, AX, ACT = mybir.AluOpType, mybir.AxisListType, mybir.ActivationFunctionType
    ds = bass.ds
    bytes_of = {f32: 4, i32: 4, f16: 2, bf16: 2, i16: 2, u16: 2}

    with ExitStack() as ctx:
        def sem(name):
            return ctx.enter_context(nc.semaphore(name))

        ARENA = 207 * KB
        arena = ctx.enter_context(nc.sbuf_tensor("arena", [P, ARENA // 4], f32))
        psum = ctx.enter_context(nc.psum_tensor("psum", [P, 8 * 512], f32))

        def at(byte, shape, dtype, parts=P):
            n = 1
            for s in shape:
                n *= s
            size = n * bytes_of[dtype]
            assert byte % 4 == 0 and byte + size <= ARENA, (byte, shape)
            v = arena[0:parts, byte // 4:byte // 4 + -(-size // 4)]
            if dtype != f32:
                v = v.bitcast(dtype)
            v = v[:, 0:n]
            if len(shape) == 2:
                v = v.rearrange("p (a b) -> p a b", a=shape[0])
            elif len(shape) == 3:
                v = v.rearrange("p (a b c) -> p a b c", a=shape[0], b=shape[1])
            return v

        pos = 0

        def small(shape, dtype, parts=P):
            nonlocal pos
            v = at(pos, shape, dtype, parts)
            n = 1
            for s in shape:
                n *= s
            pos += -(-n * bytes_of[dtype] // 4) * 4
            return v

        ident = small([P], f32)
        ident_h = small([P], f16)
        ones_h = small([2], f16)
        half = small([T], f32)
        flag_i = small([1], i32)
        over = small([1], f32)
        ones_f = small([1], f32)
        deg = small([T], f32)
        deg_hi = small([T], f32)
        dinv = small([T], f32)
        stats = small([2, 6], f32)
        mv = small([2], f32)
        veps = small([1], f32)
        rstd = small([1], f32)
        stats2 = small([C2, 2 * 6], f32)
        mv2 = small([C2, 2], f32)
        veps2 = small([C2], f32)
        rstd2 = small([C2], f32)
        asd_w = small([8, T], f32)
        asd = small([8, T], f32)
        as_s = small([4, T], f32)
        mx = small([4, T], f32)
        zz = small([4, T], f32)
        mm = small([4, T], f32)
        uv = small([8, T], f32)
        ssum = small([C1], f32)
        rsum = small([C1], f32)
        range_i = small([2 * NB], i32, 1)
        thr = small([2], f32, NB)
        span = small([2], f32, NB)
        endm1 = small([1], f32, NB)
        tmm = small([2, EG], f32)
        rows_sb = small([P], f32, 80)
        assert pos <= 4 * KB, pos
        par_rows = at(4 * KB, [4, HC], f32)
        CT = at(20 * KB, [T, NP], u16)
        assert T * NP * 2 == 25 * KB

        lo_oh = at(45 * KB, [P, ETP], f16)
        xt_hi = at(126 * KB, [KD, NP], f16)
        xt_lo = at(141 * KB, [KD, NP], f16)
        w0_hi = at(156 * KB, [KD, D], f16)
        w0_lo = at(165 * KB, [KD, D], f16)
        src_i = at(174 * KB, [EG, P], i32)
        dst_i = at(174 * KB + 1536, [EG, P], i32)
        hi_i = at(177 * KB, [EG, P], i32)
        lo_i = at(177 * KB + 1536, [EG, P], i32)
        dst_f = at(180 * KB, [EG, P], f32)
        key_f = at(180 * KB + 1536, [EG, P], f32)
        lo_f = at(120 * KB, [EG, P], f32)
        key_b = at(180 * KB, [KSLOTS, ETP], i16)
        lo_t = at(206 * KB + 256, [ETP], f16)
        jt = at(190 * KB + 512, [P, LO_STEP], f16)
        key_io = at(183 * KB, [T * WD, G], i16)
        ring = at(190 * KB + 512, [KRING, T * WD, G], f16)
        zero_h = at(205 * KB + 512, [T * WD], f16)
        t_io = at(20 * KB, [EG * P], f32, NB)
        r_a = at(22 * KB, [EG * P], f32, NB)
        r_b = at(24 * KB, [EG * P], f32, NB)
        r_c = at(26 * KB, [EG * P], f32, NB)
        r_d = at(28 * KB, [EG * P], f32, NB)
        range_t = at(30 * KB, [2 * NB], i32, 1)
        groups = at(30 * KB + 320, [NB], i32, 1)
        g_tiles = at(30 * KB + 480, [NB], i32, 1)
        g_latest = at(30 * KB + 640, [NB], i32, 1)
        wst0 = [at(40 * KB, [D], f32), at(4 * KB, [D], f32)]
        x_st = [at(31 * KB, [D], f32), at(34 * KB, [D], f32), at(37 * KB, [D], f32), at(8 * KB, [D], f32)]
        x_last = at(20 * KB, [D], f32)
        h_st = [at(174 * KB, [D], f32), at(177 * KB, [D], f32)]

        c_hi = at(45 * KB, [T, NP], f16)
        c_lo = at(70 * KB, [T, NP], f16)
        hs_hi = at(95 * KB, [T, D], f16)
        hs_lo = at(110 * KB, [T, D], f16)
        x_sb = at(126 * KB, [T, D], f32)
        h_sb = at(156 * KB, [T, D], f32)
        y0 = at(186 * KB, [2, D], f32)
        x1_sb = x_sb

        neg = at(70 * KB, [T, NP], bf16)
        x1t_hi = at(111 * KB, [KD, NP], f16)
        x1t_lo = at(189 * KB, [KD, NP], f16)
        w1_hi = at(45 * KB, [KD, HC], f16)
        w1_lo = at(57 * KB, [KD, HC], f16)
        xl = at(126 * KB, [T, 2, H * HS], f16)
        xl_hi = xl[:, :, 0, :].rearrange("p t (h n) -> p t h n", h=H)
        xl_lo = xl[:, :, 1, :].rearrange("p t (h n) -> p t h n", h=H)
        wst1 = [at(b * KB, [HC], f32) for b in (95, 99, 103, 107)]
        wr1_hi = at(176 * KB, [KD, HC], f16)
        wr1_lo = at(95 * KB, [KD, HC], f16)
        wstr1 = [at(168 * KB, [HC], f32), at(172 * KB, [HC], f32)]
        as_row = [at(45 * KB, [NP], f32), at(50 * KB, [NP], f32)]
        junk = [at(55 * KB + 2560 * i, [NP], bf16) for i in range(2)]
        r_st = [at(60 * KB, [HC], f32), at(64 * KB, [HC], f32)]
        e1 = [at(b, [W1C], f32) for b in (45 * KB, 47 * KB + 512, 178 * KB)]
        e2 = [at(b, [W1C], f32) for b in (50 * KB, 52 * KB + 512, 180 * KB + 512)]
        pf = [at(b, [W1C], f32) for b in (55 * KB, 57 * KB + 512, 183 * KB)]
        h1t_hi = at(60 * KB + 256, [KH, NP], f16)
        p_hi = [at(80 * KB + 512 + 2560 * i, [W1C], f16) for i in range(PSLOTS)]
        p_lo = [at(80 * KB + 512 + 2560 * i + 1280, [W1C], f16) for i in range(PSLOTS)]
        att = at(94 * KB, [C1, HC], f32)
        r_ld = [at(114 * KB, [HC], f32), at(118 * KB, [HC], f32)]
        uv_row = [[at(168 * KB, [W1C], f32), at(168 * KB + 2560, [W1C], f32)],
                  [at(173 * KB, [W1C], f32), at(173 * KB + 2560, [W1C], f32)]]
        h1t_f = at(122 * KB, [HC], f32)
        h1t_lo = at(186 * KB, [KH, NP], f16)

        w2_hi = at(126 * KB, [KH, D], f16)
        w2_lo = at(138 * KB, [KH, D], f16)
        wst2 = [at(b * KB, [D], f32) for b in (16, 178, 150, 153)]
        wr2_hi = at(81 * KB, [KH, D], f16)
        wr2_lo = at(94 * KB, [KH, D], f16)
        wstr2 = [at(112 * KB, [D], f32), at(115 * KB, [D], f32)]
        neg2 = at(126 * KB, [T, NP], bf16)
        xl2_hi = at(45 * KB, [T, XS], f16)
        xl2_lo = at(156 * KB, [T, XS], f16)
        as2_row = at(172 * KB, [NP], f32)
        a_junk = at(107 * KB, [8, HID], bf16)
        a2_junk = at(181 * KB, [2, D], bf16)
        junk2 = [at(177 * KB + 2560 * i, [NP], bf16) for i in range(2)]
        r2_st = [at(182 * KB + 512, [D], f32), at(119 * KB, [D], f32)]
        xb_ld = [at(106 * KB, [D], f32), at(109 * KB, [D], f32)]
        u2_row = at(126 * KB, [NP], f32)
        v2_row = at(131 * KB, [NP], f32)
        ee1 = [at(136 * KB + KB * i, [W2C], f32) for i in range(ESLOTS)]
        ee2 = [at(139 * KB + KB * i, [W2C], f32) for i in range(ESLOTS)]
        ppf = [at(152 * KB + KB * i, [W2C], f32) for i in range(ESLOTS)]
        pp_hi = [at(142 * KB + KB * i, [W2C], f16) for i in range(P2SLOTS)]
        pp_lo = [at(142 * KB + KB * i + 512, [W2C], f16) for i in range(P2SLOTS)]
        y2 = [at(94 * KB + 3 * KB * i, [D], f32) for i in range(2)]
        y3 = [at(101 * KB + 3 * KB * i, [D], f32) for i in range(2)]
        r2_ld = [at(108 * KB, [D], f32), at(112 * KB, [D], f32)]

        asd2 = asd[:, 0:2, :].rearrange("p a t -> p (a t)")
        uv2 = uv[:, 0:2, :].rearrange("p a t -> p (a t)")

        def bank(i, n=512, parts=P):
            return psum[0:parts, 512 * i:512 * i + n]

        p_key, p_lo3, p_min, p_max, p_rng = bank(0, EG * P), bank(1, EG * P), bank(2, EG * P, NB), bank(3, EG * P, NB), bank(4, 2 * NB, 1)
        p_c = [bank(5, T * WD), bank(6, T * WD)]
        p_deg, p_flag = bank(7, 2 * T), psum[0:1, 512 * 7 + 32:512 * 7 + 33]
        p_neg = [psum[:, 512 * i:512 * i + NP // 2].bitcast(f16) for i in (6, 4)]
        p_out = [psum[:, 1024 * i:1024 * i + D] for i in range(2)]
        p_tr = [psum[:, 3072:3072 + D], psum[:, 0:D]]
        p_rows = bank(1, P, 80)
        p_x = [psum[:, 1024 + 1024 * i:2048 + 1024 * i] for i in range(2)]
        p_att = psum[:, 0:512 * C1].rearrange("p (j n) -> p j n", j=C1)
        p_h = psum[:, 512 * 6:512 * 8]
        p_att2 = [psum[:, 2048 * i:2048 * i + 2048].rearrange("p (j n) -> p j n", j=C2) for i in range(2)]

        h_d = nc.dram_tensor("h_scratch", [T, P, D], f32).ap()
        x1_d = nc.dram_tensor("x1_scratch", [T, P, D], f32).ap()
        r1_d = nc.dram_tensor("r1_scratch", [T, P, HC], f32).ap()
        r2_d = nc.dram_tensor("r2_scratch", [T, P, D], f32).ap()
        neg_d = nc.dram_tensor("neg_scratch", [P, T * NP], bf16).ap()
        as_d = nc.dram_tensor("as_scratch", [8 * NP], f32).ap()
        uv_d = nc.dram_tensor("uv_scratch", [8 * NP], f32).ap()
        as2_d = nc.dram_tensor("as2_scratch", [2 * NP], f32).ap()
        uv2_d = nc.dram_tensor("uv2_scratch", [2 * NP], f32).ap()

        def everywhere(row):
            return row.rearrange("(a n) -> a n", a=1).to_broadcast([P, row.shape[0]])

        S = {n: sem(n) for n in """
            pads edges iotas ident_ok keys_prep keys_tr tile_rows ranges_f ranges_t ranges_i lo_oh_ok key_shift
            keys_ready keys_free blk_done blk_free x_in0 x_in1 x_in2 x_in3 x_in9 x_tr xt_ok xt_hi_ok xt_lo_ok w_scaled h_done h_read h_out0 h_out1 h_in0 h_in1 xr_in0 xr_in1 hs_hi_ok hs_lo_ok w_in0 w_in1 w_in2 w_in3 w_hi w_lo
            diag_ok chi_ok clo_ok deg_done dinv_ok over_ok flag_done flag_ok
            neg_tr neg_ok gcn_done gcn_read gcn_var gcn_rstd x1_ok x1_out
            x1_tr x1t_hi_ok x1t_lo_ok as_ok as_tr as_rows as_dram asr0 asr1 max_ok
            xl_done xl_hi_ok xl_lo_ok xl_ones r1_done r1_read r1_sb r1_out0 r1_out1 neg_out
            uv_free uv_ok uv_tr uv_rows uv_dram uvr0 uvr1 ex_ok g_ok pf_ok ph_even ph_odd pl_ok p_free att_read 
            ln_var ln_rstd h1_ok h1_tr h1t_f_ok h1t_hi_ok h1t_lo_ok r_in0 r_in1 
            as2_ok as2_tr as2_rows as2_dram asr2 neg_in 
            xl2_done xl2_hi_ok xl2_lo_ok xl2_ones r2_done r2_sb r2_out0 r2_out1 xb_in0 xb_in1
            uv2_ok uv2_tr uv2_rows uv2_dram uvr2 ex2_ok g2_ok pf2_ok ph2_ok pl2_ok p2_free att2_read last_done
            ln2_var ln2_rstd r2_in0 r2_in1 r2_used out_ok out_dma
            par_b0 par_a1s par_a1d par_br1 par_b1 par_g1 par_be1 par_a2s par_a2d par_br2 par_b2 par_g2 par_be2
            half_ok dve
            """.split()}
        block = ctx.enter_context(nc.Block())


        def step_count():
            here, before = 0, 0

            def steps_done(new=0):
                nonlocal here
                here += new
                return here + before

            def enter_loop(i, steps):
                nonlocal before
                outside = (here, before)
                before = before + i * steps
                return outside

            def leave_loop(outside, rounds, steps):
                nonlocal here, before
                assert here - outside[0] == steps, (here - outside[0], steps)
                here, before = outside[0] + rounds * steps, outside[1]

            return steps_done, enter_loop, leave_loop

        X1_ORDER = [s for i in range(T) for s in [("tr", t) for t in (2 * i, 2 * i + 1) if t < T] + [("xl", i)]]

        X0_ORDER = [s for t in range(T) for s in [("x", t)] + ([("w", t - 2)] if 2 <= t < 2 + KD else [])]

        def x_stage(t):
            return x_st[t % 4] if t < T - 1 else x_last

        W_ROWS = [(W0, KD), (W1, KD), (Wr1, KD), (W2, KH), (Wr2, KH)]
        W_FIRST = [sum(k for _, k in W_ROWS[:i]) for i in range(5)]
        W_STAGE = [wst0, wst1, wstr1, wst2, wstr2]
        W_PARTS = [(w0_hi, w0_lo), (w1_hi, w1_lo), (wr1_hi, wr1_lo), (w2_hi, w2_lo), (wr2_hi, wr2_lo)]

        @block.sync
        def _(sp):
            full = ET - 1
            sp.wait_ge(S["pads"], 2)
            for a, b in ((src, src_i), (dst, dst_i)):
                sp.dma_start(b[:, 0:2, :], a[0:2 * P * P].rearrange("(g p e) -> p g e", g=2, p=P)).then_inc(S["edges"], 16)
                sp.dma_start(b[0:full - 2 * P, 2, :], a[2 * P * P:full * P].rearrange("(p e) -> p e", e=P)).then_inc(S["edges"], 16)
                sp.dma_start(b[full - 2 * P:full - 2 * P + 1, 2, 0:E - full * P],
                             a[full * P:E].rearrange("(p e) -> p e", p=1)).then_inc(S["edges"], 16)

            def weights(i, ks=None):
                for k in ks if ks is not None else range(W_ROWS[i][1]):
                    q = W_FIRST[i] + k
                    slots = len(W_STAGE[i])
                    before = q - (slots if k >= slots else 4)
                    if before >= 0:
                        sp.wait_ge(S["w_hi"], before + 1)
                        sp.wait_ge(S["w_lo"], before + 1)
                    sp.dma_start(W_STAGE[i][k % slots], W_ROWS[i][0][k * P:(k + 1) * P, :]).then_inc(S[f"w_in{q % 4}"], 16)

            for what, t in X0_ORDER:
                if what == "w":
                    weights(0, [t])
                elif t < T - 1:
                    if t >= 4:
                        sp.wait_ge(S["xt_lo_ok"], t - 3)
                    sp.dma_start(x_stage(t), x[t * P:(t + 1) * P, :]).then_inc(S[f"x_in{t % 4}"], 16)
                else:
                    sp.wait_ge(S["pads"], 3)
                    sp.dma_start(x_last[0:LAST], x[(T - 1) * P:N, :]).then_inc(S["x_in9"], 16)
            sp.sem_inc(S["h_out0"], 16)
            sp.sem_inc(S["h_out1"], 16)
            for t in range(T):
                sp.wait_ge(S["h_read"], t + 3)
                sp.dma_start(h_d[t], h_st[t % 2]).then_inc(S[f"h_out{t % 2}"], 16)
            sp.wait_ge(S["blk_done"], NB)
            sp.wait_ge(S["h_out0"], 16 * (T // 2 + 1))
            sp.wait_ge(S["h_out1"], 16 * (T // 2 + 1))
            sp.dma_start(h_sb[:, 0:T // 2, :], h_d[0:T // 2].rearrange("t p d -> p t d")).then_inc(S["h_in0"], 16)
            sp.dma_start(h_sb[:, T // 2:T, :], h_d[T // 2:T].rearrange("t p d -> p t d")).then_inc(S["h_in1"], 16)
            sp.dma_start(x_sb[:, 0:T // 2, :], x[0:T // 2 * P, :].rearrange("(t p) d -> p t d", p=P)).then_inc(S["xr_in0"], 16)
            sp.wait_ge(S["pads"], 4)
            sp.dma_start(x_sb[:, T // 2:T - 1, :], x[T // 2 * P:(T - 1) * P, :].rearrange("(t p) d -> p t d", p=P)).then_inc(S["xr_in1"], 16)
            sp.dma_start(x_sb[0:LAST, T - 1, :], x[(T - 1) * P:N, :]).then_inc(S["xr_in1"], 16)
            sp.wait_ge(S["gcn_done"], T)
            weights(1)
            sp.wait_ge(S["neg_ok"], T)
            sp.dma_start(neg_d, neg.rearrange("p t n -> p (t n)")).then_inc(S["neg_out"], 16)
            for t in range(T):
                sp.wait_ge(S["x1_ok"], t + 1)
                sp.dma_start(x1_d[t], x1_sb[:, t, :]).then_inc(S["x1_out"], 16)
            weights(2)
            def rows(c, h):
                sp.wait_ge(S["uv_free"], c * H + h + 1)
                for part in range(2):
                    sp.dma_start(uv_row[h % 2][part],
                                 everywhere(uv_d[(part * H + h) * NP + c * W1C:(part * H + h) * NP + (c + 1) * W1C])).then_inc(S[f"uvr{h % 2}"], 16)

            for t in range(T):
                if t == T - 1:
                    sp.wait_ge(S["uv_rows"], 1)
                    sp.dma_start(uv_d.rearrange("(r p) -> r p", p=P), rows_sb).then_inc(S["uv_dram"], 16)
                    sp.wait_ge(S["uv_dram"], 16)
                    rows(0, 0)
                sp.wait_ge(S["r1_sb"], t + 1)
                sp.dma_start(r1_d[t], r_st[t % 2]).then_inc(S[f"r1_out{t % 2}"], 16)
                if t == T - 1:
                    sp.wait_ge(S["r1_done"], T)
                    rows(0, 1)
            sp.wait_ge(S["r1_out0"], 16 * (T // 2))
            sp.wait_ge(S["r1_out1"], 16 * (T // 2))
            sp.wait_ge(S["uv_ok"], 1)

            def residual(t):
                slot, before = t % C1 % 2, [u for u in range(t) if u % C1 % 2 == t % C1 % 2]
                if before:
                    sp.wait_ge(S["h1_ok"], before[-1] + 1)
                sp.dma_start(r_ld[slot], r1_d[t]).then_inc(S[f"r_in{slot}"], 16)

            rows(0, 2)
            rows(0, 3)
            rows(1, 0)
            rows(1, 1)
            for t in range(C1):
                residual(t)
            rows(1, 2)
            rows(1, 3)
            residual(C1)
            residual(C1 + 1)
            weights(3, [0])
            sp.wait_ge(S["p_free"], 2 * H * T + PSLOTS)
            weights(3, range(1, KH))
            for t in range(C1 + 2, T):
                residual(t)
            sp.wait_ge(S["h1_tr"], T)
            weights(4)
            sp.wait_ge(S["neg_out"], 16)
            sp.wait_ge(S["xl2_done"], T)
            sp.dma_start(neg2.rearrange("p t n -> p (t n)"), neg_d).then_inc(S["neg_in"], 16)
            sp.wait_ge(S["x1_out"], 16 * T)
            for t in range(T):
                if t >= 2:
                    sp.wait_ge(S["r2_sb"], t + 1)
                sp.dma_start(xb_ld[t % 2], x1_d[t]).then_inc(S[f"xb_in{t % 2}"], 16)
                if t >= 1:
                    sp.wait_ge(S["r2_sb"], t + 2)
                    sp.dma_start(r2_d[t - 1], r2_st[(t - 1) % 2]).then_inc(S[f"r2_out{(t - 1) % 2}"], 16)
            sp.wait_ge(S["r2_sb"], T + 2)
            sp.dma_start(r2_d[T - 1], r2_st[(T - 1) % 2]).then_inc(S[f"r2_out{(T - 1) % 2}"], 16)
            sp.wait_ge(S["r2_out0"], 16 * (T // 2))
            sp.wait_ge(S["r2_out1"], 16 * (T // 2))
            sp.sem_inc(S["out_dma"], 16)
            sp.wait_ge(S["uv2_ok"], 1)
            for t in range(T):
                if t >= 2:
                    sp.wait_ge(S["r2_used"], t - 1)
                sp.dma_start(r2_ld[t % 2], r2_d[t]).then_inc(S[f"r2_in{t % 2}"], 16)
                if t >= 1:
                    sp.wait_ge(S["out_ok"], t)
                    sp.dma_start(out[(t - 1) * P:t * P, :], y3[(t - 1) % 2]).then_inc(S["out_dma"], 16)
            sp.wait_ge(S["out_ok"], T)
            sp.dma_start(out[(T - 1) * P:N, :], y3[(T - 1) % 2][0:LAST]).then_inc(S["out_dma"], 16)
            sp.wait_ge(S["out_dma"], 16 * (T + 1))

        @block.gpsimd
        def _(pool):
            pool.memset(src_i[:, 2, :], 0).then_inc(S["pads"], 1)
            pool.memset(dst_i[:, 2, :], PAD_DST).then_inc(S["pads"], 1)
            pool.memset(ident, 0.0).then_inc(S["ident_ok"], 1)
            pool.memset(ident_h, 0.0).then_inc(S["ident_ok"], 1)
            pool.wait_ge(S["ident_ok"], 2)
            for m in (ident, ident_h):
                pool.affine_select(out=m, in_=m, compare_op=ALU.not_equal, fill=1.0, base=0,
                                   pattern=[[-1, P]], channel_multiplier=1).then_inc(S["ident_ok"], 1)
            loose = dict(channel_multiplier=0, allow_small_or_imprecise_dtypes=True)
            pool.iota(jt, [[1, P], [0, LO_STEP]], base=0, **loose).then_inc(S["iotas"], 1)
            pool.iota(key_io.rearrange("p (k j) g -> p k j g", k=T), [[KS, T], [1, WD], [0, G]], base=0,
                      channel_multiplier=0).then_inc(S["iotas"], 1)
            pool.iota(t_io, [[1, EG * P]], base=0, **loose).then_inc(S["iotas"], 1)

            for c in range(2):
                pool.iota(thr[:, c:c + 1], [[0, 1]], base=c * WD, channel_multiplier=WD,
                          allow_small_or_imprecise_dtypes=True).then_inc(S["iotas"], 1)
            pool.memset(zero_h, 0.0).then_inc(S["iotas"], 1)
            pool.memset(ones_h, 1.0).then_inc(S["iotas"], 1)
            pool.memset(ones_f, 1.0).then_inc(S["iotas"], 1)
            pool.memset(half, -0.5).then_inc(S["half_ok"], 1)

            def param(name, row, slot, n=HC):
                pool.dma_start(par_rows[:, slot, 0:n], everywhere(row)).then_inc(S[name], 16)

            flat = "h c -> (h c)"
            param("par_b0", b0, 2, D)
            param("par_br1", br1, 3)
            pool.wait_ge(S["ranges_i"], 1)
            pool.memset(x_last, 0.0).then_inc(S["pads"], 1)
            for what, t in X0_ORDER:
                if what == "x":
                    pool.wait_ge(S["xt_hi_ok"], t + 1)
                    cols = slice(t * P, (t + 1) * P)
                    pool.tensor_tensor(xt_lo[:, :, cols], x_stage(t).rearrange("p (k n) -> p k n", k=KD), xt_hi[:, :, cols],
                                       ALU.subtract).then_inc(S["xt_lo_ok"], 1)
                else:
                    pool.wait_ge(S["w_hi"], t + 1)
                    pool.tensor_tensor(w0_lo[:, t, :], wst0[t % 2], w0_hi[:, t, :], ALU.subtract).then_inc(S["w_lo"], 1)
            pool.wait_ge(S["w_lo"], KD)
            pool.wait_ge(S["xt_lo_ok"], T)
            param("par_a1s", a_src1.rearrange(flat), 0)
            param("par_a1d", a_dst1.rearrange(flat), 1)
            pool.wait_ge(S["h_done"], T)
            pool.memset(x_sb[:, T - 1, :], 0.0).then_inc(S["pads"], 1)

            pool.wait_ge(S["half_ok"], 1)
            pool.wait_ge(S["dinv_ok"], 1)
            pool.tensor_tensor(dinv, deg, half, ALU.pow).then_inc(S["dinv_ok"], 1)
            pool.sem_inc(S["gcn_rstd"], 1)
            with pool.Fori(0, T) as t:
                pool.wait_ge(S["gcn_var"], t + 1)
                pool.wait_ge(S["gcn_rstd"], t + 1)
                pool.tensor_tensor(rstd, veps, half[:, 0:1], ALU.pow).then_inc(S["gcn_rstd"], 1)
            pool.wait_ge(S["x1_tr"], T)
            pool.wait_ge(S["x1_out"], 16 * T)
            pool.memset(xl_hi[:, :, :, HID:HID + 2], 1.0).then_inc(S["xl_ones"], 1)

            pool.wait_ge(S["as_rows"], 1)
            pool.dma_start(as_d.rearrange("(r p) -> r p", p=P), rows_sb).then_inc(S["as_dram"], 16)
            pool.wait_ge(S["as_dram"], 16)
            for h in range(2):
                pool.dma_start(as_row[h % 2], everywhere(as_d[h * NP:(h + 1) * NP])).then_inc(S[f"asr{h % 2}"], 16)
            pool.wait_ge(S["par_br1"], 16)
            for t in range(T):
                pool.wait_ge(S["r1_read"], t + 3)
                pool.tensor_tensor(r_st[t % 2], r_st[t % 2], par_rows[:, 3, :], ALU.add).then_inc(S["r1_sb"], 1)
                if t == 3:
                    for h in (2, 3):
                        pool.wait_ge(S["max_ok"], 1)
                        pool.dma_start(as_row[h % 2], everywhere(as_d[h * NP:(h + 1) * NP])).then_inc(S[f"asr{h % 2}"], 16)
            param("par_b1", b1, 0)
            param("par_g1", g1, 1)
            param("par_be1", be1, 2)

            pool.sem_inc(S["ln_rstd"], 1)
            pool.sem_inc(S["pl_ok"], E_CREDIT)

            def h1_low(t):
                pool.wait_ge(S["h1t_hi_ok"], t + 1)
                cols = slice(t * P, (t + 1) * P)
                pool.tensor_tensor(h1t_lo[:, :, cols], h1t_f.rearrange("p (k n) -> p k n", k=KH), h1t_hi[:, :, cols],
                                   ALU.subtract).then_inc(S["h1t_lo_ok"], 1)

            for c in range(2):
                with pool.Fori(0, H) as h:
                    for k in range(T):
                        pool.wait_ge(S["ph_odd" if k % 2 else "ph_even"], (c * H + h) * (T // 2) + k // 2 + 1)
                        pool.tensor_tensor(p_lo[k % PSLOTS], pf[k % ESLOTS], p_hi[k % PSLOTS], ALU.subtract).then_inc(S["pl_ok"], 1)
                if c == 1:
                    pool.wait_ge(S["p_free"], 2 * H * T + PSLOTS)
                    pool.memset(xl2_hi[:, :, D:D + 2], 1.0).then_inc(S["xl2_ones"], 1)
                    pool.wait_ge(S["att_read"], (2 * H + 1) * C1)
                for j in range(C1):
                    t = c * C1 + j
                    pool.wait_ge(S["ln_var"], t + 1)
                    pool.wait_ge(S["ln_rstd"], t + 1)
                    pool.tensor_tensor(rstd, veps, half[:, 0:1], ALU.pow).then_inc(S["ln_rstd"], 1)
                    if c == 1 and j < 2:
                        for k in range(j * KH // 2, (j + 1) * KH // 2):
                            pool.wait_ge(S["w_hi"], W_FIRST[3] + k + 1)
                            pool.tensor_tensor(w2_lo[:, k, :], wst2[k % len(wst2)], w2_hi[:, k, :], ALU.subtract).then_inc(S["w_lo"], 1)
                        if j == 1:
                            pool.wait_ge(S["w_lo"], W_FIRST[4])
                            param("par_a2s", a_src2.rearrange(flat), 3, D)
                            param("par_a2d", a_dst2.rearrange(flat), 0, D)
                    if j:
                        h1_low(t - 1)
                h1_low((c + 1) * C1 - 1)


            pool.wait_ge(S["h1_ok"], T)
            param("par_g2", g2, 1, D)
            param("par_be2", be2, 2, D)
            pool.wait_ge(S["as2_ok"], 1)
            param("par_b2", b2, 0, D)
            param("par_br2", br2, 3, D)
            pool.wait_ge(S["as2_rows"], 1)
            pool.dma_start(as2_d.rearrange("(r p) -> r p", p=P), rows_sb[0:2 * T]).then_inc(S["as2_dram"], 16)
            pool.wait_ge(S["as2_dram"], 16)
            pool.dma_start(as2_row, everywhere(as2_d[0:NP])).then_inc(S["asr2"], 16)
            pool.wait_ge(S["uv2_rows"], 1)
            pool.dma_start(uv2_d.rearrange("(r p) -> r p", p=P), rows_sb[0:2 * T]).then_inc(S["uv2_dram"], 16)
            pool.wait_ge(S["uv2_dram"], 16)
            for part, row in enumerate((u2_row, v2_row)):
                pool.dma_start(row, everywhere(uv2_d[part * NP:(part + 1) * NP])).then_inc(S["uvr2"], 16)
            pool.sem_inc(S["ln2_rstd"], 1)
            pool.sem_inc(S["pl2_ok"], E_CREDIT)

            def low_parts(c):
                for k in range(T):
                    pool.wait_ge(S["ph2_ok"], c * T + k + 1)
                    pool.tensor_tensor(pp_lo[k % P2SLOTS], ppf[k % ESLOTS], pp_hi[k % P2SLOTS], ALU.subtract).then_inc(S["pl2_ok"], 1)

            def root(n, js):
                pool.wait_ge(S["ln2_var"], n + 1)
                pool.wait_ge(S["ln2_rstd"], n + 1)
                pool.tensor_tensor(rstd2[:, js], veps2[:, js], half[:, js], ALU.pow).then_inc(S["ln2_rstd"], 1)

            low_parts(0)
            with pool.Fori(0, T // C2 - 1) as c:
                low_parts(c + 1)
                root(c * 2, slice(0, C2))
                root(c * 2 + 1, slice(0, C2))
            for j in range(C2):
                for m in range(2):
                    root(2 * (T // C2 - 1) + 2 * j + m, slice(j, j + 1))

        @block.tensor
        def _(pe):
            pe.wait_ge(S["ident_ok"], 4)
            pe.wait_ge(S["keys_prep"], 4)
            for g in range(EG):
                pe.transpose(p_key[:, g * P:(g + 1) * P], key_f[:, g, :], ident)
                last = pe.transpose(p_lo3[:, g * P:(g + 1) * P], lo_f[:, g, :], ident)
            last.then_inc(S["keys_tr"], 1)
            for g in range(EG):
                for m, o in enumerate((p_min, p_max)):
                    last = pe.matmul(o[:, g * P:(g + 1) * P], tmm[:, m, g:g + 1].to_broadcast([P, NB]), ident,
                                     start=True, stop=True)
            last.then_inc(S["tile_rows"], 1)
            pe.wait_ge(S["ranges_f"], 1)
            for c in range(2):
                last = pe.matmul(p_rng[:, c * NB:(c + 1) * NB], span[:, c:c + 1], ident[0:NB, 0:NB], start=True, stop=True)
            last.then_inc(S["ranges_t"], 1)

            pe.wait_ge(S["ranges_i"], 1)
            pe.wait_ge(S["lo_oh_ok"], 1)
            for t in range(T):
                if t < T - 1:
                    pe.wait_ge(S[f"x_in{t % 4}"], 16 * (t // 4 + 1))
                else:
                    pe.wait_ge(S["x_in9"], 16)
                if t >= 2:
                    pe.wait_ge(S["xt_hi_ok"], t - 1)
                for k in range(KD):
                    last = pe.transpose(p_out[t % 2][:, k * P:(k + 1) * P], x_stage(t)[:, k * P:(k + 1) * P], ident)
                last.then_inc(S["x_tr"], 1)

            def product(o, lhs, rhs, t, kn, width, ks=None):
                for k in ks or range(kn):
                    for n, part in enumerate(lhs):
                        for m, w in enumerate(rhs[:2 - n]):
                            for a in range(0, width, 512):
                                b = min(a + 512, width)
                                ins = pe.matmul(o[:, a:b], part[:, k, ds(t * P, P)], w[:, k, a:b],
                                                start=(k == 0 and n == 0 and m == 0), stop=(k == kn - 1 and n == 1))
                return ins

            pe.wait_ge(S["ranges_i"], 1)
            pe.wait_ge(S["iotas"], 8)
            pe.wait_ge(S["lo_oh_ok"], -(-ETP // LO_STEP))
            pe.sem_inc(S["keys_free"], KRING)
            count = pe.alloc_register("pe_groups")
            pe.reg_mov(count, 2)
            r0, r1 = pe.alloc_register("pe_first"), pe.alloc_register("pe_end")

            def count_block(b, par):
                pe.reg_load(r0, range_i[0:1, ds(b, 1)])
                pe.reg_load(r1, range_i[0:1, ds(b + NB, 1)])
                first, end = pe.snap(r0, min_val=0, max_val=ETP - G), pe.snap(r1, min_val=G, max_val=ETP)
                pe.wait_ge(S["blk_free"], b + 1)
                pe.matmul(p_c[par], zero_h[:, 0:P], zero_h, start=True, stop=False)
                with pe.Fori(first, end, G) as tile:
                    g = nc.s_assert_within(tile, 0, ETP - G,
                                           skip_runtime_bounds_check_because="the loop ends at ETP at most, in steps of G from its start")
                    pe.wait_ge(S["keys_ready"], count)
                    n = pe.snap(count) - 1
                    for i in range(G):
                        last = pe.matmul(p_c[par], lo_oh[:, :, ds(g + i, 1)].rearrange("p a c -> p (a c)"),
                                         ring[:, ds(n % KRING, 1), :, i].rearrange("p a c -> p (a c)"),
                                         start=False, stop=False)
                    last.then_inc(S["keys_free"], 1)
                    pe.reg_add(count, count, 1)
                pe.matmul(p_c[par], zero_h[:, 0:P], zero_h, start=False, stop=True).then_inc(S["blk_done"], 1)

            pe.wait_ge(S["xt_lo_ok"], T)
            pe.sem_inc(S["h_read"], 2)
            with pe.Fori(0, T // 2) as i:
                for par in range(2):
                    t = i * 2 + par
                    for b in range(NB // T):
                        count_block(t * (NB // T) + b, b % 2)
                        if b == 0:
                            pe.wait_ge(S["w_lo"], KD)
                            pe.wait_ge(S["h_read"], t + 1)
                        last = product(p_out[par], (xt_hi, xt_lo), (w0_hi, w0_lo), t, KD, D,
                                       range(b * KD // (NB // T), (b + 1) * KD // (NB // T)))
                    last.then_inc(S["h_done"], 1)

            for n, c, made in ((0, c_hi, "chi_ok"), (1, c_lo, "clo_ok")):
                pe.wait_ge(S[made], 1)
                for t in range(T):
                    for k in range(T):
                        last = pe.matmul(p_deg[:, n * T + t:n * T + t + 1], c[:, k, t * P:(t + 1) * P], ones_h[:, 0:1],
                                         start=(k == 0), stop=(k == T - 1))
            last.then_inc(S["deg_done"], 1)
            pe.wait_ge(S["over_ok"], 1)
            pe.matmul(p_flag, over, ones_f, start=True, stop=True).then_inc(S["flag_done"], 1)
            pe.wait_ge(S["flag_ok"], 1)
            big = pe.alloc_register("big_counts")
            pe.reg_load(big, flag_i[0:1, 0:1])

            pe.sem_inc(S["gcn_read"], 2)
            with pe.Fori(0, T // 2) as i:
                for par in range(2):
                    t = i * 2 + par
                    pe.wait_ge(S["gcn_read"], t + 1)

                    def aggregate(counts, k):
                        for n, part in enumerate((hs_hi, hs_lo)):
                            for a, b in ((0, 512), (512, D)):
                                ins = pe.matmul(p_out[par][:, a:b], counts[:, k, ds(t * P, P)], part[:, k, a:b],
                                                start=(counts is c_hi and k == 0 and n == 0),
                                                stop=(counts is c_hi and k == T - 1 and n == 1))
                        return ins

                    for k in range(T - 1):
                        pe.wait_ge(S["hs_lo_ok"], k + 1)
                        aggregate(c_hi, k)
                    pe.wait_ge(S["hs_lo_ok"], T)
                    with pe.If_ne(big, 0):
                        for k in range(T):
                            aggregate(c_lo, k)
                    aggregate(c_hi, T - 1).then_inc(S["gcn_done"], 1)

            for t in range(T):
                if t >= 2:
                    pe.wait_ge(S["neg_ok"], t - 1)
                for k in range(T):
                    last = pe.transpose(p_neg[t % 2][:, k * P:(k + 1) * P], c_hi[:, k, t * P:(t + 1) * P], ident_h)
                last.then_inc(S["neg_tr"], 1)

            pe.wait_ge(S["neg_ok"], T)
            pe.wait_ge(S["gcn_read"], T + 2)
            pe.sem_inc(S["x1t_lo_ok"], 2)
            pe.sem_inc(S["xl_lo_ok"], 2)
            for what, t in X1_ORDER:
                if what == "tr":
                    pe.wait_ge(S["x1_ok"], t + 1)
                    pe.wait_ge(S["x1t_lo_ok"], t + 1)
                    for k in range(KD):
                        last = pe.transpose(p_tr[t % 2][:, k * P:(k + 1) * P], x1_sb[:, t, k * P:(k + 1) * P], ident)
                    last.then_inc(S["x1_tr"], 1)
                else:
                    pe.wait_ge(S["w_lo"], W_FIRST[2])
                    pe.wait_ge(S["x1t_lo_ok"], t + 3)
                    pe.wait_ge(S["xl_lo_ok"], t + 1)
                    product(p_x[t % 2], (x1t_hi, x1t_lo), (w1_hi, w1_lo), t, KD, HC).then_inc(S["xl_done"], 1)

            pe.wait_ge(S["w_lo"], W_FIRST[3])
            pe.wait_ge(S["xl_lo_ok"], T + 2)
            pe.wait_ge(S["as_ok"], 1)
            pe.transpose(p_rows, asd.rearrange("p a t -> p (a t)"), ident).then_inc(S["as_tr"], 1)
            pe.sem_inc(S["r1_read"], 2)

            def r1_tile(t, par):
                pe.wait_ge(S["r1_read"], t + 1)
                product(p_x[par], (x1t_hi, x1t_lo), (wr1_hi, wr1_lo), t, KD, HC).then_inc(S["r1_done"], 1)

            with pe.Fori(0, T // 2 - 1) as i:
                r1_tile(i * 2, 0)
                r1_tile(i * 2 + 1, 1)
            r1_tile(T - 2, 0)
            pe.wait_ge(S["uv_ok"], 1)
            pe.transpose(p_rows, uv.rearrange("p a t -> p (a t)"), ident).then_inc(S["uv_tr"], 1)
            r1_tile(T - 1, 1)
            pe.wait_ge(S["uv_rows"], 1)
            pe.wait_ge(S["r1_read"], T + 2)

            pe.wait_ge(S["xl_ones"], 1)
            pe.sem_inc(S["h1t_lo_ok"], 1)
            pe.sem_inc(S["att_read"], C1)

            def xl2_tile(t):
                pe.wait_ge(S["h1t_lo_ok"], t + 2)
                pe.wait_ge(S["xl2_lo_ok"], t + 1)
                product(p_x[t % 2], (h1t_hi, h1t_lo), (w2_hi, w2_lo), t, KH, D).then_inc(S["xl2_done"], 1)

            for c in range(2):
                with pe.Fori(0, H // 2) as hp:
                    for hpar in range(2):
                        h = hp * 2 + hpar
                        ch = c * H + h
                        for k in range(T):
                            pe.wait_ge(S["pl_ok"], ch * T + k + 1 + E_CREDIT)
                            for j in range(C1):
                                if k == 0:
                                    pe.wait_ge(S["att_read"], ch * C1 + j + 1)
                                for m, (p, xl, w) in enumerate(((p_hi, xl_hi, HID + 1), (p_hi, xl_lo, HID), (p_lo, xl_hi, HID + 1))):
                                    last = pe.matmul(p_att[:, j, 0:w], p[k % PSLOTS][:, j * P:(j + 1) * P],
                                                     xl[:, k, ds(h, 1), 0:w].rearrange("p a n -> p (a n)"),
                                                     start=(k == 0 and m == 0), stop=(k == T - 1 and m == 2))
                            last.then_inc(S["p_free"], 1)
                if c == 1:
                    pe.wait_ge(S["att_read"], (2 * H + 1) * C1)
                    pe.sem_inc(S["xl2_lo_ok"], 2)
                for j in range(C1):
                    t = c * C1 + j
                    pe.wait_ge(S["h1_ok"], t + 1)
                    if t:
                        pe.wait_ge(S["h1t_hi_ok"], t)
                    for k in range(KH):
                        last = pe.transpose(p_h[:, k * P:(k + 1) * P], att[:, j, k * P:(k + 1) * P], ident)
                    last.then_inc(S["h1_tr"], 1)
                    if c == 1:
                        pe.wait_ge(S["w_lo"], W_FIRST[4])
                        xl2_tile(j)
            for t in range(C1, T):
                xl2_tile(t)

            pe.wait_ge(S["w_lo"], W_FIRST[4] + KH)
            pe.wait_ge(S["xl2_lo_ok"], T + 2)
            pe.wait_ge(S["as2_ok"], 1)
            pe.transpose(p_rows[0:2 * T], asd2, ident).then_inc(S["as2_tr"], 1)
            pe.sem_inc(S["r2_sb"], 2)
            for first, end in ((0, SHIFT_AT), (SHIFT_AT, T)):
                if first:
                    pe.wait_ge(S["uv2_ok"], 1)
                    pe.transpose(p_rows[0:2 * T], uv2, ident).then_inc(S["uv2_tr"], 1)
                with pe.Fori(first // 2, end // 2) as i:
                    for par in range(2):
                        t = i * 2 + par
                        pe.wait_ge(S["r2_sb"], t + 1)
                        product(p_x[par], (h1t_hi, h1t_lo), (wr2_hi, wr2_lo), t, KH, D).then_inc(S["r2_done"], 1)
            pe.wait_ge(S["uv2_rows"], 1)
            pe.wait_ge(S["r2_sb"], T + 2)

            pe.wait_ge(S["xl2_ones"], 1)
            pe.sem_inc(S["att2_read"], 2)

            def attend(c, k, j):
                for m, (p, xl2, w) in enumerate(((pp_hi, xl2_hi, D + 1), (pp_hi, xl2_lo, D), (pp_lo, xl2_hi, D + 1))):
                    for a, b in ((0, 512), (512, w)):
                        ins = pe.matmul(psum[:, ds((c % 2) * 2048 + j * 1024 + a, b - a)],
                                        p[k % P2SLOTS][:, j * P:(j + 1) * P], xl2[:, k, a:b],
                                        start=(k == 0 and m == 0), stop=(k == T - 1 and m == 2))
                return ins

            with pe.Fori(0, T // C2 - 1) as c:
                pe.wait_ge(S["att2_read"], c + 1)
                for k in range(T):
                    pe.wait_ge(S["pl2_ok"], c * T + k + 1 + E_CREDIT)
                    for j in range(C2):
                        last = attend(c, k, j)
                    last.then_inc(S["p2_free"], 1)
            c = T // C2 - 1
            pe.wait_ge(S["att2_read"], c + 1)
            for j in range(C2):
                for k in range(T):
                    pe.wait_ge(S["pl2_ok"], c * T + k + 1 + E_CREDIT)
                    last = attend(c, k, j)
                last.then_inc(S["last_done"], 1)

        @block.scalar
        def _(act):
            awaited = act.alloc_register("awaited")

            def cast(out_, in_, signal, scale=1.0):
                act.activation(out_, in_, ACT.Copy, scale=scale).then_inc(signal, 1)

            def weights(i, ks=None):
                for k in ks if ks is not None else range(W_ROWS[i][1]):
                    q = W_FIRST[i] + k
                    act.wait_ge(S[f"w_in{q % 4}"], 16 * (q // 4 + 1))
                    cast(W_PARTS[i][0][:, k, :], W_STAGE[i][k % len(W_STAGE[i])], S["w_hi"], WSCALE)

            for what, t in X0_ORDER:
                if what == "x":
                    act.wait_ge(S["x_tr"], t + 1)
                    cast(x_stage(t), p_out[t % 2], S["xt_ok"])
                    cast(xt_hi[:, :, t * P:(t + 1) * P], p_out[t % 2].rearrange("p (k n) -> p k n", k=KD), S["xt_hi_ok"])
                else:
                    act.wait_ge(S[f"w_in{t % 4}"], 16 * (t // 4 + 1))
                    cast(wst0[t % 2], wst0[t % 2], S["w_scaled"], WSCALE)
                    act.wait_ge(S["w_scaled"], t + 1)
                    cast(w0_hi[:, t, :], wst0[t % 2], S["w_hi"])
            act.wait_ge(S["w_lo"], KD)
            act.wait_ge(S["xt_lo_ok"], T)
            act.wait_ge(S["ranges_i"], 1)
            act.sem_inc(S["blk_free"], 2)
            with act.Fori(0, T // 2) as i:
                for par in range(2):
                    t = i * 2 + par
                    for k in range(NB // T):
                        b = t * (NB // T) + k
                        act.reg_mov(awaited, b + 1)
                        act.wait_ge(S["iotas"], 8)
                        act.wait_ge(S["blk_done"], awaited)
                        cast(CT[:, :, ds(b * WD, WD)], p_c[k % 2].rearrange("p (k j) -> p k j", k=T), S["blk_free"])
                    act.wait_ge(S["h_done"], t + 1)
                    act.wait_ge(S[f"h_out{par}"], (i + 1) * 16)
                    cast(h_st[par], p_out[par], S["h_read"], 1 / WSCALE)
            act.wait_ge(S["dinv_ok"], 2)
            for t in range(T):
                if t % (T // 2) == 0:
                    act.wait_ge(S[f"h_in{t // (T // 2)}"], 16)
                act.activation(hs_hi[:, t, :], h_sb[:, t, :], ACT.Copy, scale=dinv[:, t:t + 1]).then_inc(S["hs_hi_ok"], 1)
            act.wait_ge(S["neg_tr"], T)
            weights(1)
            for what, t in X1_ORDER:
                if what == "tr":
                    act.wait_ge(S["x1_tr"], t + 1)
                    cast(x1t_hi[:, :, t * P:(t + 1) * P], p_tr[t % 2].rearrange("p (k n) -> p k n", k=KD), S["x1t_hi_ok"])
                else:
                    act.wait_ge(S["xl_done"], t + 1)
                    act.wait_ge(S["x1_tr"], min(2 * t + 2, T))
                    act.wait_ge(S["x1_out"], 16 * T)
                    cast(xl_hi[:, t, :, 0:HID], p_x[t % 2].rearrange("p (h n) -> p h n", h=H), S["xl_hi_ok"], 1 / WSCALE)
                    if 2 <= t < 2 + KD:
                        weights(2, [t - 2])

            act.sem_inc(S["uv_free"], 2)
            for t in range(T):
                act.wait_ge(S["r1_done"], t + 1)
                act.wait_ge(S["xl_done"], T)
                if t >= 2:
                    act.wait_ge(S[f"r1_out{t % 2}"], 16 * (t // 2))
                cast(r_st[t % 2], p_x[t % 2], S["r1_read"], 1 / WSCALE)

            act.wait_ge(S["r1_done"], T)
            act.wait_ge(S["uv_ok"], 1)
            act.wait_ge(S["neg_out"], 16)
            act.sem_inc(S["pf_ok"], E_CREDIT)
            act.sem_inc(S["p_free"], PSLOTS)

            def xl2_high(t):
                act.wait_ge(S["xl2_done"], t + 1)
                cast(xl2_hi[:, t, 0:D], p_x[t % 2][:, 0:D], S["xl2_hi_ok"], 1 / WSCALE)

            for c in range(2):
                with act.Fori(0, H // 2) as hp:
                    for hpar in range(2):
                        h = hp * 2 + hpar
                        ch = c * H + h

                        def high(k):
                            act.wait_ge(S["pf_ok"], ch * T + k + 1 + E_CREDIT)
                            act.wait_ge(S["p_free"], ch * T + k + 1)
                            cast(p_hi[k % PSLOTS], pf[k % ESLOTS], S["ph_even"])

                        act.wait_ge(S[f"uvr{hpar}"], (c * 2 + hp + 1) * 32)
                        for k in range(T):
                            act.reg_mov(awaited, ch * T + k + 1 + E_CREDIT - E_BACK[k])
                            act.wait_ge(S["iotas"], 8)
                            act.wait_ge(S["pf_ok"], awaited)
                            act.activation(e1[k % ESLOTS], uv_row[hpar][0], ACT.Exp,
                                           bias=asd[:, ds(h, 1), k:k + 1].rearrange("p a b -> p (a b)")).then_inc(S["ex_ok"], 1)
                            act.activation(e2[k % ESLOTS], uv_row[hpar][1], ACT.Exp,
                                           bias=as_s[:, ds(h, 1), k:k + 1].rearrange("p a b -> p (a b)")).then_inc(S["ex_ok"], 1)
                            if k >= 2 and k % 2 == 0:
                                high(k - 2)
                        high(T - 2)
                if c == 1:
                    for k in range(KH):
                        q = W_FIRST[3] + k
                        stage = wst2[k % len(wst2)]
                        act.wait_ge(S[f"w_in{q % 4}"], 16 * (q // 4 + 1))
                        cast(stage, stage, S["w_scaled"], WSCALE)
                        act.wait_ge(S["w_scaled"], KD + k + 1)
                        cast(w2_hi[:, k, :], stage, S["w_hi"])
                for j in range(C1):
                    t = c * C1 + j
                    act.wait_ge(S["h1_tr"], t + 1)
                    act.wait_ge(S["h1t_lo_ok"], t + 1)
                    cast(h1t_f, p_h, S["h1t_f_ok"])
                    cast(h1t_hi[:, :, t * P:(t + 1) * P], p_h.rearrange("p (k n) -> p k n", k=KH), S["h1t_hi_ok"])
                    if c == 1:
                        xl2_high(j)
            for t in range(C1, T):
                xl2_high(t)
                for k in range(2 * (t - C1), min(2 * (t - C1) + 2, KH)):
                    weights(4, [k])

            act.wait_ge(S["uvr2"], 32)
            act.sem_inc(S["pf2_ok"], E_CREDIT)
            with act.Fori(0, T // C2) as c:
                for k in range(T):
                    act.reg_mov(awaited, c * T + k + 1 + E_CREDIT - E_BACK[k])
                    act.wait_ge(S["iotas"], 8)
                    act.wait_ge(S["pf2_ok"], awaited)
                    for e, row, a in ((ee1, u2_row, asd), (ee2, v2_row, as_s)):
                        act.activation(e[k % ESLOTS], row[:, ds(c * W2C, W2C)], ACT.Exp, bias=a[:, 0, k:k + 1]).then_inc(S["ex2_ok"], 1)

        @block.vector
        def _(dve):
            steps_done, enter_loop, leave_loop = step_count()
            awaited = dve.alloc_register("awaited")

            def weights(i, ks=None):
                for k in ks if ks is not None else range(W_ROWS[i][1]):
                    q = W_FIRST[i] + k
                    dve.wait_ge(S[f"w_in{q % 4}"], 16 * (q // 4 + 1))
                    dve.wait_ge(S["w_hi"], q + 1)
                    dve.scalar_tensor_tensor(W_PARTS[i][1][:, k, :], W_STAGE[i][k % len(W_STAGE[i])], WSCALE, W_PARTS[i][0][:, k, :],
                                             ALU.mult, ALU.subtract).then_inc(S["w_lo"], 1)

            dve.wait_ge(S["edges"], 96)
            dve.tensor_copy(dst_f, dst_i).then_inc(S["dve"], 1)
            dve.wait_ge(S["dve"], steps_done(1))
            dve.tensor_scalar(hi_i, src_i, 7, None, ALU.arith_shift_right).then_inc(S["dve"], 1)
            dve.wait_ge(S["dve"], steps_done(1))
            dve.tensor_scalar(lo_i, src_i, P - 1, None, ALU.bitwise_and).then_inc(S["dve"], 1)
            dve.wait_ge(S["dve"], steps_done(1))
            dve.scalar_tensor_tensor(key_f, hi_i, float(KS), dst_f, ALU.mult, ALU.add).then_inc(S["keys_prep"], 1)
            dve.tensor_copy(lo_f, lo_i).then_inc(S["keys_prep"], 1)
            dve.tensor_reduce(tmm[:, 0, :], dst_f, axis=AX.X, op=ALU.min).then_inc(S["keys_prep"], 1)
            dve.tensor_reduce(tmm[:, 1, :], dst_f, axis=AX.X, op=ALU.max).then_inc(S["keys_prep"], 1)
            dve.wait_ge(S["keys_tr"], 1)
            dve.tensor_copy(key_b[:, 0, :], p_key[:, 0:ETP]).then_inc(S["dve"], 1)
            dve.wait_ge(S["dve"], steps_done(1))
            dve.tensor_copy(lo_t, p_lo3[:, 0:ETP]).then_inc(S["dve"], 1)
            dve.wait_ge(S["dve"], steps_done(1))
            dve.wait_ge(S["tile_rows"], 1)
            dve.wait_ge(S["iotas"], 8)
            dve.tensor_scalar(r_a, p_max, thr[:, 0:1], None, ALU.is_ge).then_inc(S["dve"], 1)
            dve.wait_ge(S["dve"], steps_done(1))
            dve.scalar_tensor_tensor(r_b, p_min, thr[:, 1:2], r_a, ALU.is_lt, ALU.mult).then_inc(S["dve"], 1)
            dve.wait_ge(S["dve"], steps_done(1))
            dve.scalar_tensor_tensor(r_c, r_b, -RANGE_BIG, t_io, ALU.mult, ALU.add).then_inc(S["dve"], 1)
            dve.wait_ge(S["dve"], steps_done(1))
            dve.scalar_tensor_tensor(r_d, t_io, 1.0, r_b, ALU.add, ALU.mult).then_inc(S["dve"], 1)
            dve.wait_ge(S["dve"], steps_done(1))
            dve.tensor_reduce(span[:, 0:1], r_c, axis=AX.X, op=ALU.min).then_inc(S["dve"], 1)
            dve.wait_ge(S["dve"], steps_done(1))
            dve.tensor_reduce(span[:, 1:2], r_d, axis=AX.X, op=ALU.max).then_inc(S["dve"], 1)
            dve.wait_ge(S["dve"], steps_done(1))
            dve.tensor_scalar(span[:, 0:1], span[:, 0:1], RANGE_BIG, None, ALU.add).then_inc(S["dve"], 1)
            dve.wait_ge(S["dve"], steps_done(1))
            dve.tensor_scalar(span[:, 1:2], span[:, 1:2], 1.0, None, ALU.max).then_inc(S["dve"], 1)
            dve.wait_ge(S["dve"], steps_done(1))
            dve.tensor_scalar(endm1, span[:, 1:2], -1.0, None, ALU.add).then_inc(S["dve"], 1)
            dve.wait_ge(S["dve"], steps_done(1))
            dve.tensor_tensor(span[:, 0:1], span[:, 0:1], endm1, ALU.min).then_inc(S["ranges_f"], 1)
            dve.wait_ge(S["ranges_t"], 1)
            dve.tensor_copy(range_t, p_rng).then_inc(S["dve"], 1)
            dve.wait_ge(S["dve"], steps_done(1))
            first_t, end_t = range_t[:, 0:NB], range_t[:, NB:2 * NB]
            dve.tensor_scalar(first_t, first_t, 2 ** 15 - 2, None, ALU.bitwise_and).then_inc(S["dve"], 1)
            dve.wait_ge(S["dve"], steps_done(1))
            dve.tensor_tensor(groups, end_t, first_t, ALU.subtract).then_inc(S["dve"], 1)
            dve.wait_ge(S["dve"], steps_done(1))
            dve.tensor_scalar(groups, groups, float(G - 1), float(G_INVERSE), ALU.add, ALU.mult).then_inc(S["dve"], 1)
            dve.wait_ge(S["dve"], steps_done(1))
            dve.tensor_scalar(groups, groups, G_SHIFT, None, ALU.arith_shift_right).then_inc(S["dve"], 1)
            dve.wait_ge(S["dve"], steps_done(1))
            dve.tensor_scalar(g_tiles, groups, float(G), None, ALU.mult).then_inc(S["dve"], 1)
            dve.tensor_scalar(g_latest, groups, float(-G), float(ETP), ALU.mult, ALU.add).then_inc(S["dve"], 1)
            dve.wait_ge(S["dve"], steps_done(2))
            dve.tensor_tensor(range_i[:, 0:NB], first_t, g_latest, ALU.min).then_inc(S["dve"], 1)
            dve.wait_ge(S["dve"], steps_done(1))
            dve.tensor_tensor(range_i[:, NB:2 * NB], range_i[:, 0:NB], g_tiles, ALU.add).then_inc(S["ranges_i"], 1)

            for a in range(0, ETP, LO_STEP):
                w = min(LO_STEP, ETP - a)
                dve.tensor_tensor(lo_oh[:, :, a:a + w], lo_t[:, a:a + w].unsqueeze(1).to_broadcast([P, P, w]),
                                  jt[:, :, 0:w], ALU.is_equal).then_inc(S["lo_oh_ok"], 1)

            dve.wait_ge(S["lo_oh_ok"], -(-ETP // LO_STEP))
            dve.wait_ge(S["ranges_i"], 1)
            count = dve.alloc_register("dve_groups")
            before = dve.alloc_register("dve_groups_before")
            dve.reg_mov(count, 1)
            dve.reg_mov(before, 1)
            dve.sem_inc(S["keys_ready"], 1)
            r0, r1 = dve.alloc_register("dve_first"), dve.alloc_register("dve_end")

            def key_block(b, slot):
                dve.reg_load(r0, range_i[0:1, ds(b, 1)])
                dve.reg_load(r1, range_i[0:1, ds(b + NB, 1)])
                first, end = dve.snap(r0, min_val=0, max_val=ETP - G), dve.snap(r1, min_val=G, max_val=ETP)
                dve.wait_ge(S["keys_ready"], before)
                dve.tensor_scalar(key_b[:, (slot + 1) % KSLOTS, :], key_b[:, slot, :], float(-WD), None, ALU.add).then_inc(S["key_shift"], 1)
                dve.reg_mov(before, count)
                with dve.Fori(first, end, G) as tile:
                    g = nc.s_assert_within(tile, 0, ETP - G,
                                           skip_runtime_bounds_check_because="the loop ends at ETP at most, in steps of G from its start")
                    dve.wait_ge(S["keys_free"], count)
                    dve.tensor_tensor(ring[:, ds(dve.snap(count) & (KRING - 1), 1), :, :].rearrange("p a c g -> p (a c) g"), key_io,
                                      key_b[:, slot, ds(g, G)].unsqueeze(1).to_broadcast([P, T * WD, G]),
                                      ALU.is_equal).then_inc(S["keys_ready"], 1)
                    dve.reg_add(count, count, 1)
                dve.wait_ge(S["key_shift"], b + 1)

            with dve.Fori(0, NB // KSLOTS) as i:
                for slot in range(KSLOTS):
                    key_block(i * KSLOTS + slot, slot)

            dve.wait_ge(S["blk_free"], NB + 2)
            for k in range(T):
                dg = CT[:, k, k * P:(k + 1) * P]
                dve.tensor_tensor(dg, dg, ident, ALU.add).then_inc(S["diag_ok"], 1)
            dve.wait_ge(S["diag_ok"], T)
            dve.wait_ge(S["blk_done"], NB)
            dve.tensor_copy(c_hi, CT).then_inc(S["chi_ok"], 1)
            dve.wait_ge(S["chi_ok"], 1)
            dve.tensor_tensor(c_lo, CT, c_hi, ALU.subtract).then_inc(S["clo_ok"], 1)
            dve.wait_ge(S["deg_done"], 1)
            dve.tensor_copy(deg_hi, p_deg[:, 0:T]).then_inc(S["dve"], 1)
            dve.wait_ge(S["dve"], steps_done(1))
            dve.tensor_tensor(deg, p_deg[:, T:2 * T], deg_hi, ALU.add).then_inc(S["dinv_ok"], 1)
            dve.wait_ge(S["dinv_ok"], 1)
            dve.tensor_scalar(zz[:, 0, :], deg, float(F16_EXACT), None, ALU.is_gt).then_inc(S["dve"], 1)
            dve.wait_ge(S["dve"], steps_done(1))
            dve.tensor_reduce(over, zz[:, 0, :], axis=AX.X, op=ALU.max).then_inc(S["over_ok"], 1)
            dve.wait_ge(S["flag_done"], 1)
            dve.tensor_copy(flag_i[0:1], p_flag).then_inc(S["flag_ok"], 1)
            dve.wait_ge(S["dinv_ok"], 2)
            for t in range(T):
                dve.wait_ge(S["hs_hi_ok"], t + 1)
                dve.scalar_tensor_tensor(hs_lo[:, t, :], h_sb[:, t, :], dinv[:, t:t + 1], hs_hi[:, t, :],
                                         ALU.mult, ALU.subtract).then_inc(S["hs_lo_ok"], 1)

            def moments(y, width, signal):
                for m in range(2):
                    ins = dve.bn_stats(stats[:, m, :], y[:, m * width // 2:(m + 1) * width // 2])
                ins.then_inc(S["dve"], 1)
                dve.reg_mov(awaited, steps_done(1))
                dve.wait_ge(S["iotas"], 8)
                dve.wait_ge(S["dve"], awaited)
                dve.bn_aggr(mv, stats.rearrange("p a b -> p (a b)")).then_inc(S["dve"], 1)
                dve.wait_ge(S["dve"], steps_done(1))
                dve.tensor_scalar(veps, mv[:, 1:2], LN_EPS, None, ALU.add).then_inc(signal, 1)

            dve.wait_ge(S["par_b0"], 16)
            dve.wait_ge(S["xr_in0"], 16)
            dve.wait_ge(S["xr_in1"], 32)
            with dve.Fori(0, T // 2) as i:
                kept = enter_loop(i, 2 * 3)
                for par in range(2):
                    t = i * 2 + par
                    xt = x_sb[:, ds(t, 1), :].rearrange("p a n -> p (a n)")
                    y = y0[:, par, :]
                    dve.wait_ge(S["gcn_done"], t + 1)
                    dve.scalar_tensor_tensor(y, p_out[par], dinv[:, ds(t, 1)], xt, ALU.mult, ALU.add).then_inc(S["gcn_read"], 1)
                    dve.wait_ge(S["gcn_read"], t + 3)
                    dve.tensor_tensor(y, y, par_rows[:, 2, 0:D], ALU.add).then_inc(S["dve"], 1)
                    dve.wait_ge(S["dve"], steps_done(1))
                    moments(y, D, S["gcn_var"])
                    dve.wait_ge(S["gcn_rstd"], t + 2)
                    dve.tensor_scalar(xt, y, mv[:, 0:1], rstd, ALU.subtract, ALU.mult).then_inc(S["x1_ok"], 1)
                    dve.wait_ge(S["x1_ok"], t + 1)
                leave_loop(kept, T // 2, 2 * 3)
            for t in range(T):
                dve.wait_ge(S["neg_tr"], t + 1)
                dve.tensor_scalar(neg[:, t, :], p_neg[t % 2], 0.0, NEG_BIG, ALU.is_equal, ALU.mult).then_inc(S["neg_ok"], 1)
            weights(1)

            def max_as(row, col, t, out_, mask):
                dve.wait_ge(S["dve"], steps_done() - 1)
                dve.tensor_tensor_reduce(out=out_, in0=mask[:, t, :], in1=row, scale=1.0, scalar=NEG_BIG,
                                         op0=ALU.add, op1=ALU.max, accum_out=mx[:, col, t:t + 1]).then_inc(S["dve"], 1)
                steps_done(1)

            def project(t, heads, width, psum_, junk_, rows=(0, 1)):
                if t:
                    dve.wait_ge(S["dve"], steps_done())
                for j in range(2 * heads):
                    a = slice(j % heads * width, (j % heads + 1) * width)
                    ins = dve.tensor_tensor_reduce(out=junk_[:, j, :], in0=psum_[:, a], in1=par_rows[:, rows[j // heads], a], scale=1.0,
                                                   scalar=0.0, op0=ALU.mult, op1=ALU.add, accum_out=asd_w[:, j, t:t + 1])
                ins.then_inc(S["dve"], 1)
                steps_done(1)

            dve.wait_ge(S["par_a1s"], 16)
            dve.wait_ge(S["par_a1d"], 16)
            for what, t in X1_ORDER:
                if what == "tr":
                    dve.wait_ge(S["x1t_hi_ok"], t + 1)
                    dve.tensor_tensor(x1t_lo[:, :, t * P:(t + 1) * P], p_tr[t % 2].rearrange("p (k n) -> p k n", k=KD),
                                      x1t_hi[:, :, t * P:(t + 1) * P], ALU.subtract).then_inc(S["x1t_lo_ok"], 1)
                else:
                    dve.wait_ge(S["xl_hi_ok"], t + 1)
                    project(t, H, HID, p_x[t % 2], a_junk)
                    dve.scalar_tensor_tensor(xl_lo[:, t, :, 0:HID], p_x[t % 2].rearrange("p (h n) -> p h n", h=H), 1 / WSCALE,
                                             xl_hi[:, t, :, 0:HID], ALU.mult, ALU.subtract).then_inc(S["xl_lo_ok"], 1)
                    if 2 <= t < 2 + KD:
                        weights(2, [t - 2])
            dve.wait_ge(S["dve"], steps_done())
            dve.tensor_scalar(asd, asd_w, 1 / WSCALE, None, ALU.mult).then_inc(S["as_ok"], 1)
            dve.wait_ge(S["as_ok"], 1)
            dve.tensor_scalar(as_s, asd[:, 0:H, :], SLOPE, None, ALU.mult).then_inc(S["dve"], 1)
            dve.wait_ge(S["dve"], steps_done(1))
            dve.wait_ge(S["as_tr"], 1)
            dve.tensor_copy(rows_sb, p_rows).then_inc(S["as_rows"], 1)

            dve.wait_ge(S["xl_done"], T)
            for t in range(T):
                second = t // (T // 2)
                for h in range(2):
                    if t % (T // 2) == 0:
                        dve.wait_ge(S[f"asr{h}"], 16 * (1 + second))
                    for i in range(2):
                        max_as(as_row[h], 2 * second + h, t % (T // 2) * 2 + i, junk[i], neg)
                if t == T // 2 - 1:
                    dve.wait_ge(S["dve"], steps_done())
                    dve.sem_inc(S["max_ok"], 1)
            dve.wait_ge(S["dve"], steps_done())

            def shifts(heads, signal):
                ad, z, m = asd[:, heads:2 * heads, :], zz[:, 0:heads, :], mm[:, 0:heads, :]
                dve.tensor_tensor(z, mx[:, 0:heads, :], ad, ALU.add).then_inc(S["dve"], 1)
                dve.wait_ge(S["dve"], steps_done(1))
                dve.scalar_tensor_tensor(m, z, SLOPE, z, ALU.mult, ALU.max).then_inc(S["dve"], 1)
                dve.wait_ge(S["dve"], steps_done(1))
                dve.tensor_tensor(uv[:, 0:heads, :], ad, m, ALU.subtract).then_inc(S["dve"], 1)
                dve.wait_ge(S["dve"], steps_done(1))
                dve.scalar_tensor_tensor(uv[:, heads:2 * heads, :], ad, SLOPE, m, ALU.mult, ALU.subtract).then_inc(signal, 1)

            shifts(H, S["uv_ok"])
            dve.wait_ge(S["uv_tr"], 1)
            dve.wait_ge(S["as_dram"], 16)
            dve.tensor_copy(rows_sb, p_rows).then_inc(S["uv_rows"], 1)


            def xl2_low(t):
                dve.wait_ge(S["xl2_hi_ok"], t + 1)
                if t == 0:
                    dve.wait_ge(S["par_a2s"], 16)
                    dve.wait_ge(S["par_a2d"], 16)
                project(t, 1, D, p_x[t % 2], a2_junk, rows=(3, 0))
                dve.scalar_tensor_tensor(xl2_lo[:, t, 0:D], p_x[t % 2][:, 0:D], 1 / WSCALE, xl2_hi[:, t, 0:D],
                                         ALU.mult, ALU.subtract).then_inc(S["xl2_lo_ok"], 1)

            for c in range(2):
                def evict(h):
                    ch = c * H + h
                    dve.wait_ge(S["p_free"], ch * T + T + PSLOTS)
                    dve.tensor_scalar(ssum, p_att[:, :, HID:HID + 1].rearrange("p j n -> p (j n)"), SOFTMAX_EPS, None, ALU.add).then_inc(S["dve"], 1)
                    dve.wait_ge(S["dve"], steps_done(1))
                    dve.reciprocal(rsum, ssum).then_inc(S["dve"], 1)
                    dve.wait_ge(S["dve"], steps_done(1))
                    cols = slice(h * HID, (h + 1) * HID)
                    for j in range(C1):
                        dve.scalar_tensor_tensor(att[:, j, cols], p_att[:, j, 0:HID], rsum[:, j:j + 1],
                                                 par_rows[:, 0, cols], ALU.mult, ALU.add).then_inc(S["att_read"], 1)

                for h in range(H):
                    ch = c * H + h

                    def high(k):
                        dve.wait_ge(S["pf_ok"], ch * T + k + 1 + E_CREDIT)
                        dve.wait_ge(S["p_free"], ch * T + k + 1)
                        dve.tensor_copy(p_hi[k % PSLOTS], pf[k % ESLOTS]).then_inc(S["ph_odd"], 1)

                    for k in range(T):
                        n, s = ch * T + k, k % ESLOTS
                        if h and k == EVICT_AT:
                            dve.wait_ge(S["par_b1"], 16)
                            evict(h - 1)
                        dve.wait_ge(S["ex_ok"], n * 2 + 2)
                        dve.tensor_tensor(e1[s], e1[s], e2[s], ALU.max).then_inc(S["g_ok"], 1)
                        if k >= 2 and k % 2 == 0:
                            high(k - 1)
                        dve.wait_ge(S["g_ok"], n + 1)
                        dve.wait_ge(S["pl_ok"], n + 1 + E_CREDIT - E_BACK[k])
                        dve.scalar_tensor_tensor(pf[s], e1[s], 1.0, CT[:, k, ds(c * W1C, W1C)],
                                                 ALU.min, ALU.mult).then_inc(S["pf_ok"], 1)
                    high(T - 1)
                    dve.sem_inc(S["uv_free"], 1)
                evict(H - 1)
                dve.wait_ge(S["att_read"], (c + 1) * H * C1 + C1)
                dve.wait_ge(S["par_g1"], 16)
                dve.wait_ge(S["par_be1"], 16)

                for j in range(C1):
                    t = c * C1 + j
                    y = att[:, j, :]
                    moments(y, HC, S["ln_var"])
                    dve.scalar_tensor_tensor(y, y, mv[:, 0:1], par_rows[:, 1, :], ALU.subtract, ALU.mult).then_inc(S["dve"], 1)
                    dve.wait_ge(S["ln_rstd"], t + 2)
                    dve.wait_ge(S["dve"], steps_done(1))
                    dve.scalar_tensor_tensor(y, y, rstd, par_rows[:, 2, :], ALU.mult, ALU.add).then_inc(S["dve"], 1)
                    dve.wait_ge(S["dve"], steps_done(1))
                    slots = (C1 + 1) // 2 if j % 2 == 0 else C1 // 2
                    dve.wait_ge(S[f"r_in{j % 2}"], (c * slots + j // 2 + 1) * 16)
                    dve.scalar_tensor_tensor(y, y, 0.0, r_ld[j % 2], ALU.max, ALU.add).then_inc(S["h1_ok"], 1)
                    if c == 1 and j:
                        xl2_low(j - 1)

            xl2_low(C1 - 1)
            for t in range(C1, T):
                xl2_low(t)
                weights(4, range(2 * (t - C1), min(2 * (t - C1) + 2, KH)))
            dve.wait_ge(S["dve"], steps_done())
            dve.tensor_scalar(asd[:, 0:2, :], asd_w[:, 0:2, :], 1 / WSCALE, None, ALU.mult).then_inc(S["as2_ok"], 1)
            dve.wait_ge(S["as2_ok"], 1)
            dve.tensor_scalar(as_s[:, 0, :], asd[:, 0, :], SLOPE, None, ALU.mult).then_inc(S["dve"], 1)
            dve.wait_ge(S["dve"], steps_done(1))
            dve.wait_ge(S["as2_tr"], 1)
            dve.tensor_copy(rows_sb[0:2 * T], p_rows[0:2 * T]).then_inc(S["as2_rows"], 1)
            dve.wait_ge(S["par_br2"], 16)
            dve.wait_ge(S["par_be2"], 16)
            dve.tensor_tensor(par_rows[:, 3, 0:D], par_rows[:, 3, 0:D], par_rows[:, 2, 0:D], ALU.add).then_inc(S["dve"], 1)
            dve.wait_ge(S["dve"], steps_done(1))
            for t in range(T):
                dve.wait_ge(S[f"xb_in{t % 2}"], 16 * (t // 2 + 1))
                dve.tensor_tensor(xb_ld[t % 2], xb_ld[t % 2], par_rows[:, 3, 0:D], ALU.add).then_inc(S["dve"], 1)
                dve.wait_ge(S["dve"], steps_done(1))
                dve.wait_ge(S["r2_done"], t + 1)
                if t >= 2:
                    dve.wait_ge(S[f"r2_out{t % 2}"], 16 * (t // 2))
                dve.scalar_tensor_tensor(r2_st[t % 2], p_x[t % 2][:, 0:D], 1 / WSCALE, xb_ld[t % 2],
                                         ALU.mult, ALU.add).then_inc(S["r2_sb"], 1)
                if t == 0:
                    dve.wait_ge(S["asr2"], 16)
                    dve.wait_ge(S["neg_in"], 16)
                for i in range(3 * t, min(3 * t + 3, T)):
                    max_as(as2_row, 0, i, junk2[i % 2], neg2)
                if t == SHIFT_AT - 1:
                    dve.wait_ge(S["dve"], steps_done())
                    shifts(1, S["uv2_ok"])
                if t == SHIFT_AT:
                    dve.wait_ge(S["uv2_tr"], 1)
                    dve.wait_ge(S["as2_dram"], 16)
                    dve.tensor_copy(rows_sb[0:2 * T], p_rows[0:2 * T]).then_inc(S["uv2_rows"], 1)
            dve.wait_ge(S["par_b2"], 16)
            dve.wait_ge(S["par_g2"], 16)

            def make_p(c):
                def high(k):
                    dve.wait_ge(S["pf2_ok"], c * T + k + 1 + E_CREDIT)
                    dve.wait_ge(S["p2_free"], c * T + k + 1)
                    dve.tensor_copy(pp_hi[k % P2SLOTS], ppf[k % ESLOTS]).then_inc(S["ph2_ok"], 1)

                for k in range(T):
                    n, s = c * T + k, k % ESLOTS
                    dve.wait_ge(S["ex2_ok"], n * 2 + 2)
                    dve.tensor_tensor(ee1[s], ee1[s], ee2[s], ALU.max).then_inc(S["g2_ok"], 1)
                    if k:
                        high(k - 1)
                    dve.wait_ge(S["g2_ok"], n + 1)
                    dve.wait_ge(S["pl2_ok"], n + 1 + E_CREDIT - E_BACK[k])
                    dve.scalar_tensor_tensor(ppf[s], ee1[s], 1.0, CT[:, k, ds(c * W2C, W2C)],
                                             ALU.min, ALU.mult).then_inc(S["pf2_ok"], 1)
                high(T - 1)

            def moments2(js, n):
                for j in js:
                    for m in range(2):
                        ins = dve.bn_stats(stats2[:, j, m * 6:(m + 1) * 6], y2[j][:, m * D // 2:(m + 1) * D // 2])
                ins.then_inc(S["dve"], 1)
                dve.reg_mov(awaited, steps_done(1))
                dve.wait_ge(S["iotas"], 8)
                dve.wait_ge(S["dve"], awaited)
                for j in js:
                    ins = dve.bn_aggr(mv2[:, j, :], stats2[:, j, :])
                ins.then_inc(S["dve"], 1)
                dve.wait_ge(S["dve"], steps_done(1))
                dve.tensor_scalar(veps2[:, js[0]:js[-1] + 1], mv2[:, js[0]:js[-1] + 1, 1:2].rearrange("p j a -> p (j a)"), LN_EPS, None,
                                  ALU.add).then_inc(S["ln2_var"], 1)

            def finish(c, js, n):
                first, end = js[0], js[-1] + 1
                acc = psum[:, ds((c % 2) * 2048, 2048)].rearrange("p (j n) -> p j n", j=C2)
                dve.tensor_scalar(ssum[:, first:end], acc[:, first:end, D:D + 1].rearrange("p j n -> p (j n)"), SOFTMAX_EPS, None, ALU.add).then_inc(S["dve"], 1)
                dve.wait_ge(S["dve"], steps_done(1))
                dve.reciprocal(rsum[:, first:end], ssum[:, first:end]).then_inc(S["dve"], 1)
                dve.wait_ge(S["dve"], steps_done(1))
                for j in js:
                    ins = dve.scalar_tensor_tensor(y2[j], acc[:, j, 0:D], rsum[:, j:j + 1], par_rows[:, 0, 0:D], ALU.mult, ALU.add)
                ins.then_inc(S["att2_read"], 1)
                dve.wait_ge(S["att2_read"], c + 3 + (first if len(js) == 1 else 0))
                moments2(js, n)
                for j in js:
                    ins = dve.scalar_tensor_tensor(y2[j], y2[j], mv2[:, j, 0:1], par_rows[:, 1, 0:D], ALU.subtract, ALU.mult)
                ins.then_inc(S["dve"], 1)
                dve.wait_ge(S["ln2_rstd"], n + 2)
                dve.wait_ge(S["dve"], steps_done(1))
                for j in js:
                    dve.wait_ge(S[f"r2_in{j}"], (c + 1) * 16)
                    dve.scalar_tensor_tensor(y2[j], y2[j], rstd2[:, j:j + 1], r2_ld[j], ALU.mult, ALU.add).then_inc(S["r2_used"], 1)
                dve.wait_ge(S["r2_used"], c * C2 + end)
                moments2(js, n + 1)
                dve.wait_ge(S["ln2_rstd"], n + 3)
                dve.wait_ge(S["out_dma"], (c * C2 + 1) * 16)
                for j in js:
                    dve.tensor_scalar(y3[j], y2[j], mv2[:, j, 0:1], rstd2[:, j:j + 1], ALU.subtract, ALU.mult).then_inc(S["out_ok"], 1)

            dve.sem_inc(S["p2_free"], P2SLOTS)
            make_p(0)
            with dve.Fori(0, T // C2 - 1) as c:
                kept = enter_loop(c, 7)
                make_p(c + 1)
                dve.wait_ge(S["p2_free"], c * T + T + P2SLOTS)
                finish(c, range(C2), c * 2)
                leave_loop(kept, T // C2 - 1, 7)
            for j in range(C2):
                dve.wait_ge(S["last_done"], j + 1)
                finish(T // C2 - 1, [j], 2 * (T // C2 - 1) + 2 * j)



_INS = ["x", "src", "dst", "L0_gnn_W", "L0_gnn_b", "L1_gnn_W1", "L1_gnn_a_src1", "L1_gnn_a_dst1", "L1_gnn_b1",
        "L1_gnn_g1", "L1_gnn_be1", "L1_gnn_Wr1", "L1_gnn_br1", "L1_gnn_W2", "L1_gnn_a_src2", "L1_gnn_a_dst2",
        "L1_gnn_b2", "L1_gnn_g2", "L1_gnn_be2", "L1_gnn_Wr2", "L1_gnn_br2"]


def kernel(**inputs):
    import numpy as _np
    import concourse.bacc as _bacc
    from concourse import mybir as _mybir
    from concourse.bass_utils import run_bass_kernel_spmd as _run

    nc = _bacc.Bacc("TRN2", target_bir_lowering=False, num_devices=1)
    arrays, args = {}, []
    for name in _INS:
        a = _np.ascontiguousarray(inputs[name])
        arrays[f"in_{name}_dram"] = a
        args.append(nc.dram_tensor(f"in_{name}_dram", a.shape, _mybir.dt.from_np(a.dtype), kind="ExternalInput").ap())
    out = nc.dram_tensor("out_dram", (N, D), _mybir.dt.float32, kind="ExternalOutput").ap()
    gnn_program(nc, *args, out)
    r = _run(nc, [arrays], core_ids=[0])
    return r.results[0]["out_dram"]
```
